# Optimizing a Trainium2 kernel written in Bass

```python
import numpy as np
import jax
import jax.numpy as jnp

def _softmax(x, axis=-1):
    return jax.nn.softmax(x, axis=axis)

def _gelu(x):
    return jax.nn.gelu(x, approximate=True)

def _silu(x):
    return jax.nn.silu(x)

def _sigmoid(x):
    return jax.nn.sigmoid(x)

def _layernorm(x, axis=-1, eps=1e-05):
    m = jnp.mean(x, axis=axis, keepdims=True)
    v = jnp.var(x, axis=axis, keepdims=True)
    return (x - m) / jnp.sqrt(v + eps)

def _scatter_add(tgt, idx, src, axis=0):
    return tgt.at[idx].add(src)

def _segment_sum(src, seg, n):
    return jax.ops.segment_sum(src, seg, n)
kernel_name = 'mk_gnn_resnorm_d2_gnn_r8_be14cf'

def setup_inputs(seed: int=0):
    np.random.seed(seed)
    _w = jnp.asarray

    def _rec_inputs():
        import jax
        import jax.numpy as jnp
        _gk = jax.random.key(seed)
        x = -0.000202 + 1 * jax.random.normal(jax.random.fold_in(_gk, 1), (6250, 128), jnp.float32)
        src = jax.random.randint(jax.random.fold_in(_gk, 2), (100000,), 0, 6250, jnp.int32)
        dst = jax.random.randint(jax.random.fold_in(_gk, 3), (100000,), 0, 6250, jnp.int32)
        _o = jnp.argsort(dst, stable=True)
        src = src[_o]
        dst = dst[_o]
        edge_attr_16 = 0.000196303 + 1.00016 * jax.random.normal(jax.random.fold_in(_gk, 11), (100000, 16), jnp.float32)
        return (x, src, dst, edge_attr_16)
    x, src, dst, edge_attr_16 = _rec_inputs()

    def _L0_gnn_setup():
        import jax, jax.numpy as jnp
        import numpy as np
        N_NODES = 6250
        N_EDGES = 200000
        D = 128
        H = 8
        DH = D // H
        FF = 512
        EPS = 1e-05

        def _layer_norm(x, g, b):
            mu = jnp.mean(x, axis=-1, keepdims=True)
            var = jnp.mean(jnp.square(x - mu), axis=-1, keepdims=True)
            return (x - mu) * jax.lax.rsqrt(var + EPS) * g + b
        key = jax.random.key(seed)
        ks = jax.random.split(key, 12)
        s = 0.05
        X = jax.random.normal(ks[0], (N_NODES, D), dtype=jnp.float32)
        edge_index = jax.random.randint(ks[1], (2, N_EDGES), 0, N_NODES, dtype=jnp.int64)
        return {'X': X, 'edge_index': edge_index, 'Wq': jax.random.normal(ks[2], (D, D), dtype=jnp.float32) * s, 'Wk': jax.random.normal(ks[3], (D, D), dtype=jnp.float32) * s, 'Wv': jax.random.normal(ks[4], (D, D), dtype=jnp.float32) * s, 'W0': jax.random.normal(ks[5], (D, D), dtype=jnp.float32) * s, 'ln1_g': jnp.ones((D,), dtype=jnp.float32), 'ln1_b': jnp.zeros((D,), dtype=jnp.float32), 'fc1_w': jax.random.normal(ks[6], (D, FF), dtype=jnp.float32) * s, 'fc1_b': jnp.zeros((FF,), dtype=jnp.float32), 'fc2_w': jax.random.normal(ks[7], (FF, D), dtype=jnp.float32) * s, 'fc2_b': jnp.zeros((D,), dtype=jnp.float32), 'ln2_g': jnp.ones((D,), dtype=jnp.float32), 'ln2_b': jnp.zeros((D,), dtype=jnp.float32)}
    _L0_gnn_all = _L0_gnn_setup()
    _L0_gnn_in = {k: v for k, v in _L0_gnn_all.items() if k in ('Wq', 'Wk', 'Wv', 'W0', 'ln1_g', 'ln1_b', 'fc1_w', 'fc1_b', 'fc2_w', 'fc2_b', 'ln2_g', 'ln2_b')}
    del _L0_gnn_all

    def _L1_gnn_setup():
        import jax, jax.numpy as jnp
        import numpy as np
        N = 6250
        IN_DIM = 128
        OUT_DIM = 128
        EA_DIM = 16
        REQ_DIM = 16
        E_TOTAL = 200000

        def _directional_msg(x, src, dst, edge_attr, req, W1, b1, W2, b2, n_nodes):
            x_j = x[src]
            req_e = jnp.broadcast_to(req, (src.shape[0], req.shape[-1]))
            m = jnp.concatenate([x_j, edge_attr, req_e], axis=-1)
            h = jax.nn.relu(m @ W1 + b1) @ W2 + b2
            return jax.ops.segment_sum(h, dst, num_segments=n_nodes)
        key = jax.random.key(seed)
        ks = jax.random.split(key, 16)
        cat_dim = IN_DIM + EA_DIM + REQ_DIM
        s = 0.02
        return {'x': jax.random.normal(ks[0], (N, IN_DIM), dtype=jnp.float32), 'edge_index': jax.random.randint(ks[1], (2, E_TOTAL), 0, N, dtype=jnp.int32), 'edge_attr': jax.random.normal(ks[2], (E_TOTAL, EA_DIM), dtype=jnp.float32), 'req_emb': jax.random.normal(ks[3], (1, REQ_DIM), dtype=jnp.float32), 'W1f': jax.random.normal(ks[4], (cat_dim, OUT_DIM), dtype=jnp.float32) * s, 'b1f': jnp.zeros((OUT_DIM,), dtype=jnp.float32), 'W2f': jax.random.normal(ks[5], (OUT_DIM, OUT_DIM), dtype=jnp.float32) * s, 'b2f': jnp.zeros((OUT_DIM,), dtype=jnp.float32), 'W1b': jax.random.normal(ks[6], (cat_dim, OUT_DIM), dtype=jnp.float32) * s, 'b1b': jnp.zeros((OUT_DIM,), dtype=jnp.float32), 'W2b': jax.random.normal(ks[7], (OUT_DIM, OUT_DIM), dtype=jnp.float32) * s, 'b2b': jnp.zeros((OUT_DIM,), dtype=jnp.float32), 'Wu': jax.random.normal(ks[8], (OUT_DIM, OUT_DIM), dtype=jnp.float32) * s, 'bu': jnp.zeros((OUT_DIM,), dtype=jnp.float32), 'eps': jnp.zeros((1,), dtype=jnp.float32)}
    _L1_gnn_all = _L1_gnn_setup()
    _L1_gnn_in = {k: v for k, v in _L1_gnn_all.items() if k in ('req_emb', 'W1f', 'b1f', 'W2f', 'b2f', 'W1b', 'b1b', 'W2b', 'b2b', 'Wu', 'bu', 'eps')}
    del _L1_gnn_all
    return {'x': x, 'src': src, 'dst': dst, 'edge_attr_16': edge_attr_16, 'L0_gnn_Wq': _L0_gnn_in['Wq'], 'L0_gnn_Wk': _L0_gnn_in['Wk'], 'L0_gnn_Wv': _L0_gnn_in['Wv'], 'L0_gnn_W0': _L0_gnn_in['W0'], 'L0_gnn_ln1_g': _L0_gnn_in['ln1_g'], 'L0_gnn_ln1_b': _L0_gnn_in['ln1_b'], 'L0_gnn_fc1_w': _L0_gnn_in['fc1_w'], 'L0_gnn_fc1_b': _L0_gnn_in['fc1_b'], 'L0_gnn_fc2_w': _L0_gnn_in['fc2_w'], 'L0_gnn_fc2_b': _L0_gnn_in['fc2_b'], 'L0_gnn_ln2_g': _L0_gnn_in['ln2_g'], 'L0_gnn_ln2_b': _L0_gnn_in['ln2_b'], 'L1_gnn_req_emb': _L1_gnn_in['req_emb'], 'L1_gnn_W1f': _L1_gnn_in['W1f'], 'L1_gnn_b1f': _L1_gnn_in['b1f'], 'L1_gnn_W2f': _L1_gnn_in['W2f'], 'L1_gnn_b2f': _L1_gnn_in['b2f'], 'L1_gnn_W1b': _L1_gnn_in['W1b'], 'L1_gnn_b1b': _L1_gnn_in['b1b'], 'L1_gnn_W2b': _L1_gnn_in['W2b'], 'L1_gnn_b2b': _L1_gnn_in['b2b'], 'L1_gnn_Wu': _L1_gnn_in['Wu'], 'L1_gnn_bu': _L1_gnn_in['bu'], 'L1_gnn_eps': _L1_gnn_in['eps']}

def reference(x, src, dst, edge_attr_16, L0_gnn_Wq, L0_gnn_Wk, L0_gnn_Wv, L0_gnn_W0, L0_gnn_ln1_g, L0_gnn_ln1_b, L0_gnn_fc1_w, L0_gnn_fc1_b, L0_gnn_fc2_w, L0_gnn_fc2_b, L0_gnn_ln2_g, L0_gnn_ln2_b, L1_gnn_req_emb, L1_gnn_W1f, L1_gnn_b1f, L1_gnn_W2f, L1_gnn_b2f, L1_gnn_W1b, L1_gnn_b1b, L1_gnn_W2b, L1_gnn_b2b, L1_gnn_Wu, L1_gnn_bu, L1_gnn_eps):
    import jax
    import jax.numpy as jnp

    def _L0_gnn_ref(X, edge_index, Wq, Wk, Wv, W0, ln1_g, ln1_b, fc1_w, fc1_b, fc2_w, fc2_b, ln2_g, ln2_b):
        import jax, jax.numpy as jnp
        import numpy as np
        N_NODES = 6250
        N_EDGES = 200000
        D = 128
        H = 8
        DH = D // H
        FF = 512
        EPS = 1e-05

        def _layer_norm(x, g, b):
            mu = jnp.mean(x, axis=-1, keepdims=True)
            var = jnp.mean(jnp.square(x - mu), axis=-1, keepdims=True)
            return (x - mu) * jax.lax.rsqrt(var + EPS) * g + b
        N = X.shape[0]
        src = edge_index[0]
        dst = edge_index[1]
        q = (X @ Wq).reshape(N, H, DH)
        k = (X @ Wk).reshape(N, H, DH)
        v = (X @ Wv).reshape(N, H, DH)
        scores = jnp.einsum('ehd,ehd->eh', q[dst], k[src]) / jnp.sqrt(jnp.float32(DH))
        m = jax.ops.segment_max(scores, dst, num_segments=N)
        ex = jnp.exp(scores - m[dst])
        denom = jax.ops.segment_sum(ex, dst, num_segments=N)
        alpha = ex / (denom[dst] + 1e-09)
        agg = jax.ops.segment_sum(alpha[:, :, None] * v[src], dst, num_segments=N)
        embedding = agg.reshape(N, D) @ W0
        h1 = _layer_norm(X + embedding, ln1_g, ln1_b)
        ff = jax.nn.relu(h1 @ fc1_w + fc1_b) @ fc2_w + fc2_b
        return _layer_norm(h1 + ff, ln2_g, ln2_b)

    def _L1_gnn_ref(x, edge_index, edge_attr, req_emb, W1f, b1f, W2f, b2f, W1b, b1b, W2b, b2b, Wu, bu, eps):
        import jax, jax.numpy as jnp
        import numpy as np
        N = 6250
        IN_DIM = 128
        OUT_DIM = 128
        EA_DIM = 16
        REQ_DIM = 16
        E_TOTAL = 200000

        def _directional_msg(x, src, dst, edge_attr, req, W1, b1, W2, b2, n_nodes):
            x_j = x[src]
            req_e = jnp.broadcast_to(req, (src.shape[0], req.shape[-1]))
            m = jnp.concatenate([x_j, edge_attr, req_e], axis=-1)
            h = jax.nn.relu(m @ W1 + b1) @ W2 + b2
            return jax.ops.segment_sum(h, dst, num_segments=n_nodes)
        n_nodes = x.shape[0]
        E = edge_index.shape[1] // 2
        req = req_emb.reshape(1, -1)
        x_self = x
        src_f, dst_f = (edge_index[0, :E], edge_index[1, :E])
        src_b, dst_b = (edge_index[0, E:], edge_index[1, E:])
        h_in = _directional_msg(x, src_f, dst_f, edge_attr[:E], req, W1f, b1f, W2f, b2f, n_nodes)
        h_out = _directional_msg(x, src_b, dst_b, edge_attr[E:], req, W1b, b1b, W2b, b2b, n_nodes)
        h = (1.0 + eps) * x_self + h_in + h_out
        return jax.nn.relu(h @ Wu + bu)
    edge_index = jnp.stack([src, dst])
    x = _layernorm(x + _L0_gnn_ref(x, edge_index, L0_gnn_Wq, L0_gnn_Wk, L0_gnn_Wv, L0_gnn_W0, L0_gnn_ln1_g, L0_gnn_ln1_b, L0_gnn_fc1_w, L0_gnn_fc1_b, L0_gnn_fc2_w, L0_gnn_fc2_b, L0_gnn_ln2_g, L0_gnn_ln2_b), axis=-1)
    x = _layernorm(x + _L1_gnn_ref(x, edge_index, edge_attr_16, L1_gnn_req_emb, L1_gnn_W1f, L1_gnn_b1f, L1_gnn_W2f, L1_gnn_b2f, L1_gnn_W1b, L1_gnn_b1b, L1_gnn_W2b, L1_gnn_b2b, L1_gnn_Wu, L1_gnn_bu, L1_gnn_eps), axis=-1)
    return x

_drawn_inputs = setup_inputs


def setup_inputs(seed=0):
    import zlib

    import numpy as np

    out = dict(_drawn_inputs(seed))
    spreads = {'L0_gnn_ln1_g': (1.0, 0.2),
     'L0_gnn_ln1_b': (0.0, 0.1),
     'L0_gnn_fc1_b': (0.0, 0.1),
     'L0_gnn_fc2_b': (0.0, 0.1),
     'L0_gnn_ln2_g': (1.0, 0.2),
     'L0_gnn_ln2_b': (0.0, 0.1),
     'L1_gnn_b1f': (0.0, 0.286),
     'L1_gnn_b2f': (0.0, 0.1),
     'L1_gnn_b1b': (0.0, 0.434),
     'L1_gnn_b2b': (0.0, 0.1),
     'L1_gnn_bu': (0.0, 0.1)}
    factors = {'edge_attr_16': 7.416, 'L0_gnn_Wq': 4.043, 'L0_gnn_Wk': 4.015}
    for name, (base, spread) in spreads.items():
        noise = np.random.default_rng([zlib.crc32(name.encode()), seed]).standard_normal(out[name].shape)
        drawn = base * np.exp(spread * noise) if base else spread * noise
        out[name] = jnp.asarray(drawn.astype(out[name].dtype))
    for name, factor in factors.items():
        out[name] = (out[name] * factor).astype(out[name].dtype)
    return out
```

```python
from contextlib import ExitStack

import concourse.bass as bass
from concourse import mybir

F32 = mybir.dt.float32
BF16 = mybir.dt.bfloat16
I32 = mybir.dt.int32
ALU = mybir.AluOpType
ACT = mybir.ActivationFunctionType
AX_X = mybir.AxisListType.X
ds = bass.ds

P = 128
N = 6250
D = 128
E = 100000
H = 8
DH = D // H
FF = 512
FC = FF // P
EA = 16
HALF = E // 2
EPS = 1e-5
BIG = 1e30

TILES = -(-N // P)
GRP = 7
GROUPS = TILES // GRP
LAST = N - (TILES - 1) * P
NPAD = TILES * P
G = 4
CH = G * P
VT = 2 * TILES
BASE1 = -(-(HALF + CH) // CH) * CH
END1 = BASE1 + HALF
AW = DH + 1
RW = H * AW
LW = D + 1

U = 6
LAG = 4
TR, TC = 88, 3
TE = TR * TC
ITERS = -(-((E + (CH - 1) * (TILES + 1)) // CH + LAG) // U)
assert ITERS * U + LAG <= TE
BASE = 8
EP, EQ = 125, 400


def gnn_kernel(nc, x, src, dst, ea, wq, wk, wv, w0, ln1g, ln1b, fc1w, fc1b, fc2w, fc2b, ln2g, ln2b,
               req, w1f, b1f, w2f, b2f, w1b, b1b, w2b, b2b, wu, bu, eps, out):
    with ExitStack() as ctx:
        def dram(name, shape, dt):
            return nc.dram_tensor(name, shape, dt, kind="Internal").ap()

        def sb(name, shape, dt=F32):
            return ctx.enter_context(nc.sbuf_tensor(name, shape, dt))

        def sem(name):
            return ctx.enter_context(nc.semaphore(name))

        kv_tab = dram("kv_tab", (NPAD, 2 * D), F32)
        y_tab = dram("y_tab", (2 * NPAD, D), F32)
        d0 = dram("d0", (E + CH + 1,), F32)
        pen0 = dram("pen0", (E + CH + 1,), F32)
        i0 = dram("i0", (E + CH,), I32)
        d1 = dram("d1", (END1 + CH,), F32)
        i1 = dram("i1", (END1 + CH,), I32)
        ea1 = dram("ea1", (END1 + CH, EA), F32)
        tabs = [dram(f"tab{l}", (TE, 4), I32) for l in range(2)]
        negs = [dram(f"neg{l}", (TE,), F32) for l in range(2)]

        xs = sb("xs", [P, TILES * D])
        ident = sb("ident", [P, P])
        ident_neg = sb("ident_neg", [H, H])
        iota_row = sb("iota_row", [P, P])
        iota_col = sb("iota_col", [P, 1])
        ones = sb("ones", [P, P])
        wqkv = sb("wqkv", [P, 3 * D])
        w0_sb = sb("w0_sb", [P, D])
        fc1_sb = sb("fc1_sb", [P, FF])
        fc2_sb = sb("fc2_sb", [P, FC, D])
        fc1b_sb = sb("fc1b_sb", [P, FC])
        rows = sb("rows", [P, 5, D])
        w1x = sb("w1x", [P, 2 * D])
        w1blk = sb("w1blk", [G * EA + 1, 2 * CH])
        w1r = sb("w1r", [EA, 2 * D])
        reql = sb("reql", [EA, G * EA + 1])
        b1row = sb("b1row", [1, 2 * D])
        w2wu = sb("w2wu", [P, 4 * D])
        w2u = sb("w2u", [P, 3 * D])
        b2col = sb("b2col", [P, 3])
        burow = sb("burow", [1, D])
        dbu = sb("dbu", [3, D])
        sel3 = sb("sel3", [1, 3])
        epsc = sb("epsc", [P, 1])
        eps_ln = sb("eps_ln", [P, 1])
        blockones = sb("blockones", [P, H])
        tab_sb = [sb(f"tab_sb{l}", [1, 4 * TE], I32) for l in range(2)]
        iters_sb = sb("iters_sb", [1, 4], I32)
        nj = [sb(f"nj{l}", [P, TE]) for l in range(2)]
        pj = sb("pj", [P, TE])

        mark = sb("mark", [P, 4])
        reql_one = sb("reql_one", [1, G * EA + 1])

        ARENA = 38200
        arena = sb("arena", [P, ARENA])
        top = [0]

        def carve(n, start=None):
            if start is not None:
                top[0] = start
            a = arena[:, top[0]:top[0] + n]
            top[0] += n
            assert top[0] <= ARENA, top[0]
            return a

        PENW = CH + 8
        acc0 = carve((TILES + 1) * RW, 0)
        qsp = carve(TILES * 3 * D // 2).bitcast(BF16)
        zero0 = top[0]
        contrib = carve(2 * (H + G * RW))
        prod = carve(2 * CH)
        kts = carve(2 * CH)
        scr = carve(2 * CH)
        fmx = carve(2 * CH)
        cmx = carve(2 * CH)
        ucar = carve(2)
        pen = carve(3 * PENW)
        s_hot = carve(U * CH)
        kvw = G * 2 * D
        kv = carve(U * kvw)
        zero1 = top[0]
        st = carve(U * CH // 2).bitcast(BF16)
        drow = carve(3 * CH)
        dcol = carve(U * G)
        idx = carve(U * G).bitcast(I32)
        rsc = carve(H)
        atmp = carve(RW)
        xT = carve(GRP * P, zero1 - U * kvw)
        kvst = carve(2 * GRP * 2 * D)
        qres = carve(GRP * D)
        xcp = carve(GRP * D)
        assert top[0] <= zero1 + U * CH // 2
        srci = carve(2 * EQ, 0).bitcast(I32)
        srcb = carve(EQ).bitcast(I32)
        dsti = carve(2 * EQ).bitcast(I32)
        dstf = carve(2 * EQ)
        dprev = carve(2 * EQ)
        cmpj = dsti.bitcast(F32)
        fill = carve(2 * CH)
        filli = carve(CH).bitcast(I32)
        assert top[0] <= TILES * RW
        carve(0, zero1 + U * CH // 2 + 3 * CH + 2 * U * G + H + RW)
        cnt = carve(VT)
        kcol = carve(TC)
        iota_u = carve(64)
        thr = carve(TILES)
        seg = carve(VT)
        nch = carve(VT)
        nchi = carve(VT).bitcast(I32)
        cum = carve(VT)
        spos = carve(VT)
        hotv = carve(VT)
        col = carve(8 * TC)
        tbe = carve(16 * 2 + 8)
        av = carve(GRP * D, (TILES + 1) * RW)
        rden = carve(GRP * H)
        nT = carve(GRP * P)
        res = carve(GRP * D)
        h1 = carve(GRP * D)
        h1c = carve(GRP * D)
        ffT = carve(FC * GRP * P)
        stats = carve(GRP * 6)
        mv = carve(GRP * 2)
        sd = carve(GRP)
        rs = carve(GRP)
        yst = carve(GRP * 2 * D)
        acc1 = carve((VT + 1) * LW, 0)
        late = max(top[0], (TILES + 1) * RW + 17000)
        con1 = carve(3 * G * LW, late)
        eaT = carve(2 * P)
        deg3 = carve(GRP * 3)
        yg = carve(U * G * D)
        s1 = carve(U * CH)
        hid = carve(2 * CH)
        eat = carve(U * P)
        dcol1 = carve(U * G)
        idx1 = carve(U * G).bitcast(I32)
        late_end = top[0]
        aT = carve(GRP * P * 3, late_end - (U * G * D + U * CH + 2 * CH + U * P + 2 * U * G))
        degT = carve(GRP * P)
        fin = carve(GRP * D)
        fstats = carve(GRP * 6)
        fmv = carve(GRP * 2)
        fsd = carve(GRP)
        frs = carve(GRP)
        fout = carve(GRP * D)
        fx = carve(3 * GRP * D)

        ps = ctx.enter_context(nc.psum_tensor("ps", [P, 8 * 512], F32))

        def bank(b, n=1):
            return ps[:, b * 512:(b + n) * 512]

        s_zero = sem("s_zero"); s_const = sem("s_const"); s_pool = sem("s_pool")
        s_w = sem("s_w"); s_w2 = sem("s_w2"); s_blk = sem("s_blk"); s_x = sem("s_x"); s_dst = sem("s_dst")
        s_wmm = sem("s_wmm"); s_wcp = sem("s_wcp")
        s_xTp = sem("s_xTp"); s_xT = sem("s_xT"); s_q = sem("s_q"); s_kv = sem("s_kv")
        s_qs = sem("s_qs"); s_kvst = sem("s_kvst"); s_kvo = sem("s_kvo"); s_kvfree = sem("s_kvfree"); s_kz = sem("s_kz")
        s_pre = sem("s_pre"); s_dst_out = sem("s_dst_out"); s_prev = sem("s_prev"); s_pen = sem("s_pen")
        s_cnt = sem("s_cnt"); s_seg = sem("s_seg"); s_tab = sem("s_tab"); s_tabo = sem("s_tabo")
        s_tabi = sem("s_tabi"); s_arr = sem("s_arr"); s_ea = sem("s_ea"); s_eac = sem("s_eac"); s_dv = sem("s_dv")
        s_init = sem("s_init"); s_bank = sem("s_bank"); s_pj = sem("s_pj"); s_xcp = sem("s_xcp"); s_wu = sem("s_wu"); s_mark = sem("s_mark")
        l_ld = [sem(f"l_ld{k}") for k in range(U)]
        l_ix = [sem(f"l_ix{k}") for k in range(U)]
        l_g = [sem(f"l_g{k}") for k in range(U)]
        l_hot = sem("l_hot"); l_kq = sem("l_kq"); l_kt = sem("l_kt"); l_kc = sem("l_kc"); l_prod = sem("l_prod"); l_s = sem("l_s")
        l_scr = sem("l_scr"); l_f = sem("l_f"); l_c = sem("l_c"); l_d = sem("l_d"); l_e = sem("l_e")
        l_pv = sem("l_pv"); l_agg = sem("l_agg"); l_acc = sem("l_acc"); l_over = sem("l_over"); m_over = sem("m_over")
        n_a = sem("n_a"); n_aTp = sem("n_aTp"); n_aT = sem("n_aT"); n_emb = sem("n_emb")
        n_var = sem("n_var"); n_sd = sem("n_sd"); n_h1 = sem("n_h1"); n_hTp = sem("n_hTp")
        n_hT = sem("n_hT"); n_f1 = sem("n_f1"); n_f1s = sem("n_f1s"); n_f2 = sem("n_f2")
        n_h1c = sem("n_h1c"); n_x1 = sem("n_x1"); n_x1c = sem("n_x1c"); n_xTp = sem("n_xTp"); n_xT = sem("n_xT")
        n_y = sem("n_y"); n_ys = sem("n_ys"); n_yo = sem("n_yo"); n_yfree = sem("n_yfree")
        m_zero = sem("m_zero"); m_pool = sem("m_pool")
        m_ld = [sem(f"m_ld{k}") for k in range(U)]
        m_ix = [sem(f"m_ix{k}") for k in range(U)]
        m_g = [sem(f"m_g{k}") for k in range(U)]
        m_hot = sem("m_hot"); m_eTp = sem("m_eTp"); m_eT = sem("m_eT"); m_u = sem("m_u")
        m_hid = sem("m_hid"); m_con = sem("m_con"); m_agg = sem("m_agg"); m_acc = sem("m_acc")
        f_deg = sem("f_deg"); f_tp = sem("f_tp"); f_t = sem("f_t"); f_o = sem("f_o"); f_r = sem("f_r"); f_b = sem("f_b"); f_x = sem("f_x")
        f_var = sem("f_var"); f_sd = sem("f_sd"); f_out = sem("f_out"); f_dma = sem("f_dma"); f_free = sem("f_free")

        block = ctx.enter_context(nc.Block())
        dst_halves = dst.rearrange("(h p c) -> p h c", h=2, c=EQ)
        src_halves = src.rearrange("(h p c) -> p h c", h=2, c=EQ)
        v3 = lambda a, b: a.rearrange("p (b c) -> p b c", b=b)

        def bases(eng, *pairs):
            for s_, lag in pairs:
                eng.sem_inc(s_, BASE - lag)

        def linker(eng, s_):
            made = eng.alloc_register("made")
            eng.reg_mov(made, 0)

            def link(ins, apart=False):
                ins.then_inc(s_, 1)
                eng.reg_add(made, made, 1)
                if apart:
                    eng.wait_ge(s_, 1)
                eng.wait_ge(s_, made)
            return link

        @block.sync
        def _(sp):
            for k, w in enumerate((wq, wk, wv)):
                sp.dma_start(wqkv[:, k * D:(k + 1) * D], w).then_inc(s_w, 16)
            sp.wait_ge(s_zero, 1)
            sp.dma_start(v3(xs[:, :], TILES)[:, 0:TILES - 1, :],
                         x[0:(TILES - 1) * P, :].rearrange("(t p) d -> p t d", p=P)).then_inc(s_x, 16)
            sp.dma_start(xs[0:LAST, (TILES - 1) * D:], x[(TILES - 1) * P:N, :]).then_inc(s_x, 16)
            sp.dma_start(v3(dsti, 2)[0:EP], dst_halves).then_inc(s_dst, 16)
            sp.dma_start(v3(srci, 2)[0:EP], src_halves).then_inc(s_dst, 16)
            sp.wait_ge(s_pool, 4)
            one = lambda a: a.rearrange("(a n) -> a n", a=1)
            sp.dma_start(one(d0[0:1]), fill[0:1, 0:1]).then_inc(s_arr, 16)
            sp.dma_start(one(d0[E + 1:E + 1 + CH]), fill[0:1, 0:CH]).then_inc(s_arr, 16)
            sp.dma_start(one(pen0[E:E + CH + 1]), fill[1:2, 0:CH + 1]).then_inc(s_arr, 16)
            sp.dma_start(one(i0[E:E + CH]), filli[0:1, 0:CH]).then_inc(s_arr, 16)
            gap = BASE1 - HALF
            sp.dma_start(one(d1[HALF:BASE1]), fill[0:1, 0:gap]).then_inc(s_ea, 16)
            sp.dma_start(one(d1[END1:END1 + CH]), fill[0:1, 0:CH]).then_inc(s_ea, 16)
            sp.dma_start(one(i1[HALF:BASE1]), fill[2:3, 0:gap].bitcast(I32)).then_inc(s_ea, 16)
            sp.dma_start(one(i1[END1:END1 + CH]), filli[0:1, 0:CH]).then_inc(s_ea, 16)
            sp.dma_start(ea1[HALF:BASE1, :].rearrange("(p a) f -> p (a f)", p=16),
                         fill[4:20, 0:gap * EA // 16]).then_inc(s_ea, 16)
            sp.dma_start(ea1[END1:END1 + CH, :].rearrange("(p a) f -> p (a f)", p=16),
                         fill[4:20, 0:CH * EA // 16]).then_inc(s_ea, 16)
            sp.wait_ge(s_pre, 1)
            sp.dma_start(d0[1:1 + E].rearrange("(h p c) -> p h c", h=2, c=EQ), v3(dstf, 2)[0:EP]).then_inc(s_dst_out, 16)
            sp.dma_start(i0[0:E].rearrange("(h p c) -> p h c", h=2, c=EQ), v3(srci, 2)[0:EP]).then_inc(s_arr, 16)
            for h, b in ((0, 0), (1, BASE1)):
                sp.dma_start(d1[b:b + HALF].rearrange("(p c) -> p c", c=EQ), v3(dstf, 2)[0:EP, h, :]).then_inc(s_ea, 16)
            sp.wait_ge(s_arr, 16 * 5)
            sp.wait_ge(s_dst_out, 16)
            sp.dma_start(v3(dprev, 2)[0:EP], d0[0:E].rearrange("(h p c) -> p h c", h=2, c=EQ)).then_inc(s_prev, 16)
            sp.wait_ge(s_pen, 2)
            sp.dma_start(pen0[0:E].rearrange("(h p c) -> p h c", h=2, c=EQ), v3(dprev, 2)[0:EP]).then_inc(s_arr, 16)
            for h, b in ((0, 0), (1, BASE1)):
                sp.dma_start(i1[b:b + HALF].rearrange("(p c) -> p c", c=EQ), (v3(srci, 2)[0:EP, 0, :], srcb[0:EP])[h]).then_inc(s_ea, 16)
            sp.sem_inc(s_kvfree, 2)
            with sp.Fori(0, GROUPS) as i:
                sp.wait_ge(s_kvst, i + 2)
                sp.dma_start(kv_tab[ds(i * (GRP * P), GRP * P), :].rearrange("(t p) d -> p t d", p=P),
                             v3(kvst[:, ds((i % 2) * (GRP * 2 * D), GRP * 2 * D)], GRP)).then_inc(s_kvo, 16)
                sp.wait_ge(s_kvo, 16 * i + 16)
                sp.sem_inc(s_kvfree, 1)
            sp.wait_ge(s_tab, 1)
            for l in range(2):
                sp.dma_start(tabs[l].rearrange("(p c) f -> p c f", p=TR),
                             tbe[0:TR, 16 * l:16 * l + 12].bitcast(I32).rearrange("p (c f) -> p c f", c=TC)).then_inc(s_tabo, 16)
                sp.dma_start(negs[l].rearrange("(p c) -> p c", p=TR), tbe[0:TR, 32 + 4 * l:32 + 4 * l + TC]).then_inc(s_tabo, 16)
            sp.wait_ge(s_tabo, 64)
            for l in range(2):
                sp.dma_start(tab_sb[l][:, :], tabs[l].rearrange("(a e) f -> a (e f)", a=1)).then_inc(s_tabi, 16)
                sp.dma_start(nj[l][:, :], negs[l].rearrange("(a e) -> a e", a=1).to_broadcast([P, TE])).then_inc(s_tabi, 16)
            for h, b in ((0, 0), (1, BASE1)):
                sp.dma_start(ea1[b:b + HALF, :].rearrange("(p c) f -> p (c f)", p=EP),
                             ea[h * HALF:(h + 1) * HALF, :].rearrange("(p c) f -> p (c f)", p=EP)).then_inc(s_eac, 16)

            sp.wait_ge(s_tabi, 64)
            sp.wait_ge(s_arr, 16 * 6)
            sp.wait_ge(s_init, 3)
            n0 = sp.value_load(iters_sb[0:1, 0:1], min_val=1, max_val=ITERS)
            free6 = sp.alloc_register("free6")
            free3 = sp.alloc_register("free3")
            sp.reg_mov(free6, BASE - U + 1)
            sp.reg_mov(free3, BASE - 3 + 1)
            with sp.Fori(0, n0) as i:
                for u in range(U):
                    off = sp.value_load(tab_sb[0][0:1, ds(4 * (i * U + (u + LAG)), 1)], min_val=0, max_val=E)
                    sp.wait_ge(s_init, 3)
                    sp.wait_ge(l_pv, free6)
                    sp.dma_start(v3(idx, U)[:, u, :], i0[ds(off, CH)].rearrange("(p g) -> p g", g=G)).then_inc(l_ix[u], 16)
                    sp.dma_start(v3(dcol, U)[:, u, :], d0[ds(off + 1, CH)].rearrange("(p g) -> p g", g=G)).then_inc(l_ld[u], 16)
                    sp.wait_ge(s_init, 3)
                    sp.wait_ge(l_c, free3)
                    sp.dma_start(v3(drow, 3)[:, u % 3, :],
                                 d0[ds(off + 1, CH)].rearrange("(a n) -> a n", a=1).to_broadcast([P, CH])).then_inc(l_ld[u], 16)
                    sp.dma_start(v3(pen, 3)[0:H, u % 3, 0:CH],
                                 pen0[ds(off, CH)].rearrange("(a n) -> a n", a=1).to_broadcast([H, CH])).then_inc(l_ld[u], 16)
                    sp.reg_add(free6, free6, 1)
                    sp.reg_add(free3, free3, 1)

            sp.sem_inc(n_yfree, 1)
            with sp.Fori(0, GROUPS) as i:
                sp.wait_ge(n_ys, i + 2)
                for h in range(2):
                    sp.dma_start(y_tab[ds(h * NPAD + i * (GRP * P), GRP * P), :].rearrange("(t p) d -> p t d", p=P),
                                 v3(yst, GRP)[:, :, h * D:(h + 1) * D]).then_inc(n_yo, 16)
                sp.wait_ge(n_yo, 32 * i + 32)
                sp.sem_inc(n_yfree, 1)

            sp.wait_ge(m_pool, 5)
            sp.wait_ge(s_ea, 16 * 10)
            sp.wait_ge(s_eac, 32)
            n1 = sp.value_load(iters_sb[0:1, 1:2], min_val=1, max_val=ITERS)
            sp.reg_mov(free6, BASE - U + 1)
            with sp.Fori(0, n1) as i:
                for u in range(U):
                    off = sp.value_load(tab_sb[1][0:1, ds(4 * (i * U + (u + LAG)), 1)], min_val=0, max_val=END1)
                    sp.wait_ge(m_pool, 5)
                    sp.wait_ge(m_hid, free6)
                    sp.dma_start(v3(idx1, U)[:, u, :], i1[ds(off, CH)].rearrange("(p g) -> p g", g=G)).then_inc(m_ix[u], 16)
                    sp.dma_start(v3(dcol1, U)[:, u, :], d1[ds(off, CH)].rearrange("(p g) -> p g", g=G)).then_inc(m_ld[u], 16)
                    sp.dma_start(v3(eat, U)[:, u, 0:G * EA], ea1[ds(off, CH), :].rearrange("(p g) f -> p (g f)", g=G)).then_inc(m_ld[u], 16)
                    sp.reg_add(free6, free6, 1)

            sp.sem_inc(f_free, 1)
            with sp.Fori(0, GROUPS - 1) as i:
                sp.wait_ge(f_out, i + 1)
                sp.dma_start(out[ds(i * (GRP * P), GRP * P), :].rearrange("(t p) d -> p t d", p=P),
                             v3(fout, GRP)).then_inc(f_dma, 16)
                sp.wait_ge(f_dma, 16 * i + 16)
                sp.sem_inc(f_free, 1)
            sp.wait_ge(f_out, GROUPS)
            done = (GROUPS - 1) * GRP * P
            sp.dma_start(out[done:done + (GRP - 1) * P, :].rearrange("(t p) d -> p t d", p=P),
                         v3(fout, GRP)[:, 0:GRP - 1, :]).then_inc(f_dma, 16)
            sp.dma_start(out[done + (GRP - 1) * P:N, :], fout[0:LAST, (GRP - 1) * D:]).then_inc(f_dma, 16)
            sp.wait_ge(f_dma, 16 * (GROUPS + 1))
            sp.wait_ge(n_yo, 32 * GROUPS)

        @block.gpsimd
        def _(pool):
            g = nc.gpsimd
            g.memset(xs[:, (TILES - 1) * D:], 0.0).then_inc(s_zero, 1)
            g.memset(ident[:, :], 0.0).then_inc(s_const, 1)
            g.memset(ones[:, :], 1.0).then_inc(s_const, 1)
            pool.wait_ge(s_const, 2)
            g.affine_select(out=ident[:, :], in_=ident[:, :], compare_op=ALU.not_equal, fill=1.0, base=0,
                            pattern=[[-1, P]], channel_multiplier=1).then_inc(s_const, 1)
            g.memset(blockones[:, :], 0.25).then_inc(s_const, 1)
            pool.wait_ge(s_const, 4)
            g.affine_select(out=blockones[:, :], in_=blockones[:, :], compare_op=ALU.is_ge, fill=0.0, base=0,
                            pattern=[[-DH, H]], channel_multiplier=1).then_inc(s_const, 1)
            pool.wait_ge(s_const, 5)
            g.affine_select(out=blockones[:, :], in_=blockones[:, :], compare_op=ALU.is_ge, fill=0.0, base=DH - 1,
                            pattern=[[DH, H]], channel_multiplier=-1).then_inc(s_const, 1)
            g.iota(iota_row[:, :], [[1, P]], base=0, channel_multiplier=0, allow_small_or_imprecise_dtypes=True).then_inc(s_const, 1)
            g.iota(iota_col[:, :], [[0, 1]], base=0, channel_multiplier=1, allow_small_or_imprecise_dtypes=True).then_inc(s_const, 1)
            g.memset(fill, 0.0).then_inc(s_pool, 1)
            pool.wait_ge(s_pool, 1)
            g.affine_select(out=fill, in_=fill, compare_op=ALU.not_equal, fill=-BIG, base=-1,
                            pattern=[[0, 2 * CH]], channel_multiplier=1).then_inc(s_pool, 1)
            g.memset(filli, 0).then_inc(s_pool, 1)
            pool.wait_ge(s_pool, 3)
            g.memset(fill[0:1, :], -1.0).then_inc(s_pool, 1)
            g.iota(kcol[0:TR, :], [[1, TC]], base=-LAG, channel_multiplier=TC, allow_small_or_imprecise_dtypes=True).then_inc(s_pool, 1)
            g.iota(iota_u, [[U, 64]], base=0, channel_multiplier=0, allow_small_or_imprecise_dtypes=True).then_inc(s_pool, 1)
            g.iota(thr, [[P, TILES]], base=0, channel_multiplier=0, allow_small_or_imprecise_dtypes=True).then_inc(s_pool, 1)

            pool.wait_ge(s_x, 32)
            with pool.Fori(0, GROUPS) as i:
                pool.wait_ge(s_q, i + 1)
                g.tensor_copy(xcp, xs[:, ds(i * (GRP * D), GRP * D)]).then_inc(s_xcp, 1)

            g.memset(arena[:, zero0:zero1 - U * kvw], 0.0).then_inc(s_init, 1)
            pool.wait_ge(s_cnt, 1)
            pool.wait_ge(s_pen, 2)
            pool.wait_ge(s_prev, 16)
            pool.wait_ge(s_dst_out, 16)
            pool.wait_ge(s_arr, 16 * 6)
            pool.wait_ge(s_ea, 16 * 10)
            g.memset(acc0, 0.0).then_inc(s_init, 1)
            pool.wait_ge(s_qs, GROUPS + 1)
            pool.wait_ge(s_kvo, 16 * GROUPS)
            g.memset(kv[:, (U - 1) * kvw:], 0.0).then_inc(s_kz, 1)
            g.memset(kv[:, (U - 3) * kvw:(U - 1) * kvw], 0.0).then_inc(s_kz, 1)
            pool.wait_ge(s_kz, 2)
            pool.wait_ge(s_tabi, 64)
            pool.sem_inc(s_init, 1)

            pool.wait_ge(s_init, 3)
            slot_free = pool.alloc_register("slot_free")
            landed = pool.alloc_register("landed")
            pool.reg_mov(slot_free, BASE - U + 1)
            pool.reg_mov(landed, 16)
            n0 = pool.value_load(iters_sb[0:1, 0:1], min_val=1, max_val=ITERS)
            kv_s = kv.rearrange("p (u g d) -> p u g d", u=U, g=G)
            with pool.Fori(0, n0):
                for u in range(U):
                    pool.wait_ge(s_init, 3)
                    pool.wait_ge(l_pv, slot_free)
                    pool.wait_ge(l_ix[u], landed)
                    for t in range(G):
                        g.indirect_dma_start(kv_s[:, u, t, :], None, kv_tab,
                                             bass.IndirectOffsetOnAxis(ap=v3(idx, U)[:, u, t:t + 1], axis=0)).then_inc(l_g[u], 16)
                    pool.reg_add(slot_free, slot_free, 1)
                pool.reg_add(landed, landed, 16)

            pool.wait_ge(l_over, 3)
            g.memset(con1, 1.0).then_inc(m_pool, 1)
            g.memset(eaT, 1.0).then_inc(m_pool, 1)
            g.memset(deg3, 1.0).then_inc(m_pool, 1)
            g.memset(yg, 0.0).then_inc(m_pool, 1)
            g.memset(arena[:, late + 3 * G * LW + 2 * P + GRP * 3 + U * G * D:late_end], 0.0).then_inc(m_pool, 1)

            pool.sem_inc(n_x1c, 1)
            with pool.Fori(0, GROUPS) as i:
                pool.wait_ge(n_h1, i + 1)
                g.tensor_tensor(v3(h1c, GRP), v3(h1, GRP), rows[:, 2:3, :].to_broadcast([P, GRP, D]), ALU.add).then_inc(n_h1c, 1)
                pool.wait_ge(n_x1, i + 1)
                g.tensor_copy(xs[:, ds(i * (GRP * D), GRP * D)], res).then_inc(n_x1c, 1)

            pool.wait_ge(m_pool, 5)
            pool.wait_ge(n_yo, 32 * GROUPS)
            pool.reg_mov(slot_free, BASE - U + 1)
            pool.reg_mov(landed, 16)
            n1 = pool.value_load(iters_sb[0:1, 1:2], min_val=1, max_val=ITERS)
            yg_s = yg.rearrange("p (u g d) -> p u g d", u=U, g=G)
            with pool.Fori(0, n1):
                for u in range(U):
                    pool.wait_ge(m_pool, 5)
                    pool.wait_ge(m_hid, slot_free)
                    pool.wait_ge(m_ix[u], landed)
                    for t in range(G):
                        g.indirect_dma_start(yg_s[:, u, t, :], None, y_tab,
                                             bass.IndirectOffsetOnAxis(ap=v3(idx1, U)[:, u, t:t + 1], axis=0)).then_inc(m_g[u], 16)
                    pool.reg_add(slot_free, slot_free, 1)
                pool.reg_add(landed, landed, 16)

            pool.wait_ge(m_over, 3)
            with pool.Fori(0, GROUPS) as i:
                pool.wait_ge(f_deg, i + 1)
                g.tensor_copy(fx[:, 2 * GRP * D:], xs[:, ds(i * (GRP * D), GRP * D)]).then_inc(f_x, 1)

        @block.scalar
        def _(act):
            a = nc.scalar
            row = lambda t: t.rearrange("(a n) -> a n", a=1)
            act.dma_start(w0_sb[:, :], w0).then_inc(s_w2, 16)
            act.dma_start(fc1_sb[:, :], fc1w).then_inc(s_w2, 16)
            act.dma_start(fc2_sb[:, :, :], fc2w.rearrange("(c p) d -> p c d", p=P)).then_inc(s_w2, 16)
            act.dma_start(fc1b_sb[:, :], fc1b.rearrange("(c p) -> p c", p=P), allow_slow_non_contiguous=True).then_inc(s_w2, 16)
            for k, t in enumerate((ln1g, ln1b, fc2b, ln2g, ln2b)):
                act.dma_start(rows[:, k, :], row(t).to_broadcast([P, D])).then_inc(s_w2, 16)
            for k, (w, b) in enumerate(((w1f, b1f), (w1b, b1b))):
                act.dma_start(w1x[:, k * D:(k + 1) * D], w[0:D, :]).then_inc(s_w2, 16)
                act.dma_start(w1r[:, k * D:(k + 1) * D], w[D + EA:D + 2 * EA, :]).then_inc(s_w2, 16)
                act.dma_start(b1row[:, k * D:(k + 1) * D], row(b)).then_inc(s_w2, 16)
            for k, w in enumerate((w2f, w2b, wu)):
                act.dma_start(w2wu[:, k * D:(k + 1) * D], w).then_inc(s_w2, 16)
            act.dma_start(burow[:, :], row(bu)).then_inc(s_w2, 16)
            act.dma_start(epsc[:, :], row(eps).to_broadcast([P, 1])).then_inc(s_w2, 16)
            act.wait_ge(s_blk, 3)
            for k, w in enumerate((w1f, w1b)):
                for t in range(G):
                    act.dma_start(w1blk[t * EA:(t + 1) * EA, k * CH + t * D:k * CH + (t + 1) * D],
                                  w[D:D + EA, :]).then_inc(s_w2, 16)
            act.dma_start(reql[:, G * EA:G * EA + 1], req.rearrange("a f -> f a"), allow_slow_non_contiguous=True).then_inc(s_w2, 16)
            act.dma_start(b2col[:, 0:1], b2f.rearrange("(p a) -> p a", a=1)).then_inc(s_w2, 16)
            act.dma_start(b2col[:, 1:2], b2b.rearrange("(p a) -> p a", a=1)).then_inc(s_w2, 16)

            act.sem_inc(s_kvst, 1)
            with act.Fori(0, GROUPS) as i:
                act.wait_ge(s_xTp, i + 1)
                a.activation(xT, bank(2, 2)[:, 0:GRP * P], ACT.Copy).then_inc(s_xT, 1)
                act.wait_ge(s_kv, i + 1)
                act.wait_ge(s_kvfree, i + 1)
                a.activation(kvst[:, ds((i % 2) * (GRP * 2 * D), GRP * 2 * D)], bank(4, 4)[:, 0:GRP * 2 * D], ACT.Copy).then_inc(s_kvst, 1)

            act.wait_ge(s_wmm, 1)
            a.activation(w2u[:, 0:2 * D], bank(0)[:, 0:2 * D], ACT.Copy).then_inc(s_wcp, 1)
            act.wait_ge(s_wmm, 2)
            a.activation(w1blk[G * EA:G * EA + 1, :].rearrange("p (k g d) -> p k g d", k=2, g=G),
                         bank(1)[G * EA:G * EA + 1, 0:2 * D].rearrange("p (k d) -> p k d", k=2)[:, :, None, :].to_broadcast([1, 2, G, D]),
                         ACT.Copy).then_inc(s_wcp, 1)
            act.wait_ge(s_wmm, 3)
            a.activation(w2u[:, 0:2 * D], bank(2)[:, 0:2 * D], ACT.Copy).then_inc(s_wcp, 1)
            a.activation(dbu[:, :], bank(3)[0:3, 0:D], ACT.Copy).then_inc(s_wcp, 1)

            act.wait_ge(s_init, 3)
            n0 = act.value_load(iters_sb[0:1, 0:1], min_val=1, max_val=ITERS)
            bases(act, (l_kc, 0), (l_scr, 1), (l_e, 2))
            con_s = v3(contrib, 2)
            with act.Fori(0, n0) as i:
                for u in range(U):
                    act.wait_ge(l_kt, i * U + (u + 1 + BASE))
                    act.wait_ge(l_prod, i * U + (u - 2 + 1 + BASE))
                    a.activation(v3(kts, 2)[:, u % 2, :], bank(2 + u % 2), ACT.Copy).then_inc(l_kc, 1)
                    act.wait_ge(l_s, i * U + (u - 1 + 1 + BASE))
                    a.activation(v3(scr, 2)[0:H, (u - 1) % 2, :], bank(4)[0:H, :], ACT.Copy).then_inc(l_scr, 1)
                    act.wait_ge(l_d, i * U + (u - 2 + 1 + BASE))
                    act.wait_ge(l_agg, i * U + (u - 4 + 1 + BASE))
                    dps = bank(5)[:, 0:40]
                    c = con_s[:, (u - 2) % 2, :]
                    a.activation(c[:, H:].rearrange("p (g h w) -> p g h w", g=G, h=H)[:, :, :, DH],
                                 dps[:, 0:G * H].rearrange("p (g h) -> p g h", g=G), ACT.Exp)
                    a.activation(c[0:1, 0:H], dps[0:1, G * H:G * H + H], ACT.Exp).then_inc(l_e, 1)

            a.activation(mark[:, 2:3], eps_ln[:, :], ACT.Copy).then_inc(l_over, 1)
            act.wait_ge(l_over, 3)

            act.sem_inc(n_ys, 1)
            with act.Fori(0, GROUPS) as i:
                act.wait_ge(n_aTp, i + 1)
                a.activation(nT, bank(0, 2)[:, 0:GRP * P], ACT.Copy).then_inc(n_aT, 1)
                act.wait_ge(n_var, 3 * i + 1)
                a.activation(sd, v3(mv, GRP)[:, :, 1], ACT.Sqrt, bias=eps_ln[:, :]).then_inc(n_sd, 1)
                act.wait_ge(n_hTp, i + 1)
                a.activation(nT, bank(0, 2)[:, 0:GRP * P], ACT.Copy).then_inc(n_hT, 1)
                for c in range(FC):
                    act.wait_ge(n_f1, FC * i + (c + 1))
                    a.activation(v3(ffT, FC)[:, c, :], bank(4 + 2 * (c % 2), 2)[:, 0:GRP * P], ACT.Relu,
                                 bias=fc1b_sb[:, c:c + 1]).then_inc(n_f1s, 1)
                for k in (2, 3):
                    act.wait_ge(n_var, 3 * i + k)
                    a.activation(sd, v3(mv, GRP)[:, :, 1], ACT.Sqrt, bias=eps_ln[:, :]).then_inc(n_sd, 1)
                act.wait_ge(n_xTp, i + 1)
                a.activation(nT, bank(0, 2)[:, 0:GRP * P], ACT.Copy).then_inc(n_xT, 1)
                act.wait_ge(n_y, i + 1)
                act.wait_ge(n_yfree, i + 1)
                a.activation(yst, bank(4, 4)[:, 0:GRP * 2 * D], ACT.Copy).then_inc(n_ys, 1)

            act.wait_ge(m_pool, 5)
            bases(act, (m_eT, 0), (m_con, 1))
            n1 = act.value_load(iters_sb[0:1, 1:2], min_val=1, max_val=ITERS)
            hid_s = v3(hid, 2)
            con1_s = con1.rearrange("p (u g w) -> p u g w", u=3, g=G)
            with act.Fori(0, n1) as i:
                for u in range(U):
                    act.wait_ge(m_eTp, i * U + (u + 1 + BASE))
                    a.activation(v3(eaT, 2)[0:G * EA, u % 2, :], bank(4 * (u % 2))[0:G * EA, 0:P], ACT.Copy).then_inc(m_eT, 1)
                    act.wait_ge(m_hid, i * U + (u - 1 + 1 + BASE))
                    act.wait_ge(m_agg, i * U + (u - 4 + 1 + BASE))
                    a.activation(con1_s[:, (u - 1) % 3, :, 0:D], v3(hid_s[:, (u - 1) % 2, :], G), ACT.Relu).then_inc(m_con, 1)

            a.activation(mark[:, 3:4], eps_ln[:, :], ACT.Copy).then_inc(m_over, 1)
            act.wait_ge(m_over, 3)

            act.sem_inc(f_r, 1)
            with act.Fori(0, GROUPS) as i:
                act.wait_ge(f_deg, i + 1)
                a.activation(v3(fx[:, GRP * D:2 * GRP * D], GRP),
                             v3(acc1[:, ds(i * (GRP * LW) + TILES * LW, GRP * LW)], GRP)[:, :, 0:D], ACT.Copy).then_inc(f_b, 1)
                act.wait_ge(f_tp, i + 2)
                a.activation(aT, bank(0, 6)[:, :].rearrange("p (k n) -> p k n", k=3)[:, :, 0:GRP * P], ACT.Copy)
                a.activation(degT[0:3, :], bank(6, 2)[0:3, 0:GRP * P], ACT.Copy).then_inc(f_t, 1)
                act.wait_ge(f_o, i + 1)
                a.activation(fin, bank(0, 2)[:, 0:GRP * D], ACT.Relu).then_inc(f_r, 1)
                act.wait_ge(f_var, i + 1)
                a.activation(fsd, v3(fmv, GRP)[:, :, 1], ACT.Sqrt, bias=eps_ln[:, :]).then_inc(f_sd, 1)

        @block.tensor
        def _(pe):
            mm = nc.tensor.matmul
            tp = nc.tensor.transpose
            pe.wait_ge(s_const, 8)
            pe.wait_ge(s_bank, 1)
            pe.wait_ge(s_w, 48)
            pe.sem_inc(s_q, 1)
            with pe.Fori(0, GROUPS) as i:
                pe.wait_ge(s_xcp, i + 1)
                for t in range(GRP):
                    last = tp(bank(2, 2)[:, t * P:(t + 1) * P], xcp[:, t * D:(t + 1) * D], ident[:, :])
                last.then_inc(s_xTp, 1)
                pe.wait_ge(s_xT, i + 1)
                pe.wait_ge(s_qs, i + 1)
                for t in range(GRP):
                    last = mm(bank(0, 2)[:, t * D:(t + 1) * D], xT[:, t * P:(t + 1) * P], wqkv[:, 0:D])
                last.then_inc(s_q, 1)
                pe.wait_ge(s_kvst, i + 1)
                for t in range(GRP):
                    last = mm(bank(4, 4)[:, t * 2 * D:(t + 1) * 2 * D], xT[:, t * P:(t + 1) * P], wqkv[:, D:3 * D])
                last.then_inc(s_kv, 1)

            pe.wait_ge(s_cnt, 1)
            pe.wait_ge(s_kvst, GROUPS + 1)
            mm(bank(7)[:, 0:VT], ones[0:EP, :], cnt[0:EP, 0:VT]).then_inc(s_seg, 1)
            pe.wait_ge(s_w2, 16 * (9 + 6 + 5 + 8 + 3))
            pe.wait_ge(s_blk, 7)
            pe.wait_ge(s_qs, GROUPS + 1)
            for k in range(2):
                last = tp(bank(0)[:, k * D:(k + 1) * D], w2wu[:, k * D:(k + 1) * D], ident[:, :])
            last.then_inc(s_wmm, 1)
            for k in range(2):
                mm(bank(1)[0:G * EA + 1, k * D:(k + 1) * D], reql[:, :], w1r[:, k * D:(k + 1) * D], start=True, stop=False)
                last = mm(bank(1)[0:G * EA + 1, k * D:(k + 1) * D], reql_one[:, :], b1row[:, k * D:(k + 1) * D], start=False, stop=True)
            last.then_inc(s_wmm, 1)
            pe.wait_ge(s_wcp, 1)
            for k in range(2):
                mm(bank(2)[:, k * D:(k + 1) * D], w2u[:, k * D:(k + 1) * D], w2wu[:, 2 * D:3 * D])
            mm(bank(3)[0:3, 0:D], b2col[:, :], w2wu[:, 2 * D:3 * D], start=True, stop=False)
            mm(bank(3)[0:3, 0:D], sel3[:, :], burow[:, :], start=False, stop=True).then_inc(s_wmm, 1)

            pe.wait_ge(s_init, 3)
            pe.wait_ge(s_wcp, 4)
            n0 = pe.value_load(iters_sb[0:1, 0:1], min_val=1, max_val=ITERS)
            kv_s = kv.rearrange("p (u g d) -> p u g d", u=U, g=G)
            st_s = v3(st, U)
            con_s = v3(contrib, 2)
            bases(pe, (l_kt, 0), (l_kq, 0), (l_s, 1), (l_d, 2), (l_agg, 3))
            with pe.Fori(0, n0) as i:
                for u in range(U):
                    tile = pe.value_load(tab_sb[0][0:1, ds(4 * (i * U + (u + LAG)) + 1, 1)], min_val=0, max_val=TILES - 1)
                    pe.wait_ge(l_g[u], (i + 1) * (16 * G))
                    pe.wait_ge(l_kc, i * U + (u - 2 + 1 + BASE))
                    for t in range(G):
                        last = tp(bank(2 + u % 2)[:, t * P:(t + 1) * P], kv_s[:, u, t, 0:D], ident[:, :])
                    last.then_inc(l_kt, 1)
                    pe.wait_ge(l_hot, i * U + (u + 1 + BASE))
                    pe.wait_ge(l_prod, i * U + (u - 2 + 1 + BASE))
                    for k in range(3):
                        last = mm(bank(u % 2), qsp[:, ds(tile * (3 * D) + k * D, D)], st_s[:, u, :], start=(k == 0), stop=(k == 2))
                    last.then_inc(l_kq, 1)
                    pe.wait_ge(l_prod, i * U + (u - 1 + 1 + BASE))
                    pe.wait_ge(l_scr, i * U + (u - 2 + 1 + BASE))
                    mm(bank(4)[0:H, :], blockones[:, :], v3(prod, 2)[:, (u - 1) % 2, :]).then_inc(l_s, 1)
                    pe.wait_ge(l_c, i * U + (u - 2 + 1 + BASE))
                    pe.wait_ge(l_e, i * U + (u - 3 + 1 + BASE))
                    dps = bank(5)[:, 0:40]
                    sc = v3(scr, 2)[0:H, (u - 2) % 2, :].rearrange("h (p g) -> h g p", g=G)
                    cm = v3(cmx, 2)[0:H, (u - 2) % 2, :].rearrange("h (p g) -> h g p", g=G)
                    for t in range(G):
                        mm(dps[:, t * H:(t + 1) * H], sc[:, t, :], ident[0:H, 0:H], start=True, stop=False)
                        mm(dps[:, t * H:(t + 1) * H], cm[:, t, :], ident_neg[:, :], start=False, stop=True)
                    mm(dps[0:1, G * H:G * H + H], ucar[0:H, (u - 2) % 2:(u - 2) % 2 + 1], ident[0:H, 0:H], start=True, stop=False)
                    mm(dps[0:1, G * H:G * H + H], cm[:, 0, 0:1], ident_neg[:, :], start=False, stop=True).then_inc(l_d, 1)
                    pe.wait_ge(l_pv, i * U + (u - 3 + 1 + BASE))
                    pe.wait_ge(l_acc, i * U + (u - 5 + 1 + BASE))
                    agg = bank(6 + (u - 3) % 2)[:, 0:H + RW]
                    c = con_s[:, (u - 3) % 2, :]
                    hot = s_hot.rearrange("p (u g n) -> p u g n", u=U, g=G)[:, (u - 3) % U]
                    mm(agg, hot[:, 0, :], c[:, 0:H + RW], start=True, stop=False)
                    for t in range(1, G):
                        last = mm(agg[:, H:], hot[:, t, :], c[:, H + t * RW:H + (t + 1) * RW], start=False, stop=(t == G - 1))
                    last.then_inc(l_agg, 1)

            mm(bank(1)[0:1, 0:1], ones[:, 0:1], ones[:, 0:1]).then_inc(l_over, 1)
            pe.wait_ge(l_over, 3)

            with pe.Fori(0, GROUPS) as i:
                pe.wait_ge(n_a, i + 1)
                for t in range(GRP):
                    last = tp(bank(0, 2)[:, t * P:(t + 1) * P], av[:, t * D:(t + 1) * D], ident[:, :])
                last.then_inc(n_aTp, 1)
                pe.wait_ge(n_aT, i + 1)
                for t in range(GRP):
                    last = mm(bank(2, 2)[:, t * D:(t + 1) * D], nT[:, t * P:(t + 1) * P], w0_sb[:, :])
                last.then_inc(n_emb, 1)
                pe.wait_ge(n_h1, i + 1)
                for t in range(GRP):
                    last = tp(bank(0, 2)[:, t * P:(t + 1) * P], h1[:, t * D:(t + 1) * D], ident[:, :])
                last.then_inc(n_hTp, 1)
                pe.wait_ge(n_hT, i + 1)
                pe.wait_ge(n_ys, i + 1)
                for c in range(FC):
                    if c >= 2:
                        pe.wait_ge(n_f1s, FC * i + (c - 1))
                    for a0, a1 in ((0, 512), (512, GRP * P)):
                        last = mm(bank(4 + 2 * (c % 2), 2)[:, a0:a1], fc1_sb[:, c * P:(c + 1) * P], nT[:, a0:a1])
                    last.then_inc(n_f1, 1)
                pe.wait_ge(n_f1s, FC * i + FC)
                for t in range(GRP):
                    for c in range(FC):
                        last = mm(bank(2, 2)[:, t * D:(t + 1) * D], v3(ffT, FC)[:, c, t * P:(t + 1) * P], fc2_sb[:, c, :],
                                  start=(c == 0), stop=(c == FC - 1))
                last.then_inc(n_f2, 1)
                pe.wait_ge(n_x1, i + 1)
                for t in range(GRP):
                    last = tp(bank(0, 2)[:, t * P:(t + 1) * P], res[:, t * D:(t + 1) * D], ident[:, :])
                last.then_inc(n_xTp, 1)
                pe.wait_ge(n_xT, i + 1)
                for t in range(GRP):
                    last = mm(bank(4, 4)[:, t * 2 * D:(t + 1) * 2 * D], nT[:, t * P:(t + 1) * P], w1x[:, :])
                last.then_inc(n_y, 1)

            pe.wait_ge(m_pool, 5)
            pe.wait_ge(n_ys, GROUPS + 1)
            bases(pe, (m_eTp, 0), (m_u, 1), (m_agg, 2))
            n1 = pe.value_load(iters_sb[0:1, 1:2], min_val=1, max_val=ITERS)
            con1_s = con1.rearrange("p (u g w) -> p u g w", u=3, g=G)
            hot1 = s1.rearrange("p (u g n) -> p u g n", u=U, g=G)
            with pe.Fori(0, n1) as i:
                for u in range(U):
                    way = pe.value_load(tab_sb[1][0:1, ds(4 * (i * U + (u + LAG - 1)) + 3, 1)], min_val=0, max_val=1)
                    pe.wait_ge(m_ld[u], (i + 1) * 32)
                    pe.wait_ge(m_g[u], (i + 1) * (16 * G))
                    pe.wait_ge(m_eT, i * U + (u - 2 + 1 + BASE))
                    tp(bank(4 * (u % 2))[:, 0:P], v3(eat, U)[:, u, :], ident[:, :]).then_inc(m_eTp, 1)
                    pe.wait_ge(m_eT, i * U + (u - 1 + 1 + BASE))
                    pe.wait_ge(m_hid, i * U + (u - 3 + 1 + BASE))
                    mm(bank(1 + (u - 1) % 2), v3(eaT, 2)[0:G * EA + 1, (u - 1) % 2, :], w1blk[:, ds(way * CH, CH)]).then_inc(m_u, 1)
                    pe.wait_ge(m_con, i * U + (u - 2 + 1 + BASE))
                    pe.wait_ge(m_acc, i * U + (u - 4 + 1 + BASE))
                    agg = bank(3 + 2 * ((u - 2) % 2))[:, 0:LW]
                    for t in range(G):
                        last = mm(agg, hot1[:, (u - 2) % U, t, :], con1_s[:, (u - 2) % 3, t, :], start=(t == 0), stop=(t == G - 1))
                    last.then_inc(m_agg, 1)

            mm(bank(7)[0:1, 0:1], ones[:, 0:1], ones[:, 0:1]).then_inc(m_over, 1)
            pe.wait_ge(m_over, 3)

            pe.sem_inc(f_tp, 1)
            with pe.Fori(0, GROUPS) as i:
                pe.wait_ge(f_deg, i + 1)
                pe.wait_ge(f_b, i + 1)
                pe.wait_ge(f_x, i + 1)
                pe.wait_ge(f_r, i + 1)
                for t in range(GRP):
                    for k in range(3):
                        tp(bank(2 * k, 2)[:, t * P:(t + 1) * P], fx[:, (k * GRP + t) * D:(k * GRP + t + 1) * D], ident[:, :])
                    last = mm(bank(6, 2)[0:3, t * P:(t + 1) * P], v3(deg3, GRP)[:, t, :], ident[:, :])
                last.then_inc(f_tp, 1)
                pe.wait_ge(f_t, i + 1)
                for t in range(GRP):
                    for k in range(3):
                        mm(bank(0, 2)[:, t * D:(t + 1) * D], aT[:, (k * GRP + t) * P:(k * GRP + t + 1) * P], w2u[:, k * D:(k + 1) * D],
                           start=(k == 0), stop=False)
                    last = mm(bank(0, 2)[:, t * D:(t + 1) * D], degT[0:3, t * P:(t + 1) * P], dbu[:, :], start=False, stop=True)
                last.then_inc(f_o, 1)

        @block.vector
        def _(dve):
            v = nc.vector
            tt, ts = v.tensor_tensor, v.tensor_scalar
            link = linker(dve, s_dv)

            v.memset(ps[:, :], 0.0).then_inc(s_bank, 1)
            v.memset(w1blk[:, :], 0.0).then_inc(s_blk, 1)
            v.memset(reql[:, :], 0.0).then_inc(s_blk, 1)
            v.memset(b2col[:, :], 0.0).then_inc(s_blk, 1)
            v.memset(reql_one[:, :], 0.0)
            link(v.memset(sel3[:, :], 0.0))
            v.memset(reql_one[:, G * EA:], 1.0).then_inc(s_blk, 1)
            v.memset(sel3[:, 2:3], 1.0).then_inc(s_blk, 1)
            v.memset(eps_ln[:, :], EPS).then_inc(s_blk, 1)
            dve.wait_ge(s_const, 8)
            ts(ident_neg[:, :], ident[0:H, 0:H], -1.0, None, ALU.mult).then_inc(s_blk, 1)

            dve.wait_ge(s_dst, 32)
            d3 = v3(dstf, 2)
            v.tensor_copy(dstf[0:EP], dsti[0:EP]).then_inc(s_pre, 1)
            dve.wait_ge(s_pre, 1)
            ts(srcb[0:EP], v3(srci, 2)[0:EP, 1, :], float(NPAD), None, ALU.add).then_inc(s_pen, 1)
            dve.wait_ge(s_pool, 7)
            with dve.Fori(0, TILES) as i:
                for h in range(2):
                    link(ts(v3(cmpj, 2)[0:EP, h, :], d3[0:EP, h, :], thr[0:EP, ds(i, 1)], 0.0, ALU.is_lt, ALU.add,
                            accum_out=cnt[0:EP, ds(h * TILES + i, 1)]))
            v.tensor_copy(cmpj[0:EP, 0:1], cmpj[0:EP, 1:2]).then_inc(s_cnt, 1)

            dve.wait_ge(s_prev, 16)
            link(tt(dprev[0:EP], dprev[0:EP], dstf[0:EP], ALU.not_equal))
            ts(dprev[0:EP], dprev[0:EP], -BIG, None, ALU.mult).then_inc(s_pen, 1)

            dve.sem_inc(s_qs, 1)
            with dve.Fori(0, GROUPS) as i:
                dve.wait_ge(s_q, i + 2)
                q = v3(bank(0, 2)[:, 0:GRP * D], GRP)
                part = qsp[:, ds(i * (GRP * 3 * D), GRP * 3 * D)].rearrange("p (t k d) -> p t k d", t=GRP, k=3)
                r = v3(qres, GRP)
                link(v.tensor_copy(part[:, :, 0, :], q))
                link(tt(r, q, part[:, :, 0, :], ALU.subtract))
                link(v.tensor_copy(part[:, :, 1, :], r))
                tt(part[:, :, 2, :], r, part[:, :, 1, :], ALU.subtract).then_inc(s_qs, 1)

            dve.wait_ge(s_seg, 1)
            link(v.tensor_copy(seg, bank(7)[:, 0:VT]))
            for l in (1, 0):
                nv = (TILES, VT)[l]
                end = (E, END1)[l]
                if l:
                    s2, n2 = v3(seg, 2), v3(nch, 2)
                    link(tt(n2[:, :, 0:TILES - 1], s2[:, :, 1:TILES], s2[:, :, 0:TILES - 1], ALU.subtract))
                    link(ts(n2[:, :, TILES - 1:TILES], s2[:, :, TILES - 1:TILES], -1.0, float(HALF), ALU.mult, ALU.add))
                    v.tensor_copy(spos[:, 0:TILES], seg[:, 0:TILES])
                    link(ts(spos[:, TILES:VT], seg[:, TILES:VT], float(BASE1), None, ALU.add))
                else:
                    link(tt(spos[:, 0:nv], seg[:, 0:TILES], seg[:, TILES:VT], ALU.add))
                    link(tt(nch[:, 0:nv - 1], spos[:, 1:nv], spos[:, 0:nv - 1], ALU.subtract))
                    link(ts(nch[:, nv - 1:nv], spos[:, nv - 1:nv], -1.0, float(E), ALU.mult, ALU.add))
                link(ts(nchi[:, 0:nv], nch[:, 0:nv], float(CH - 1), None, ALU.add))
                link(ts(nchi[:, 0:nv], nchi[:, 0:nv], CH.bit_length() - 1, None, ALU.arith_shift_right))
                link(v.tensor_copy(nch[:, 0:nv], nchi[:, 0:nv]))
                link(v.tensor_tensor_scan(cum[:, 0:nv], ones[:, 0:nv], nch[:, 0:nv], 0.0, op0=ALU.mult, op1=ALU.add))
                link(tt(nch[:, 0:nv], cum[:, 0:nv], nch[:, 0:nv], ALU.subtract))
                link(ts(nch[:, 0:nv], nch[:, 0:nv], -float(CH), None, ALU.mult))
                link(tt(spos[:, 0:nv], spos[:, 0:nv], nch[:, 0:nv], ALU.add))
                link(ts(col[0:1, 0:1], cum[0:1, nv - 1:nv], float(LAG), None, ALU.add))
                link(ts(hotv[0:1, 0:64], iota_u[0:1, :], col[0:1, 0:1], 0.0, ALU.is_lt, ALU.add, accum_out=col[0:1, 1:2]))
                link(v.tensor_copy(iters_sb[0:1, l:l + 1], col[0:1, 1:2]))
                k = kcol[0:TR, :]
                c = lambda n: col[0:TR, n * TC:(n + 1) * TC]
                which, below, off, tile, way, summed = (c(n) for n in range(6))
                for j in range(TC):
                    link(ts(hotv[0:TR, 0:nv], cum[0:TR, 0:nv], k[:, j:j + 1], 0.0, ALU.is_le, ALU.add, accum_out=which[:, j:j + 1]))
                link(ts(below, k, 0.0, float(nv), ALU.is_lt, ALU.mult))
                link(tt(which, which, below, ALU.add))
                for j in range(TC):
                    link(ts(hotv[0:TR, 0:nv], iota_row[0:TR, 0:nv], which[:, j:j + 1], None, ALU.is_equal))
                    link(tt(hotv[0:TR, 0:nv], hotv[0:TR, 0:nv], spos[0:TR, 0:nv], ALU.mult))
                    link(v.tensor_reduce(off[:, j:j + 1], hotv[0:TR, 0:nv], AX_X, ALU.add))
                link(ts(tile, k, float(CH), None, ALU.mult))
                link(tt(off, off, tile, ALU.add))
                link(ts(below, which, float(nv), float(2 * end), ALU.is_ge, ALU.mult))
                link(tt(off, off, below, ALU.add))
                link(ts(off, off, float(end), None, ALU.min))
                link(ts(way, which, float(TILES), None, ALU.is_ge))
                link(ts(tile, way, -float(TILES * l), None, ALU.mult))
                link(tt(tile, tile, which, ALU.add))
                link(ts(tile, tile, float(TILES - 1), None, ALU.min))
                entry = tbe[0:TR, 16 * l:16 * l + 12].bitcast(I32).rearrange("p (c f) -> p c f", c=TC)
                v.tensor_copy(entry[:, :, 0], off)
                v.tensor_copy(entry[:, :, 1], tile)
                v.tensor_copy(entry[:, :, 2], which)
                v.tensor_copy(entry[:, :, 3], way)
                link(ts(tbe[0:TR, 32 + 4 * l:32 + 4 * l + TC], tile, -float(P), None, ALU.mult))
            dve.sem_inc(s_tab, 1)
            dve.wait_ge(s_tabi, 64)
            ts(pj[:, :], nj[0][:, :], -1.0, iota_col[:, :], ALU.mult, ALU.add).then_inc(s_pj, 1)
            dve.wait_ge(s_pj, 1)

            dve.wait_ge(s_w2, 16 * 31)
            link(ts(epsc[:, :], epsc[:, :], 1.0, None, ALU.add))
            ts(w2u[:, 2 * D:3 * D], w2wu[:, 2 * D:3 * D], epsc[:, :], None, ALU.mult).then_inc(s_wu, 1)
            dve.wait_ge(s_wu, 1)

            dve.wait_ge(s_init, 3)
            dve.wait_ge(s_wcp, 4)
            n0 = dve.value_load(iters_sb[0:1, 0:1], min_val=1, max_val=ITERS)
            bases(dve, (l_hot, 0), (l_prod, 1), (l_f, 2), (l_c, 2), (l_pv, 3), (l_acc, 4))
            kv_s = kv.rearrange("p (u g d) -> p u g d", u=U, g=G)
            hot = s_hot.rearrange("p (u g n) -> p u g n", u=U, g=G)
            pen_s = v3(pen, 3)
            F, C, SC = v3(fmx, 2), v3(cmx, 2), v3(scr, 2)
            con_s = v3(contrib, 2)
            with dve.Fori(0, n0) as i:
                for u in range(U):
                    dve.wait_ge(l_ld[u], (i + 1) * 48)
                    entry = i * U + (u + LAG)
                    ts(v3(st, U)[:, u, :], v3(drow, 3)[:, u % 3, :], pj[:, ds(entry, 1)], None, ALU.is_equal)
                    for t in range(G):
                        last = ts(hot[:, u, t, :], iota_row[:, :], v3(dcol, U)[:, u, t:t + 1], nj[0][:, ds(entry, 1)],
                                  ALU.subtract, ALU.is_equal)
                    last.then_inc(l_hot, 1)
                    dve.wait_ge(l_kc, i * U + (u - 1 + 1 + BASE))
                    dve.wait_ge(l_kq, i * U + (u - 1 + 1 + BASE))
                    tt(v3(prod, 2)[:, (u - 1) % 2, :].rearrange("d (p g) -> d p g", g=G),
                       bank((u - 1) % 2).rearrange("d (p g) -> d p g", g=G),
                       v3(kts, 2)[:, (u - 1) % 2, :].rearrange("d (g p) -> d p g", g=G), ALU.mult).then_inc(l_prod, 1)
                    w = (u - 2) % 2
                    dve.wait_ge(l_scr, i * U + (u - 2 + 1 + BASE))
                    dve.wait_ge(l_c, i * U + (u - 3 + 1 + BASE))
                    before = F[0:H, 1 - w, CH - 1:CH]
                    pn = pen_s[0:H, (u - 2) % 3, :]
                    tt(ucar[0:H, w:w + 1], before, pn[:, 0:1], ALU.add)
                    v.tensor_tensor_scan(F[0:H, w, :], pn[:, 0:CH], SC[0:H, w, :], before, op0=ALU.add, op1=ALU.max).then_inc(l_f, 1)
                    dve.wait_ge(l_f, i * U + (u - 2 + 1 + BASE))
                    v.tensor_tensor_scan(C[0:H, w, ::-1], pn[:, CH:0:-1], F[0:H, w, ::-1], -BIG, op0=ALU.add, op1=ALU.max).then_inc(l_c, 1)
                    dve.wait_ge(l_e, i * U + (u - 3 + 1 + BASE))
                    c = con_s[:, (u - 3) % 2, :]
                    rows_ = c[:, H:].rearrange("p (g h w) -> p g h w", g=G, h=H)
                    ts(c[0:1, 0:H], c[0:1, 0:H], 1.0, None, ALU.subtract)
                    for t in range(G):
                        last = tt(rows_[:, t, :, 0:DH], kv_s[:, (u - 3) % U, t, D:2 * D].rearrange("p (h w) -> p h w", h=H),
                                  rows_[:, t, :, DH:AW].to_broadcast([P, H, DH]), ALU.mult)
                    last.then_inc(l_pv, 1)
                    into = dve.value_load(tab_sb[0][0:1, ds(4 * (i * U + u) + 2, 1)], min_val=0, max_val=TILES)
                    sums = acc0[:, ds(into * RW, RW)].rearrange("p (h w) -> p h w", h=H)
                    agg = bank(6 + (u - 4) % 2)[:, 0:H + RW]
                    dve.wait_ge(l_agg, i * U + (u - 4 + 1 + BASE))
                    dve.wait_ge(l_acc, i * U + (u - 5 + 1 + BASE))
                    link(ts(rsc, agg[:, 0:H], 1.0, None, ALU.add))
                    at = atmp.rearrange("p (h w) -> p h w", h=H)
                    link(tt(at, sums, rsc[:, :, None].to_broadcast([P, H, AW]), ALU.mult))
                    tt(sums, at, agg[:, H:].rearrange("p (h w) -> p h w", h=H), ALU.add).then_inc(l_acc, 1)
            v.memset(mark[:, 0:1], 0.0).then_inc(l_over, 1)
            dve.wait_ge(l_over, 3)

            def normalise(to, t3, var, sdev, got, std_, mv_, sd_, rs_, inc=None):
                for t in range(GRP):
                    last = v.bn_stats(std_[:, t * 6:(t + 1) * 6], t3[:, t, :])
                link(last, apart=True)
                for t in range(GRP):
                    last = v.bn_aggr(mv_[:, 2 * t:2 * t + 2], std_[:, t * 6:(t + 1) * 6])
                last.then_inc(var, 1)
                dve.wait_ge(sdev, got)
                link(v.reciprocal(rs_, sd_))
                for t in range(GRP):
                    last = ts(to[:, t, :], t3[:, t, :], mv_[:, 2 * t:2 * t + 1], rs_[:, t:t + 1], ALU.subtract, ALU.mult)
                return last

            r3, h3, hc3, a4 = v3(res, GRP), v3(h1, GRP), v3(h1c, GRP), av.rearrange("p (t h w) -> p t h w", t=GRP, h=H)
            rowb = lambda k: rows[:, k:k + 1, :].to_broadcast([P, GRP, D])
            rd = rden.rearrange("p (t h) -> p t h", t=GRP)
            with dve.Fori(0, GROUPS) as i:
                sums = acc0[:, ds(i * (GRP * RW), GRP * RW)].rearrange("p (t h w) -> p t h w", t=GRP, h=H)
                xg = v3(xs[:, ds(i * (GRP * D), GRP * D)], GRP)
                link(ts(rd, sums[:, :, :, DH], 1e-9, None, ALU.add))
                link(v.reciprocal(rd, rd))
                tt(a4, sums[:, :, :, 0:DH], rd[:, :, :, None].to_broadcast([P, GRP, H, DH]), ALU.mult).then_inc(n_a, 1)
                dve.wait_ge(n_emb, i + 1)
                dve.wait_ge(n_x1c, i + 1)
                link(tt(r3, xg, v3(bank(2, 2)[:, 0:GRP * D], GRP), ALU.add))
                link(normalise(r3, r3, n_var, n_sd, 3 * i + 1, stats, mv, sd, rs))
                link(tt(r3, r3, rowb(0), ALU.mult))
                tt(h3, r3, rowb(1), ALU.add).then_inc(n_h1, 1)
                dve.wait_ge(n_f2, i + 1)
                dve.wait_ge(n_h1c, i + 1)
                link(tt(r3, hc3, v3(bank(2, 2)[:, 0:GRP * D], GRP), ALU.add))
                link(normalise(r3, r3, n_var, n_sd, 3 * i + 2, stats, mv, sd, rs))
                link(tt(r3, r3, rowb(3), ALU.mult))
                link(tt(r3, r3, rowb(4), ALU.add))
                link(tt(r3, r3, xg, ALU.add))
                normalise(r3, r3, n_var, n_sd, 3 * i + 3, stats, mv, sd, rs).then_inc(n_x1, 1)

            dve.wait_ge(n_y, GROUPS)
            dve.wait_ge(n_x1c, GROUPS + 1)
            v.memset(acc1, 0.0).then_inc(m_zero, 1)
            dve.wait_ge(m_zero, 1)
            dve.wait_ge(m_pool, 5)
            n1 = dve.value_load(iters_sb[0:1, 1:2], min_val=1, max_val=ITERS)
            bases(dve, (m_hot, 0), (m_hid, 1), (m_acc, 3))
            hot1 = s1.rearrange("p (u g n) -> p u g n", u=U, g=G)
            with dve.Fori(0, n1) as i:
                for u in range(U):
                    dve.wait_ge(m_ld[u], (i + 1) * 32)
                    entry = i * U + (u + LAG)
                    for t in range(G):
                        last = ts(hot1[:, u, t, :], iota_row[:, :], v3(dcol1, U)[:, u, t:t + 1], nj[1][:, ds(entry, 1)],
                                  ALU.subtract, ALU.is_equal)
                    last.then_inc(m_hot, 1)
                    dve.wait_ge(m_u, i * U + (u - 1 + 1 + BASE))
                    dve.wait_ge(m_con, i * U + (u - 3 + 1 + BASE))
                    tt(v3(hid, 2)[:, (u - 1) % 2, :], bank(1 + (u - 1) % 2), v3(yg, U)[:, (u - 1) % U, :], ALU.add).then_inc(m_hid, 1)
                    into = dve.value_load(tab_sb[1][0:1, ds(4 * (i * U + (u + LAG - 3)) + 2, 1)], min_val=0, max_val=VT)
                    dve.wait_ge(m_agg, i * U + (u - 3 + 1 + BASE))
                    dve.wait_ge(m_acc, i * U + (u - 4 + 1 + BASE))
                    sums = acc1[:, ds(into * LW, LW)]
                    tt(sums, sums, bank(3 + 2 * ((u - 3) % 2))[:, 0:LW], ALU.add).then_inc(m_acc, 1)

            d33, f3, o3 = v3(deg3, GRP), v3(fin, GRP), v3(fout, GRP)
            v.memset(mark[:, 1:2], 0.0).then_inc(m_over, 1)
            dve.wait_ge(m_over, 3)
            with dve.Fori(0, GROUPS) as i:
                xg = v3(xs[:, ds(i * (GRP * D), GRP * D)], GRP)
                dve.wait_ge(f_tp, i + 1)
                for k in range(2):
                    part = v3(acc1[:, ds(i * (GRP * LW) + k * TILES * LW, GRP * LW)], GRP)
                    v.tensor_copy(d33[:, :, k:k + 1], part[:, :, D:LW])
                v.tensor_copy(v3(fx[:, 0:GRP * D], GRP), v3(acc1[:, ds(i * (GRP * LW), GRP * LW)], GRP)[:, :, 0:D]).then_inc(f_deg, 1)
                dve.wait_ge(f_r, i + 2)
                link(tt(f3, f3, xg, ALU.add))
                dve.wait_ge(f_free, i + 1)
                normalise(o3, f3, f_var, f_sd, i + 1, fstats, fmv, fsd, frs).then_inc(f_out, 1)


_INS = ['x', 'src', 'dst', 'edge_attr_16', 'L0_gnn_Wq', 'L0_gnn_Wk', 'L0_gnn_Wv', 'L0_gnn_W0', 'L0_gnn_ln1_g',
        'L0_gnn_ln1_b', 'L0_gnn_fc1_w', 'L0_gnn_fc1_b', 'L0_gnn_fc2_w', 'L0_gnn_fc2_b', 'L0_gnn_ln2_g', 'L0_gnn_ln2_b',
        'L1_gnn_req_emb', 'L1_gnn_W1f', 'L1_gnn_b1f', 'L1_gnn_W2f', 'L1_gnn_b2f', 'L1_gnn_W1b', 'L1_gnn_b1b',
        'L1_gnn_W2b', 'L1_gnn_b2b', 'L1_gnn_Wu', 'L1_gnn_bu', 'L1_gnn_eps']
_OUTS = [((6250, 128), 'float32')]


def kernel(**inputs):
    import numpy as _np
    import concourse.bacc as _bacc
    from concourse import mybir as _mybir
    from concourse.bass_utils import run_bass_kernel_spmd as _run

    nc = _bacc.Bacc("TRN2", target_bir_lowering=False, num_devices=1)
    arrays, args = {}, []
    for name in _INS:
        a = _np.ascontiguousarray(inputs[name])
        arrays[f"in_{name}_dram"] = a
        args.append(nc.dram_tensor(f"in_{name}_dram", a.shape, _mybir.dt.from_np(a.dtype), kind="ExternalInput").ap())
    for i, (shape, dtype) in enumerate(_OUTS):
        dt = _mybir.dt.from_np(_np.dtype(dtype))
        args.append(nc.dram_tensor(f"out_{i}_dram", shape, dt, kind="ExternalOutput").ap())
    gnn_kernel(nc, *args)
    r = _run(nc, [arrays], core_ids=[0])
    got = tuple(r.results[0][f"out_{i}_dram"] for i in range(len(_OUTS)))
    return got[0]
```

```python
from contextlib import ExitStack

import concourse.bass as bass
from concourse import mybir

F32 = mybir.dt.float32
BF16 = mybir.dt.bfloat16
I32 = mybir.dt.int32
ALU = mybir.AluOpType
ACT = mybir.ActivationFunctionType
AX_X = mybir.AxisListType.X
ds = bass.ds

P = 128
N = 6250
D = 128
E = 100000
H = 8
DH = D // H
FF = 512
FC = FF // P
EA = 16
HALF = E // 2
EPS = 1e-5
BIG = 1e30

TILES = -(-N // P)
GRP = 7
GROUPS = TILES // GRP
LAST = N - (TILES - 1) * P
NPAD = TILES * P
G = 4
CH = G * P
VT = 2 * TILES
BASE1 = -(-(HALF + CH) // CH) * CH
END1 = BASE1 + HALF
CP = 32
AW = DH + 1
RW = H * AW
LW = D + 1

U = 6
LAG = 4
TR, TC = 88, 3
TE = TR * TC
ITERS = -(-((E + (CH - 1) * (TILES + 1)) // CH + LAG) // U)
assert ITERS * U + LAG <= TE
BASE = 8
EP, EQ = 125, 400


def gnn_kernel(nc, x, src, dst, ea, wq, wk, wv, w0, ln1g, ln1b, fc1w, fc1b, fc2w, fc2b, ln2g, ln2b,
               req, w1f, b1f, w2f, b2f, w1b, b1b, w2b, b2b, wu, bu, eps, out):
    with ExitStack() as ctx:
        def dram(name, shape, dt):
            return nc.dram_tensor(name, shape, dt, kind="Internal").ap()

        def sb(name, shape, dt=F32):
            return ctx.enter_context(nc.sbuf_tensor(name, shape, dt))

        def sem(name):
            return ctx.enter_context(nc.semaphore(name))

        kv_tab = dram("kv_tab", (NPAD, 2 * D), F32)
        y_tab = dram("y_tab", (2 * NPAD, D), F32)
        d0 = dram("d0", (E + CH + 1,), F32)
        pen0 = dram("pen0", (E + CH + 1,), F32)
        i0 = dram("i0", (E + CH,), I32)
        d1 = dram("d1", (END1 + CH,), F32)
        i1 = dram("i1", (END1 + CH,), I32)
        ea1 = dram("ea1", (END1 + CH, EA), F32)
        tabs = [dram(f"tab{l}", (TE, 4), I32) for l in range(2)]
        negs = [dram(f"neg{l}", (TE,), F32) for l in range(2)]
        keeps = dram("keeps", (TE,), F32)
        dm0 = dram("dm0", (E + CH,), F32)

        xs = sb("xs", [P, TILES * D])
        ident = sb("ident", [P, P])
        minus_low = sb("minus_low", [CP + H, H])
        minus = sb("minus", [CP + H, H])
        iota_row = sb("iota_row", [P, P])
        iota_col = sb("iota_col", [P, 1])
        ones = sb("ones", [P, P])
        wqkv = sb("wqkv", [P, 3 * D])
        w0_sb = sb("w0_sb", [P, D])
        fc1_sb = sb("fc1_sb", [P, FF])
        fc2_sb = sb("fc2_sb", [P, FC, D])
        fc1b_sb = sb("fc1b_sb", [P, FC])
        rows = sb("rows", [P, 5, D])
        w1x = sb("w1x", [P, 2 * D])
        w1blk = sb("w1blk", [G * EA + 1, 2 * CH])
        w1r = sb("w1r", [EA, 2 * D])
        reql = sb("reql", [EA, G * EA + 1])
        b1row = sb("b1row", [1, 2 * D])
        w2wu = sb("w2wu", [P, 4 * D])
        w2u = sb("w2u", [P, 3 * D])
        b2col = sb("b2col", [P, 3])
        burow = sb("burow", [1, D])
        dbu = sb("dbu", [3, D])
        sel3 = sb("sel3", [1, 3])
        epsc = sb("epsc", [P, 1])
        eps_ln = sb("eps_ln", [P, 1])
        blockones = sb("blockones", [P, H])
        tab_sb = [sb(f"tab_sb{l}", [1, 4 * TE], I32) for l in range(2)]
        iters_sb = sb("iters_sb", [1, 4], I32)
        nj = [sb(f"nj{l}", [P, TE]) for l in range(2)]
        keep = sb("keep", [P, TE])

        mark = sb("mark", [P, 4])
        reql_one = sb("reql_one", [1, G * EA + 1])

        ARENA = 38200
        arena = sb("arena", [P, ARENA])
        top = [0]

        def carve(n, start=None):
            if start is not None:
                top[0] = start
            a = arena[:, top[0]:top[0] + n]
            top[0] += n
            assert top[0] <= ARENA, top[0]
            return a

        PENW = CH + 8
        acc0 = carve((TILES + 1) * RW, 0)
        qsp = carve(TILES * 3 * D // 2).bitcast(BF16)
        zero0 = top[0]
        contrib = carve(2 * (H + G * RW))
        prod = carve(2 * CH)
        kts = carve(2 * CH)
        stk = carve(2 * CH)
        fmx = carve(2 * CH)
        cur = carve(2 * RW)
        ucar = carve(2)
        pen = carve(3 * PENW)
        s_hot = carve(U * CH)
        kvw = G * 2 * D
        kv = carve(U * kvw)
        zero1 = top[0]
        st = carve(U * CH // 2).bitcast(BF16)
        drow = carve(3 * CH)
        dcol = carve(U * G)
        idx = carve(U * G).bitcast(I32)
        dcr = carve(G)
        rsc = carve(H)
        atmp = carve(RW)
        xT = carve(GRP * P, zero1 - U * kvw)
        kvst = carve(2 * GRP * 2 * D)
        qres = carve(GRP * D)
        xcp = carve(GRP * D)
        assert top[0] <= zero1 + U * CH // 2
        srci = carve(2 * EQ, 0).bitcast(I32)
        srcb = carve(EQ).bitcast(I32)
        dsti = carve(2 * EQ).bitcast(I32)
        dstf = carve(2 * EQ)
        dprev = carve(2 * EQ)
        cmpj = dsti.bitcast(F32)
        dstm = carve(2 * EQ)
        fill = carve(2 * CH)
        filli = carve(CH).bitcast(I32)
        assert top[0] <= TILES * RW
        carve(0, zero1 + U * CH // 2 + 3 * CH + 2 * U * G + G + H + RW)
        cnt = carve(VT)
        kcol = carve(TC)
        iota_u = carve(64)
        thr = carve(TILES)
        seg = carve(VT)
        nch = carve(VT)
        nchi = carve(VT).bitcast(I32)
        cum = carve(VT)
        spos = carve(VT)
        hotv = carve(VT)
        col = carve(8 * TC)
        tbe = carve(16 * 2 + 12)
        av = carve(GRP * D, (TILES + 1) * RW)
        rden = carve(GRP * H)
        nT = carve(GRP * P)
        res = carve(GRP * D)
        h1 = carve(GRP * D)
        h1c = carve(GRP * D)
        ffT = carve(FC * GRP * P)
        stats = carve(GRP * 6)
        mv = carve(GRP * 2)
        sd = carve(GRP)
        rs = carve(GRP)
        yst = carve(GRP * 2 * D)
        acc1 = carve((VT + 1) * LW, 0)
        late = max(top[0], (TILES + 1) * RW + 17000)
        con1 = carve(3 * G * LW, late)
        eaT = carve(2 * P)
        deg3 = carve(GRP * 3)
        yg = carve(U * G * D)
        s1 = carve(U * CH)
        hid = carve(2 * CH)
        eat = carve(U * P)
        dcol1 = carve(U * G)
        idx1 = carve(U * G).bitcast(I32)
        late_end = top[0]
        aT = carve(GRP * P * 3, late_end - (U * G * D + U * CH + 2 * CH + U * P + 2 * U * G))
        degT = carve(GRP * P)
        fin = carve(GRP * D)
        fstats = carve(GRP * 6)
        fmv = carve(GRP * 2)
        fsd = carve(GRP)
        frs = carve(GRP)
        fout = carve(GRP * D)
        fx = carve(3 * GRP * D)

        ps = ctx.enter_context(nc.psum_tensor("ps", [P, 8 * 512], F32))

        def bank(b, n=1):
            return ps[:, b * 512:(b + n) * 512]

        s_zero = sem("s_zero"); s_const = sem("s_const"); s_pool = sem("s_pool")
        s_w = sem("s_w"); s_w2 = sem("s_w2"); s_blk = sem("s_blk"); s_x = sem("s_x"); s_dst = sem("s_dst")
        s_wmm = sem("s_wmm"); s_wcp = sem("s_wcp")
        s_xTp = sem("s_xTp"); s_xT = sem("s_xT"); s_q = sem("s_q"); s_kv = sem("s_kv")
        s_qs = sem("s_qs"); s_kvst = sem("s_kvst"); s_kvo = sem("s_kvo"); s_kvfree = sem("s_kvfree"); s_kz = sem("s_kz")
        s_pre = sem("s_pre"); s_dst_out = sem("s_dst_out"); s_prev = sem("s_prev"); s_pen = sem("s_pen")
        s_cnt = sem("s_cnt"); s_seg = sem("s_seg"); s_tab = sem("s_tab"); s_tabo = sem("s_tabo")
        s_tabi = sem("s_tabi"); s_arr = sem("s_arr"); s_ea = sem("s_ea"); s_eac = sem("s_eac"); s_dv = sem("s_dv")
        s_init = sem("s_init"); s_bank = sem("s_bank"); s_pj = sem("s_pj"); s_xcp = sem("s_xcp"); s_wu = sem("s_wu"); s_mark = sem("s_mark")
        l_ld = [sem(f"l_ld{k}") for k in range(U)]
        l_ix = [sem(f"l_ix{k}") for k in range(U)]
        l_g = [sem(f"l_g{k}") for k in range(U)]
        l_hot = sem("l_hot"); l_kq = sem("l_kq"); l_kt = sem("l_kt"); l_kc = sem("l_kc"); l_prod = sem("l_prod"); l_s = sem("l_s")
        l_scr = sem("l_scr"); l_f = sem("l_f"); l_c = sem("l_c"); l_d = sem("l_d"); l_e = sem("l_e")
        l_pv = sem("l_pv"); l_agg = sem("l_agg"); l_acc = sem("l_acc"); l_over = sem("l_over"); l_dcr = sem("l_dcr"); l_rsc = sem("l_rsc"); l_at = sem("l_at"); m_over = sem("m_over")
        n_a = sem("n_a"); n_aTp = sem("n_aTp"); n_aT = sem("n_aT"); n_emb = sem("n_emb")
        n_var = sem("n_var"); n_sd = sem("n_sd"); n_h1 = sem("n_h1"); n_hTp = sem("n_hTp")
        n_hT = sem("n_hT"); n_f1 = sem("n_f1"); n_f1s = sem("n_f1s"); n_f2 = sem("n_f2")
        n_h1c = sem("n_h1c"); n_x1 = sem("n_x1"); n_x1c = sem("n_x1c"); n_xTp = sem("n_xTp"); n_xT = sem("n_xT")
        n_y = sem("n_y"); n_ys = sem("n_ys"); n_yo = sem("n_yo"); n_yfree = sem("n_yfree")
        m_zero = sem("m_zero"); m_pool = sem("m_pool")
        m_ld = [sem(f"m_ld{k}") for k in range(U)]
        m_ix = [sem(f"m_ix{k}") for k in range(U)]
        m_g = [sem(f"m_g{k}") for k in range(U)]
        m_hot = sem("m_hot"); m_eTp = sem("m_eTp"); m_eT = sem("m_eT"); m_u = sem("m_u")
        m_hid = sem("m_hid"); m_con = sem("m_con"); m_agg = sem("m_agg"); m_acc = sem("m_acc")
        f_deg = sem("f_deg"); f_tp = sem("f_tp"); f_t = sem("f_t"); f_o = sem("f_o"); f_r = sem("f_r"); f_b = sem("f_b"); f_x = sem("f_x")
        f_var = sem("f_var"); f_sd = sem("f_sd"); f_out = sem("f_out"); f_dma = sem("f_dma"); f_free = sem("f_free")

        block = ctx.enter_context(nc.Block())
        dst_halves = dst.rearrange("(h p c) -> p h c", h=2, c=EQ)
        src_halves = src.rearrange("(h p c) -> p h c", h=2, c=EQ)
        v3 = lambda a, b: a.rearrange("p (b c) -> p b c", b=b)

        def bases(eng, *pairs):
            for s_, lag in pairs:
                eng.sem_inc(s_, BASE - lag)

        def counter(eng, name, start):
            c = eng.alloc_register(name)
            eng.reg_mov(c, start)
            return c

        def linker(eng, s_):
            made = eng.alloc_register("made")
            eng.reg_mov(made, 0)

            def link(ins, apart=False):
                ins.then_inc(s_, 1)
                eng.reg_add(made, made, 1)
                if apart:
                    eng.wait_ge(s_, 1)
                eng.wait_ge(s_, made)
            return link

        @block.sync
        def _(sp):
            for k, w in enumerate((wq, wk, wv)):
                sp.dma_start(wqkv[:, k * D:(k + 1) * D], w).then_inc(s_w, 16)
            sp.wait_ge(s_zero, 1)
            sp.dma_start(v3(xs[:, :], TILES)[:, 0:TILES - 1, :],
                         x[0:(TILES - 1) * P, :].rearrange("(t p) d -> p t d", p=P)).then_inc(s_x, 16)
            sp.dma_start(xs[0:LAST, (TILES - 1) * D:], x[(TILES - 1) * P:N, :]).then_inc(s_x, 16)
            sp.dma_start(v3(dsti, 2)[0:EP], dst_halves).then_inc(s_dst, 16)
            sp.dma_start(v3(srci, 2)[0:EP], src_halves).then_inc(s_dst, 16)
            sp.wait_ge(s_pool, 4)
            one = lambda a: a.rearrange("(a n) -> a n", a=1)
            sp.dma_start(one(d0[0:1]), fill[0:1, 0:1]).then_inc(s_arr, 16)
            sp.dma_start(one(d0[E + 1:E + 1 + CH]), fill[0:1, 0:CH]).then_inc(s_arr, 16)
            sp.dma_start(one(pen0[E:E + CH + 1]), fill[1:2, 0:CH + 1]).then_inc(s_arr, 16)
            sp.dma_start(one(i0[E:E + CH]), filli[0:1, 0:CH]).then_inc(s_arr, 16)
            sp.dma_start(one(dm0[E:E + CH]), fill[0:1, 0:CH]).then_inc(s_arr, 16)
            gap = BASE1 - HALF
            sp.dma_start(one(d1[HALF:BASE1]), fill[0:1, 0:gap]).then_inc(s_ea, 16)
            sp.dma_start(one(d1[END1:END1 + CH]), fill[0:1, 0:CH]).then_inc(s_ea, 16)
            sp.dma_start(one(i1[HALF:BASE1]), fill[2:3, 0:gap].bitcast(I32)).then_inc(s_ea, 16)
            sp.dma_start(one(i1[END1:END1 + CH]), filli[0:1, 0:CH]).then_inc(s_ea, 16)
            sp.dma_start(ea1[HALF:BASE1, :].rearrange("(p a) f -> p (a f)", p=16),
                         fill[4:20, 0:gap * EA // 16]).then_inc(s_ea, 16)
            sp.dma_start(ea1[END1:END1 + CH, :].rearrange("(p a) f -> p (a f)", p=16),
                         fill[4:20, 0:CH * EA // 16]).then_inc(s_ea, 16)
            sp.wait_ge(s_pre, 3)
            sp.dma_start(d0[1:1 + E].rearrange("(h p c) -> p h c", h=2, c=EQ), v3(dstf, 2)[0:EP]).then_inc(s_dst_out, 16)
            sp.dma_start(i0[0:E].rearrange("(h p c) -> p h c", h=2, c=EQ), v3(srci, 2)[0:EP]).then_inc(s_arr, 16)
            sp.dma_start(dm0[0:E].rearrange("(h p c) -> p h c", h=2, c=EQ), v3(dstm, 2)[0:EP]).then_inc(s_arr, 16)
            for h, b in ((0, 0), (1, BASE1)):
                sp.dma_start(d1[b:b + HALF].rearrange("(p c) -> p c", c=EQ), v3(dstf, 2)[0:EP, h, :]).then_inc(s_ea, 16)
            sp.wait_ge(s_arr, 16 * 7)
            sp.wait_ge(s_dst_out, 16)
            sp.dma_start(v3(dprev, 2)[0:EP], d0[0:E].rearrange("(h p c) -> p h c", h=2, c=EQ)).then_inc(s_prev, 16)
            sp.wait_ge(s_pen, 2)
            sp.dma_start(pen0[0:E].rearrange("(h p c) -> p h c", h=2, c=EQ), v3(dprev, 2)[0:EP]).then_inc(s_arr, 16)
            for h, b in ((0, 0), (1, BASE1)):
                sp.dma_start(i1[b:b + HALF].rearrange("(p c) -> p c", c=EQ), (v3(srci, 2)[0:EP, 0, :], srcb[0:EP])[h]).then_inc(s_ea, 16)
            sp.sem_inc(s_kvfree, 2)
            with sp.Fori(0, GROUPS) as i:
                sp.wait_ge(s_kvst, i + 2)
                sp.dma_start(kv_tab[ds(i * (GRP * P), GRP * P), :].rearrange("(t p) d -> p t d", p=P),
                             v3(kvst[:, ds((i % 2) * (GRP * 2 * D), GRP * 2 * D)], GRP)).then_inc(s_kvo, 16)
                sp.wait_ge(s_kvo, 16 * i + 16)
                sp.sem_inc(s_kvfree, 1)
            sp.wait_ge(s_tab, 1)
            for l in range(2):
                sp.dma_start(tabs[l].rearrange("(p c) f -> p c f", p=TR),
                             tbe[0:TR, 16 * l:16 * l + 12].bitcast(I32).rearrange("p (c f) -> p c f", c=TC)).then_inc(s_tabo, 16)
                sp.dma_start(negs[l].rearrange("(p c) -> p c", p=TR), tbe[0:TR, 32 + 4 * l:32 + 4 * l + TC]).then_inc(s_tabo, 16)
            sp.dma_start(keeps.rearrange("(p c) -> p c", p=TR), tbe[0:TR, 40:40 + TC]).then_inc(s_tabo, 16)
            sp.wait_ge(s_tabo, 80)
            sp.dma_start(keep[:, :], keeps.rearrange("(a e) -> a e", a=1).to_broadcast([P, TE])).then_inc(s_tabi, 16)
            for l in range(2):
                sp.dma_start(tab_sb[l][:, :], tabs[l].rearrange("(a e) f -> a (e f)", a=1)).then_inc(s_tabi, 16)
                sp.dma_start(nj[l][:, :], negs[l].rearrange("(a e) -> a e", a=1).to_broadcast([P, TE])).then_inc(s_tabi, 16)
            for h, b in ((0, 0), (1, BASE1)):
                sp.dma_start(ea1[b:b + HALF, :].rearrange("(p c) f -> p (c f)", p=EP),
                             ea[h * HALF:(h + 1) * HALF, :].rearrange("(p c) f -> p (c f)", p=EP)).then_inc(s_eac, 16)

            sp.wait_ge(s_tabi, 80)
            sp.wait_ge(s_arr, 16 * 8)
            sp.wait_ge(s_init, 3)
            n0 = sp.value_load(iters_sb[0:1, 0:1], min_val=1, max_val=ITERS)
            used = counter(sp, "used", BASE - 2)
            with sp.Fori(0, n0) as i:
                for u in range(U):
                    off = sp.value_load(tab_sb[0][0:1, ds(4 * (i * U + (u + LAG)), 1)], min_val=0, max_val=E)
                    off2 = sp.value_load(tab_sb[0][0:1, ds(4 * (i * U + (u + LAG - 2)), 1)], min_val=0, max_val=E)
                    sp.wait_ge(s_init, 3)
                    sp.wait_ge(l_pv, used)
                    sp.dma_start(v3(idx, U)[:, u, :], i0[ds(off, CH)].rearrange("(p g) -> p g", g=G)).then_inc(l_ix[u], 16)
                    sp.dma_start(v3(dcol, U)[:, u, :], d0[ds(off + 1, CH)].rearrange("(p g) -> p g", g=G)).then_inc(l_ld[u], 16)
                    sp.dma_start(v3(drow, 3)[:, u % 3, :],
                                 dm0[ds(off, CH)].rearrange("(a n) -> a n", a=1).to_broadcast([P, CH])).then_inc(l_ld[u], 16)
                    sp.dma_start(v3(pen, 3)[0:H, (u - 2) % 3, 0:CH],
                                 pen0[ds(off2, CH)].rearrange("(a n) -> a n", a=1).to_broadcast([H, CH])).then_inc(l_ld[u], 16)
                    sp.reg_add(used, used, 1)

            sp.sem_inc(n_yfree, 1)
            with sp.Fori(0, GROUPS) as i:
                sp.wait_ge(n_ys, i + 2)
                for h in range(2):
                    sp.dma_start(y_tab[ds(h * NPAD + i * (GRP * P), GRP * P), :].rearrange("(t p) d -> p t d", p=P),
                                 v3(yst, GRP)[:, :, h * D:(h + 1) * D]).then_inc(n_yo, 16)
                sp.wait_ge(n_yo, 32 * i + 32)
                sp.sem_inc(n_yfree, 1)

            sp.wait_ge(m_pool, 5)
            sp.wait_ge(s_ea, 16 * 10)
            sp.wait_ge(s_eac, 32)
            n1 = sp.value_load(iters_sb[0:1, 1:2], min_val=1, max_val=ITERS)
            free6 = counter(sp, "free6", BASE - U + 1)
            with sp.Fori(0, n1) as i:
                for u in range(U):
                    off = sp.value_load(tab_sb[1][0:1, ds(4 * (i * U + (u + LAG)), 1)], min_val=0, max_val=END1)
                    sp.wait_ge(m_pool, 5)
                    sp.wait_ge(m_hid, free6)
                    sp.dma_start(v3(idx1, U)[:, u, :], i1[ds(off, CH)].rearrange("(p g) -> p g", g=G)).then_inc(m_ix[u], 16)
                    sp.dma_start(v3(dcol1, U)[:, u, :], d1[ds(off, CH)].rearrange("(p g) -> p g", g=G)).then_inc(m_ld[u], 16)
                    sp.dma_start(v3(eat, U)[:, u, 0:G * EA], ea1[ds(off, CH), :].rearrange("(p g) f -> p (g f)", g=G)).then_inc(m_ld[u], 16)
                    sp.reg_add(free6, free6, 1)

            sp.sem_inc(f_free, 1)
            with sp.Fori(0, GROUPS - 1) as i:
                sp.wait_ge(f_out, i + 1)
                sp.dma_start(out[ds(i * (GRP * P), GRP * P), :].rearrange("(t p) d -> p t d", p=P),
                             v3(fout, GRP)).then_inc(f_dma, 16)
                sp.wait_ge(f_dma, 16 * i + 16)
                sp.sem_inc(f_free, 1)
            sp.wait_ge(f_out, GROUPS)
            done = (GROUPS - 1) * GRP * P
            sp.dma_start(out[done:done + (GRP - 1) * P, :].rearrange("(t p) d -> p t d", p=P),
                         v3(fout, GRP)[:, 0:GRP - 1, :]).then_inc(f_dma, 16)
            sp.dma_start(out[done + (GRP - 1) * P:N, :], fout[0:LAST, (GRP - 1) * D:]).then_inc(f_dma, 16)
            sp.wait_ge(f_dma, 16 * (GROUPS + 1))
            sp.wait_ge(n_yo, 32 * GROUPS)

        @block.gpsimd
        def _(pool):
            g = nc.gpsimd
            g.memset(xs[:, (TILES - 1) * D:], 0.0).then_inc(s_zero, 1)
            g.memset(ident[:, :], 0.0).then_inc(s_const, 1)
            g.memset(ones[:, :], 1.0).then_inc(s_const, 1)
            pool.wait_ge(s_const, 2)
            g.affine_select(out=ident[:, :], in_=ident[:, :], compare_op=ALU.not_equal, fill=1.0, base=0,
                            pattern=[[-1, P]], channel_multiplier=1).then_inc(s_const, 1)
            g.memset(blockones[:, :], 0.25).then_inc(s_const, 1)
            pool.wait_ge(s_const, 4)
            g.affine_select(out=blockones[:, :], in_=blockones[:, :], compare_op=ALU.is_ge, fill=0.0, base=0,
                            pattern=[[-DH, H]], channel_multiplier=1).then_inc(s_const, 1)
            pool.wait_ge(s_const, 5)
            g.affine_select(out=blockones[:, :], in_=blockones[:, :], compare_op=ALU.is_ge, fill=0.0, base=DH - 1,
                            pattern=[[DH, H]], channel_multiplier=-1).then_inc(s_const, 1)
            g.iota(iota_row[:, :], [[1, P]], base=0, channel_multiplier=0, allow_small_or_imprecise_dtypes=True).then_inc(s_const, 1)
            g.iota(iota_col[:, :], [[0, 1]], base=0, channel_multiplier=1, allow_small_or_imprecise_dtypes=True).then_inc(s_const, 1)
            g.memset(fill, 0.0).then_inc(s_pool, 1)
            pool.wait_ge(s_pool, 1)
            g.affine_select(out=fill, in_=fill, compare_op=ALU.not_equal, fill=-BIG, base=-1,
                            pattern=[[0, 2 * CH]], channel_multiplier=1).then_inc(s_pool, 1)
            g.memset(filli, 0).then_inc(s_pool, 1)
            pool.wait_ge(s_pool, 3)
            g.memset(fill[0:1, :], -1.0).then_inc(s_pool, 1)
            g.iota(kcol[0:TR, :], [[1, TC]], base=-LAG, channel_multiplier=TC, allow_small_or_imprecise_dtypes=True).then_inc(s_pool, 1)
            g.iota(iota_u, [[U, 64]], base=0, channel_multiplier=0, allow_small_or_imprecise_dtypes=True).then_inc(s_pool, 1)
            g.iota(thr, [[P, TILES]], base=0, channel_multiplier=0, allow_small_or_imprecise_dtypes=True).then_inc(s_pool, 1)

            pool.wait_ge(s_x, 32)
            with pool.Fori(0, GROUPS) as i:
                pool.wait_ge(s_q, i + 1)
                g.tensor_copy(xcp, xs[:, ds(i * (GRP * D), GRP * D)]).then_inc(s_xcp, 1)

            g.memset(arena[:, zero0:zero1 - U * kvw], 0.0).then_inc(s_init, 1)
            pool.wait_ge(s_cnt, 1)
            pool.wait_ge(s_pen, 2)
            pool.wait_ge(s_prev, 16)
            pool.wait_ge(s_dst_out, 16)
            pool.wait_ge(s_arr, 16 * 8)
            pool.wait_ge(s_ea, 16 * 10)
            g.memset(acc0, 0.0).then_inc(s_init, 1)
            pool.wait_ge(s_qs, GROUPS + 1)
            pool.wait_ge(s_kvo, 16 * GROUPS)
            g.memset(kv[:, (U - 1) * kvw:], 0.0).then_inc(s_kz, 1)
            g.memset(kv[:, (U - 3) * kvw:(U - 1) * kvw], 0.0).then_inc(s_kz, 1)
            pool.wait_ge(s_kz, 2)
            pool.wait_ge(s_tabi, 80)
            pool.sem_inc(s_init, 1)

            pool.wait_ge(s_init, 3)
            slot_free = counter(pool, "slot_free", BASE - 2)
            landed = counter(pool, "landed", 16)
            n0 = pool.value_load(iters_sb[0:1, 0:1], min_val=1, max_val=ITERS)
            kv_s = kv.rearrange("p (u g d) -> p u g d", u=U, g=G)
            with pool.Fori(0, n0):
                for u in range(U):
                    pool.wait_ge(s_init, 3)
                    pool.wait_ge(l_pv, slot_free)
                    pool.wait_ge(l_ix[u], landed)
                    for t in range(G):
                        g.indirect_dma_start(kv_s[:, u, t, :], None, kv_tab,
                                             bass.IndirectOffsetOnAxis(ap=v3(idx, U)[:, u, t:t + 1], axis=0)).then_inc(l_g[u], 16)
                    pool.reg_add(slot_free, slot_free, 1)
                pool.reg_add(landed, landed, 16)

            pool.wait_ge(l_over, 3)
            g.memset(con1, 1.0).then_inc(m_pool, 1)
            g.memset(eaT, 1.0).then_inc(m_pool, 1)
            g.memset(deg3, 1.0).then_inc(m_pool, 1)
            g.memset(yg, 0.0).then_inc(m_pool, 1)
            g.memset(arena[:, late + 3 * G * LW + 2 * P + GRP * 3 + U * G * D:late_end], 0.0).then_inc(m_pool, 1)

            pool.sem_inc(n_x1c, 1)
            with pool.Fori(0, GROUPS) as i:
                pool.wait_ge(n_h1, i + 1)
                g.tensor_tensor(v3(h1c, GRP), v3(h1, GRP), rows[:, 2:3, :].to_broadcast([P, GRP, D]), ALU.add).then_inc(n_h1c, 1)
                pool.wait_ge(n_x1, i + 1)
                g.tensor_copy(xs[:, ds(i * (GRP * D), GRP * D)], res).then_inc(n_x1c, 1)

            pool.wait_ge(m_pool, 5)
            pool.wait_ge(n_yo, 32 * GROUPS)
            pool.reg_mov(slot_free, BASE - U + 1)
            pool.reg_mov(landed, 16)
            n1 = pool.value_load(iters_sb[0:1, 1:2], min_val=1, max_val=ITERS)
            yg_s = yg.rearrange("p (u g d) -> p u g d", u=U, g=G)
            with pool.Fori(0, n1):
                for u in range(U):
                    pool.wait_ge(m_pool, 5)
                    pool.wait_ge(m_hid, slot_free)
                    pool.wait_ge(m_ix[u], landed)
                    for t in range(G):
                        g.indirect_dma_start(yg_s[:, u, t, :], None, y_tab,
                                             bass.IndirectOffsetOnAxis(ap=v3(idx1, U)[:, u, t:t + 1], axis=0)).then_inc(m_g[u], 16)
                    pool.reg_add(slot_free, slot_free, 1)
                pool.reg_add(landed, landed, 16)

            pool.wait_ge(m_over, 3)
            with pool.Fori(0, GROUPS) as i:
                pool.wait_ge(f_deg, i + 1)
                g.tensor_copy(fx[:, 2 * GRP * D:], xs[:, ds(i * (GRP * D), GRP * D)]).then_inc(f_x, 1)

        @block.scalar
        def _(act):
            a = nc.scalar
            row = lambda t: t.rearrange("(a n) -> a n", a=1)
            act.dma_start(w0_sb[:, :], w0).then_inc(s_w2, 16)
            act.dma_start(fc1_sb[:, :], fc1w).then_inc(s_w2, 16)
            act.dma_start(fc2_sb[:, :, :], fc2w.rearrange("(c p) d -> p c d", p=P)).then_inc(s_w2, 16)
            act.dma_start(fc1b_sb[:, :], fc1b.rearrange("(c p) -> p c", p=P), allow_slow_non_contiguous=True).then_inc(s_w2, 16)
            for k, t in enumerate((ln1g, ln1b, fc2b, ln2g, ln2b)):
                act.dma_start(rows[:, k, :], row(t).to_broadcast([P, D])).then_inc(s_w2, 16)
            for k, (w, b) in enumerate(((w1f, b1f), (w1b, b1b))):
                act.dma_start(w1x[:, k * D:(k + 1) * D], w[0:D, :]).then_inc(s_w2, 16)
                act.dma_start(w1r[:, k * D:(k + 1) * D], w[D + EA:D + 2 * EA, :]).then_inc(s_w2, 16)
                act.dma_start(b1row[:, k * D:(k + 1) * D], row(b)).then_inc(s_w2, 16)
            for k, w in enumerate((w2f, w2b, wu)):
                act.dma_start(w2wu[:, k * D:(k + 1) * D], w).then_inc(s_w2, 16)
            act.dma_start(burow[:, :], row(bu)).then_inc(s_w2, 16)
            act.dma_start(epsc[:, :], row(eps).to_broadcast([P, 1])).then_inc(s_w2, 16)
            act.wait_ge(s_blk, 3)
            for k, w in enumerate((w1f, w1b)):
                for t in range(G):
                    act.dma_start(w1blk[t * EA:(t + 1) * EA, k * CH + t * D:k * CH + (t + 1) * D],
                                  w[D:D + EA, :]).then_inc(s_w2, 16)
            act.dma_start(reql[:, G * EA:G * EA + 1], req.rearrange("a f -> f a"), allow_slow_non_contiguous=True).then_inc(s_w2, 16)
            act.dma_start(b2col[:, 0:1], b2f.rearrange("(p a) -> p a", a=1)).then_inc(s_w2, 16)
            act.dma_start(b2col[:, 1:2], b2b.rearrange("(p a) -> p a", a=1)).then_inc(s_w2, 16)

            act.sem_inc(s_kvst, 1)
            with act.Fori(0, GROUPS) as i:
                act.wait_ge(s_xTp, i + 1)
                a.activation(xT, bank(2, 2)[:, 0:GRP * P], ACT.Copy).then_inc(s_xT, 1)
                act.wait_ge(s_kv, i + 1)
                act.wait_ge(s_kvfree, i + 1)
                a.activation(kvst[:, ds((i % 2) * (GRP * 2 * D), GRP * 2 * D)], bank(4, 4)[:, 0:GRP * 2 * D], ACT.Copy).then_inc(s_kvst, 1)

            act.wait_ge(s_wmm, 1)
            a.activation(w2u[:, 0:2 * D], bank(0)[:, 0:2 * D], ACT.Copy).then_inc(s_wcp, 1)
            act.wait_ge(s_wmm, 2)
            a.activation(w1blk[G * EA:G * EA + 1, :].rearrange("p (k g d) -> p k g d", k=2, g=G),
                         bank(1)[G * EA:G * EA + 1, 0:2 * D].rearrange("p (k d) -> p k d", k=2)[:, :, None, :].to_broadcast([1, 2, G, D]),
                         ACT.Copy).then_inc(s_wcp, 1)
            act.wait_ge(s_wmm, 3)
            a.activation(w2u[:, 0:2 * D], bank(2)[:, 0:2 * D], ACT.Copy).then_inc(s_wcp, 1)
            a.activation(dbu[:, :], bank(3)[0:3, 0:D], ACT.Copy).then_inc(s_wcp, 1)

            act.wait_ge(s_init, 3)
            n0 = act.value_load(iters_sb[0:1, 0:1], min_val=1, max_val=ITERS)
            for s_, below in ((l_kc, 0), (l_scr, 0), (l_e, 0), (l_dcr, 1), (l_rsc, 1)):
                act.sem_inc(s_, BASE - below)
            last_ = counter(act, "act_last", BASE)
            now = counter(act, "act_now", BASE + 1)
            landed_ = counter(act, "act_landed", 48)
            con_s = v3(contrib, 2)
            with act.Fori(0, n0) as i:
                for u in range(U):
                    into = act.value_load(tab_sb[0][0:1, ds(4 * (i * U + u) + 2, 1)], min_val=0, max_val=TILES * RW)
                    act.wait_ge(l_ld[u], landed_)
                    a.activation(dcr, v3(dcol, U)[:, u, :], ACT.Identity, bias=nj[0][:, ds(i * U + (u + LAG), 1)]).then_inc(l_dcr, 1)
                    act.wait_ge(l_kt, now)
                    act.wait_ge(l_prod, last_)
                    a.activation(v3(kts, 2)[:, u % 2, :], bank(2 + u % 2), ACT.Copy).then_inc(l_kc, 1)
                    act.wait_ge(l_agg, last_)
                    kp = keep[:, ds(i * U + u, 1)]
                    a.activation(rsc, bank(6 + (u - 4) % 2)[:, 0:H], ACT.Identity, scale=kp, bias=kp).then_inc(l_rsc, 1)
                    act.wait_ge(l_s, now)
                    a.activation(v3(stk, 2)[0:H, (u - 1) % 2, :], bank(4)[0:H, :], ACT.Copy).then_inc(l_scr, 1)
                    act.wait_ge(l_d, now)
                    dps = bank(5)[:, 0:40]
                    c = con_s[:, (u - 2) % 2, :]
                    a.activation(c[:, H:].rearrange("p (g h w) -> p g h w", g=G, h=H)[:, :, :, DH],
                                 dps[:, 0:G * H].rearrange("p (g h) -> p g h", g=G), ACT.Exp)
                    a.activation(c[0:1, 0:H], dps[0:1, G * H:G * H + H], ACT.Exp).then_inc(l_e, 1)
                    act.wait_ge(l_acc, now)
                    a.activation(acc0[:, ds(into, RW)], v3(cur, 2)[:, u % 2, :], ACT.Copy)
                    act.reg_add(last_, last_, 1)
                    act.reg_add(now, now, 1)
                act.reg_add(landed_, landed_, 48)

            a.activation(mark[:, 2:3], eps_ln[:, :], ACT.Copy).then_inc(l_over, 1)
            act.wait_ge(l_over, 3)

            act.sem_inc(n_ys, 1)
            with act.Fori(0, GROUPS) as i:
                act.wait_ge(n_aTp, i + 1)
                a.activation(nT, bank(0, 2)[:, 0:GRP * P], ACT.Copy).then_inc(n_aT, 1)
                act.wait_ge(n_var, 3 * i + 1)
                a.activation(sd, v3(mv, GRP)[:, :, 1], ACT.Sqrt, bias=eps_ln[:, :]).then_inc(n_sd, 1)
                act.wait_ge(n_hTp, i + 1)
                a.activation(nT, bank(0, 2)[:, 0:GRP * P], ACT.Copy).then_inc(n_hT, 1)
                for c in range(FC):
                    act.wait_ge(n_f1, FC * i + (c + 1))
                    a.activation(v3(ffT, FC)[:, c, :], bank(4 + 2 * (c % 2), 2)[:, 0:GRP * P], ACT.Relu,
                                 bias=fc1b_sb[:, c:c + 1]).then_inc(n_f1s, 1)
                for k in (2, 3):
                    act.wait_ge(n_var, 3 * i + k)
                    a.activation(sd, v3(mv, GRP)[:, :, 1], ACT.Sqrt, bias=eps_ln[:, :]).then_inc(n_sd, 1)
                act.wait_ge(n_xTp, i + 1)
                a.activation(nT, bank(0, 2)[:, 0:GRP * P], ACT.Copy).then_inc(n_xT, 1)
                act.wait_ge(n_y, i + 1)
                act.wait_ge(n_yfree, i + 1)
                a.activation(yst, bank(4, 4)[:, 0:GRP * 2 * D], ACT.Copy).then_inc(n_ys, 1)

            act.wait_ge(m_pool, 5)
            bases(act, (m_eT, 0), (m_con, 1))
            n1 = act.value_load(iters_sb[0:1, 1:2], min_val=1, max_val=ITERS)
            hid_s = v3(hid, 2)
            con1_s = con1.rearrange("p (u g w) -> p u g w", u=3, g=G)
            with act.Fori(0, n1) as i:
                for u in range(U):
                    act.wait_ge(m_eTp, i * U + (u + 1 + BASE))
                    a.activation(v3(eaT, 2)[0:G * EA, u % 2, :], bank(4 * (u % 2))[0:G * EA, 0:P], ACT.Copy).then_inc(m_eT, 1)
                    act.wait_ge(m_hid, i * U + (u - 1 + 1 + BASE))
                    act.wait_ge(m_agg, i * U + (u - 4 + 1 + BASE))
                    a.activation(con1_s[:, (u - 1) % 3, :, 0:D], v3(hid_s[:, (u - 1) % 2, :], G), ACT.Relu).then_inc(m_con, 1)

            a.activation(mark[:, 3:4], eps_ln[:, :], ACT.Copy).then_inc(m_over, 1)
            act.wait_ge(m_over, 3)

            act.sem_inc(f_r, 1)
            with act.Fori(0, GROUPS) as i:
                act.wait_ge(f_deg, i + 1)
                a.activation(v3(fx[:, GRP * D:2 * GRP * D], GRP),
                             v3(acc1[:, ds(i * (GRP * LW) + TILES * LW, GRP * LW)], GRP)[:, :, 0:D], ACT.Copy).then_inc(f_b, 1)
                act.wait_ge(f_tp, i + 2)
                a.activation(aT, bank(0, 6)[:, :].rearrange("p (k n) -> p k n", k=3)[:, :, 0:GRP * P], ACT.Copy)
                a.activation(degT[0:3, :], bank(6, 2)[0:3, 0:GRP * P], ACT.Copy).then_inc(f_t, 1)
                act.wait_ge(f_o, i + 1)
                a.activation(fin, bank(0, 2)[:, 0:GRP * D], ACT.Relu).then_inc(f_r, 1)
                act.wait_ge(f_var, i + 1)
                a.activation(fsd, v3(fmv, GRP)[:, :, 1], ACT.Sqrt, bias=eps_ln[:, :]).then_inc(f_sd, 1)

        @block.tensor
        def _(pe):
            mm = nc.tensor.matmul
            tp = nc.tensor.transpose
            pe.wait_ge(s_const, 8)
            pe.wait_ge(s_bank, 1)
            pe.wait_ge(s_w, 48)
            pe.sem_inc(s_q, 1)
            with pe.Fori(0, GROUPS) as i:
                pe.wait_ge(s_xcp, i + 1)
                for t in range(GRP):
                    last = tp(bank(2, 2)[:, t * P:(t + 1) * P], xcp[:, t * D:(t + 1) * D], ident[:, :])
                last.then_inc(s_xTp, 1)
                pe.wait_ge(s_xT, i + 1)
                pe.wait_ge(s_qs, i + 1)
                for t in range(GRP):
                    last = mm(bank(0, 2)[:, t * D:(t + 1) * D], xT[:, t * P:(t + 1) * P], wqkv[:, 0:D])
                last.then_inc(s_q, 1)
                pe.wait_ge(s_kvst, i + 1)
                for t in range(GRP):
                    last = mm(bank(4, 4)[:, t * 2 * D:(t + 1) * 2 * D], xT[:, t * P:(t + 1) * P], wqkv[:, D:3 * D])
                last.then_inc(s_kv, 1)

            pe.wait_ge(s_cnt, 1)
            pe.wait_ge(s_kvst, GROUPS + 1)
            mm(bank(7)[:, 0:VT], ones[0:EP, :], cnt[0:EP, 0:VT]).then_inc(s_seg, 1)
            pe.wait_ge(s_w2, 16 * (9 + 6 + 5 + 8 + 3))
            pe.wait_ge(s_blk, 7)
            pe.wait_ge(s_qs, GROUPS + 1)
            for k in range(2):
                last = tp(bank(0)[:, k * D:(k + 1) * D], w2wu[:, k * D:(k + 1) * D], ident[:, :])
            last.then_inc(s_wmm, 1)
            for k in range(2):
                mm(bank(1)[0:G * EA + 1, k * D:(k + 1) * D], reql[:, :], w1r[:, k * D:(k + 1) * D], start=True, stop=False)
                last = mm(bank(1)[0:G * EA + 1, k * D:(k + 1) * D], reql_one[:, :], b1row[:, k * D:(k + 1) * D], start=False, stop=True)
            last.then_inc(s_wmm, 1)
            pe.wait_ge(s_wcp, 1)
            for k in range(2):
                mm(bank(2)[:, k * D:(k + 1) * D], w2u[:, k * D:(k + 1) * D], w2wu[:, 2 * D:3 * D])
            mm(bank(3)[0:3, 0:D], b2col[:, :], w2wu[:, 2 * D:3 * D], start=True, stop=False)
            mm(bank(3)[0:3, 0:D], sel3[:, :], burow[:, :], start=False, stop=True).then_inc(s_wmm, 1)

            pe.wait_ge(s_init, 3)
            pe.wait_ge(s_wcp, 4)
            n0 = pe.value_load(iters_sb[0:1, 0:1], min_val=1, max_val=ITERS)
            kv_s = kv.rearrange("p (u g d) -> p u g d", u=U, g=G)
            st_s = v3(st, U)
            con_s = v3(contrib, 2)
            for s_ in (l_kt, l_kq, l_s, l_d, l_agg):
                pe.sem_inc(s_, BASE)
            last_ = counter(pe, "pe_last", BASE)
            now = counter(pe, "pe_now", BASE + 1)
            landed_ = counter(pe, "pe_landed", 16 * G)
            with pe.Fori(0, n0) as i:
                for u in range(U):
                    tile = pe.value_load(tab_sb[0][0:1, ds(4 * (i * U + (u + LAG)) + 1, 1)], min_val=0, max_val=(TILES - 1) * 3 * D)
                    pe.wait_ge(l_g[u], landed_)
                    pe.wait_ge(l_kc, last_)
                    for t in range(G):
                        last = tp(bank(2 + u % 2)[:, t * P:(t + 1) * P], kv_s[:, u, t, 0:D], ident[:, :])
                    last.then_inc(l_kt, 1)
                    pe.wait_ge(l_hot, now)
                    pe.wait_ge(l_prod, last_)
                    for k in range(3):
                        last = mm(bank(u % 2), qsp[:, ds(tile + k * D, D)], st_s[:, u, :], start=(k == 0), stop=(k == 2))
                    last.then_inc(l_kq, 1)
                    pe.wait_ge(l_prod, now)
                    pe.wait_ge(l_scr, last_)
                    mm(bank(4)[0:H, :], blockones[:, :], v3(prod, 2)[:, (u - 1) % 2, :]).then_inc(l_s, 1)
                    pe.wait_ge(l_c, now)
                    pe.wait_ge(l_e, last_)
                    dps = bank(5)[:, 0:40]
                    w = (u - 2) % 2
                    both = v3(stk, 2)[0:CP + H, w, :].rearrange("h (p g) -> h g p", g=G)
                    for t in range(G):
                        mm(dps[:, t * H:(t + 1) * H], both[:, t, :], minus[:, :])
                    mm(dps[0:1, G * H:G * H + H], ucar[0:CP + H, w:w + 1], minus[:, :], start=True, stop=False)
                    mm(dps[0:1, G * H:G * H + H], both[:, 0, 0:1], minus_low[:, :], start=False, stop=True).then_inc(l_d, 1)
                    pe.wait_ge(l_pv, now)
                    pe.wait_ge(l_acc, last_)
                    agg = bank(6 + (u - 3) % 2)[:, 0:H + RW]
                    c = con_s[:, (u - 3) % 2, :]
                    hot = s_hot.rearrange("p (u g n) -> p u g n", u=U, g=G)[:, (u - 3) % U]
                    mm(agg, hot[:, 0, :], c[:, 0:H + RW], start=True, stop=False)
                    for t in range(1, G):
                        last = mm(agg[:, H:], hot[:, t, :], c[:, H + t * RW:H + (t + 1) * RW], start=False, stop=(t == G - 1))
                    last.then_inc(l_agg, 1)
                    pe.reg_add(last_, last_, 1)
                    pe.reg_add(now, now, 1)
                pe.reg_add(landed_, landed_, 16 * G)

            mm(bank(1)[0:1, 0:1], ones[:, 0:1], ones[:, 0:1]).then_inc(l_over, 1)
            pe.wait_ge(l_over, 3)

            with pe.Fori(0, GROUPS) as i:
                pe.wait_ge(n_a, i + 1)
                for t in range(GRP):
                    last = tp(bank(0, 2)[:, t * P:(t + 1) * P], av[:, t * D:(t + 1) * D], ident[:, :])
                last.then_inc(n_aTp, 1)
                pe.wait_ge(n_aT, i + 1)
                for t in range(GRP):
                    last = mm(bank(2, 2)[:, t * D:(t + 1) * D], nT[:, t * P:(t + 1) * P], w0_sb[:, :])
                last.then_inc(n_emb, 1)
                pe.wait_ge(n_h1, i + 1)
                for t in range(GRP):
                    last = tp(bank(0, 2)[:, t * P:(t + 1) * P], h1[:, t * D:(t + 1) * D], ident[:, :])
                last.then_inc(n_hTp, 1)
                pe.wait_ge(n_hT, i + 1)
                pe.wait_ge(n_ys, i + 1)
                for c in range(FC):
                    if c >= 2:
                        pe.wait_ge(n_f1s, FC * i + (c - 1))
                    for a0, a1 in ((0, 512), (512, GRP * P)):
                        last = mm(bank(4 + 2 * (c % 2), 2)[:, a0:a1], fc1_sb[:, c * P:(c + 1) * P], nT[:, a0:a1])
                    last.then_inc(n_f1, 1)
                pe.wait_ge(n_f1s, FC * i + FC)
                for t in range(GRP):
                    for c in range(FC):
                        last = mm(bank(2, 2)[:, t * D:(t + 1) * D], v3(ffT, FC)[:, c, t * P:(t + 1) * P], fc2_sb[:, c, :],
                                  start=(c == 0), stop=(c == FC - 1))
                last.then_inc(n_f2, 1)
                pe.wait_ge(n_x1, i + 1)
                for t in range(GRP):
                    last = tp(bank(0, 2)[:, t * P:(t + 1) * P], res[:, t * D:(t + 1) * D], ident[:, :])
                last.then_inc(n_xTp, 1)
                pe.wait_ge(n_xT, i + 1)
                for t in range(GRP):
                    last = mm(bank(4, 4)[:, t * 2 * D:(t + 1) * 2 * D], nT[:, t * P:(t + 1) * P], w1x[:, :])
                last.then_inc(n_y, 1)

            pe.wait_ge(m_pool, 5)
            pe.wait_ge(n_ys, GROUPS + 1)
            bases(pe, (m_eTp, 0), (m_u, 1), (m_agg, 2))
            n1 = pe.value_load(iters_sb[0:1, 1:2], min_val=1, max_val=ITERS)
            con1_s = con1.rearrange("p (u g w) -> p u g w", u=3, g=G)
            hot1 = s1.rearrange("p (u g n) -> p u g n", u=U, g=G)
            with pe.Fori(0, n1) as i:
                for u in range(U):
                    way = pe.value_load(tab_sb[1][0:1, ds(4 * (i * U + (u + LAG - 1)) + 3, 1)], min_val=0, max_val=CH)
                    pe.wait_ge(m_ld[u], (i + 1) * 32)
                    pe.wait_ge(m_g[u], (i + 1) * (16 * G))
                    pe.wait_ge(m_eT, i * U + (u - 2 + 1 + BASE))
                    tp(bank(4 * (u % 2))[:, 0:P], v3(eat, U)[:, u, :], ident[:, :]).then_inc(m_eTp, 1)
                    pe.wait_ge(m_eT, i * U + (u - 1 + 1 + BASE))
                    pe.wait_ge(m_hid, i * U + (u - 3 + 1 + BASE))
                    mm(bank(1 + (u - 1) % 2), v3(eaT, 2)[0:G * EA + 1, (u - 1) % 2, :], w1blk[:, ds(way, CH)]).then_inc(m_u, 1)
                    pe.wait_ge(m_con, i * U + (u - 2 + 1 + BASE))
                    pe.wait_ge(m_acc, i * U + (u - 4 + 1 + BASE))
                    agg = bank(3 + 2 * ((u - 2) % 2))[:, 0:LW]
                    for t in range(G):
                        last = mm(agg, hot1[:, (u - 2) % U, t, :], con1_s[:, (u - 2) % 3, t, :], start=(t == 0), stop=(t == G - 1))
                    last.then_inc(m_agg, 1)

            mm(bank(7)[0:1, 0:1], ones[:, 0:1], ones[:, 0:1]).then_inc(m_over, 1)
            pe.wait_ge(m_over, 3)

            pe.sem_inc(f_tp, 1)
            with pe.Fori(0, GROUPS) as i:
                pe.wait_ge(f_deg, i + 1)
                pe.wait_ge(f_b, i + 1)
                pe.wait_ge(f_x, i + 1)
                pe.wait_ge(f_r, i + 1)
                for t in range(GRP):
                    for k in range(3):
                        tp(bank(2 * k, 2)[:, t * P:(t + 1) * P], fx[:, (k * GRP + t) * D:(k * GRP + t + 1) * D], ident[:, :])
                    last = mm(bank(6, 2)[0:3, t * P:(t + 1) * P], v3(deg3, GRP)[:, t, :], ident[:, :])
                last.then_inc(f_tp, 1)
                pe.wait_ge(f_t, i + 1)
                for t in range(GRP):
                    for k in range(3):
                        mm(bank(0, 2)[:, t * D:(t + 1) * D], aT[:, (k * GRP + t) * P:(k * GRP + t + 1) * P], w2u[:, k * D:(k + 1) * D],
                           start=(k == 0), stop=False)
                    last = mm(bank(0, 2)[:, t * D:(t + 1) * D], degT[0:3, t * P:(t + 1) * P], dbu[:, :], start=False, stop=True)
                last.then_inc(f_o, 1)

        @block.vector
        def _(dve):
            v = nc.vector
            tt, ts = v.tensor_tensor, v.tensor_scalar
            link = linker(dve, s_dv)

            v.memset(ps[:, :], 0.0).then_inc(s_bank, 1)
            v.memset(w1blk[:, :], 0.0).then_inc(s_blk, 1)
            v.memset(reql[:, :], 0.0).then_inc(s_blk, 1)
            v.memset(b2col[:, :], 0.0).then_inc(s_blk, 1)
            v.memset(reql_one[:, :], 0.0)
            link(v.memset(sel3[:, :], 0.0))
            v.memset(reql_one[:, G * EA:], 1.0).then_inc(s_blk, 1)
            v.memset(sel3[:, 2:3], 1.0).then_inc(s_blk, 1)
            v.memset(eps_ln[:, :], EPS).then_inc(s_blk, 1)
            dve.wait_ge(s_const, 8)
            v.memset(minus_low[:, :], 0.0)
            link(v.memset(minus[:, :], 0.0))
            ts(minus_low[CP:CP + H, :], ident[0:H, 0:H], -1.0, None, ALU.mult)
            v.tensor_copy(minus[0:H, :], ident[0:H, 0:H])
            ts(minus[CP:CP + H, :], ident[0:H, 0:H], -1.0, None, ALU.mult).then_inc(s_blk, 1)

            dve.wait_ge(s_dst, 32)
            d3 = v3(dstf, 2)
            v.tensor_copy(dstf[0:EP], dsti[0:EP]).then_inc(s_pre, 1)
            ts(dstm[0:EP].bitcast(I32), dsti[0:EP], P - 1, None, ALU.bitwise_and).then_inc(s_pre, 1)
            dve.wait_ge(s_pre, 2)
            v.tensor_copy(dstm[0:EP], dstm[0:EP].bitcast(I32)).then_inc(s_pre, 1)
            ts(srcb[0:EP], v3(srci, 2)[0:EP, 1, :], float(NPAD), None, ALU.add).then_inc(s_pen, 1)
            dve.wait_ge(s_pool, 7)
            with dve.Fori(0, TILES) as i:
                for h in range(2):
                    link(ts(v3(cmpj, 2)[0:EP, h, :], d3[0:EP, h, :], thr[0:EP, ds(i, 1)], 0.0, ALU.is_lt, ALU.add,
                            accum_out=cnt[0:EP, ds(h * TILES + i, 1)]))
            v.tensor_copy(cmpj[0:EP, 0:1], cmpj[0:EP, 1:2]).then_inc(s_cnt, 1)

            dve.wait_ge(s_prev, 16)
            link(tt(dprev[0:EP], dprev[0:EP], dstf[0:EP], ALU.not_equal))
            ts(dprev[0:EP], dprev[0:EP], -BIG, None, ALU.mult).then_inc(s_pen, 1)

            dve.sem_inc(s_qs, 1)
            with dve.Fori(0, GROUPS) as i:
                dve.wait_ge(s_q, i + 2)
                q = v3(bank(0, 2)[:, 0:GRP * D], GRP)
                part = qsp[:, ds(i * (GRP * 3 * D), GRP * 3 * D)].rearrange("p (t k d) -> p t k d", t=GRP, k=3)
                r = v3(qres, GRP)
                link(v.tensor_copy(part[:, :, 0, :], q))
                link(tt(r, q, part[:, :, 0, :], ALU.subtract))
                link(v.tensor_copy(part[:, :, 1, :], r))
                tt(part[:, :, 2, :], r, part[:, :, 1, :], ALU.subtract).then_inc(s_qs, 1)

            dve.wait_ge(s_seg, 1)
            link(v.tensor_copy(seg, bank(7)[:, 0:VT]))
            for l in (1, 0):
                nv = (TILES, VT)[l]
                end = (E, END1)[l]
                if l:
                    s2, n2 = v3(seg, 2), v3(nch, 2)
                    link(tt(n2[:, :, 0:TILES - 1], s2[:, :, 1:TILES], s2[:, :, 0:TILES - 1], ALU.subtract))
                    link(ts(n2[:, :, TILES - 1:TILES], s2[:, :, TILES - 1:TILES], -1.0, float(HALF), ALU.mult, ALU.add))
                    v.tensor_copy(spos[:, 0:TILES], seg[:, 0:TILES])
                    link(ts(spos[:, TILES:VT], seg[:, TILES:VT], float(BASE1), None, ALU.add))
                else:
                    link(tt(spos[:, 0:nv], seg[:, 0:TILES], seg[:, TILES:VT], ALU.add))
                    link(tt(nch[:, 0:nv - 1], spos[:, 1:nv], spos[:, 0:nv - 1], ALU.subtract))
                    link(ts(nch[:, nv - 1:nv], spos[:, nv - 1:nv], -1.0, float(E), ALU.mult, ALU.add))
                link(ts(nchi[:, 0:nv], nch[:, 0:nv], float(CH - 1), None, ALU.add))
                link(ts(nchi[:, 0:nv], nchi[:, 0:nv], CH.bit_length() - 1, None, ALU.arith_shift_right))
                link(v.tensor_copy(nch[:, 0:nv], nchi[:, 0:nv]))
                link(v.tensor_tensor_scan(cum[:, 0:nv], ones[:, 0:nv], nch[:, 0:nv], 0.0, op0=ALU.mult, op1=ALU.add))
                link(tt(nch[:, 0:nv], cum[:, 0:nv], nch[:, 0:nv], ALU.subtract))
                link(ts(nch[:, 0:nv], nch[:, 0:nv], -float(CH), None, ALU.mult))
                link(tt(spos[:, 0:nv], spos[:, 0:nv], nch[:, 0:nv], ALU.add))
                link(ts(col[0:1, 0:1], cum[0:1, nv - 1:nv], float(LAG), None, ALU.add))
                link(ts(hotv[0:1, 0:64], iota_u[0:1, :], col[0:1, 0:1], 0.0, ALU.is_lt, ALU.add, accum_out=col[0:1, 1:2]))
                link(v.tensor_copy(iters_sb[0:1, l:l + 1], col[0:1, 1:2]))
                k = kcol[0:TR, :]
                c = lambda n: col[0:TR, n * TC:(n + 1) * TC]
                which, below, off, tile, way, summed = (c(n) for n in range(6))
                for j in range(TC):
                    link(ts(hotv[0:TR, 0:nv], cum[0:TR, 0:nv], k[:, j:j + 1], 0.0, ALU.is_le, ALU.add, accum_out=which[:, j:j + 1]))
                if l == 0:
                    for j in range(TC):
                        link(ts(hotv[0:TR, 0:nv], cum[0:TR, 0:nv], k[:, j:j + 1], 0.0, ALU.is_lt, ALU.add, accum_out=below[:, j:j + 1]))
                    link(tt(tbe[0:TR, 40:40 + TC], which, below, ALU.is_equal))
                    link(ts(below, k, 0.0, None, ALU.is_gt))
                    link(tt(tbe[0:TR, 40:40 + TC], tbe[0:TR, 40:40 + TC], below, ALU.mult))
                link(ts(below, k, 0.0, float(nv), ALU.is_lt, ALU.mult))
                link(tt(which, which, below, ALU.add))
                for j in range(TC):
                    link(ts(hotv[0:TR, 0:nv], iota_row[0:TR, 0:nv], which[:, j:j + 1], None, ALU.is_equal))
                    link(tt(hotv[0:TR, 0:nv], hotv[0:TR, 0:nv], spos[0:TR, 0:nv], ALU.mult))
                    link(v.tensor_reduce(off[:, j:j + 1], hotv[0:TR, 0:nv], AX_X, ALU.add))
                link(ts(tile, k, float(CH), None, ALU.mult))
                link(tt(off, off, tile, ALU.add))
                link(ts(below, which, float(nv), float(2 * end), ALU.is_ge, ALU.mult))
                link(tt(off, off, below, ALU.add))
                link(ts(off, off, float(end), None, ALU.min))
                link(ts(way, which, float(TILES), None, ALU.is_ge))
                link(ts(tile, way, -float(TILES * l), None, ALU.mult))
                link(tt(tile, tile, which, ALU.add))
                link(ts(tile, tile, float(TILES - 1), None, ALU.min))
                entry = tbe[0:TR, 16 * l:16 * l + 12].bitcast(I32).rearrange("p (c f) -> p c f", c=TC)
                v.tensor_copy(entry[:, :, 0], off)
                ts(entry[:, :, 1], tile, float(3 * D), None, ALU.mult)
                ts(entry[:, :, 2], which, float((RW, LW)[l]), None, ALU.mult)
                ts(entry[:, :, 3], way, float(CH), None, ALU.mult)
                link(ts(tbe[0:TR, 32 + 4 * l:32 + 4 * l + TC], tile, -float(P), None, ALU.mult))
            dve.sem_inc(s_tab, 1)
            dve.wait_ge(s_tabi, 80)

            dve.wait_ge(s_w2, 16 * 31)
            link(ts(epsc[:, :], epsc[:, :], 1.0, None, ALU.add))
            ts(w2u[:, 2 * D:3 * D], w2wu[:, 2 * D:3 * D], epsc[:, :], None, ALU.mult).then_inc(s_wu, 1)
            dve.wait_ge(s_wu, 1)

            dve.wait_ge(s_init, 3)
            dve.wait_ge(s_wcp, 4)
            n0 = dve.value_load(iters_sb[0:1, 0:1], min_val=1, max_val=ITERS)
            for s_, below in ((l_hot, 0), (l_prod, 0), (l_c, 0), (l_pv, 0), (l_acc, 0), (l_f, 1), (l_at, 1)):
                dve.sem_inc(s_, BASE - below)
            last_ = counter(dve, "dve_last", BASE)
            landed_ = counter(dve, "dve_landed", 48)
            kv_s = kv.rearrange("p (u g d) -> p u g d", u=U, g=G)
            hot = s_hot.rearrange("p (u g n) -> p u g n", u=U, g=G)
            pen_s = v3(pen, 3)
            F, SC = v3(fmx, 2), v3(stk, 2)
            con_s, cur_s = v3(contrib, 2), v3(cur, 2)
            with dve.Fori(0, n0) as i:
                for u in range(U):
                    dve.wait_ge(l_ld[u], landed_)
                    ts(v3(st, U)[:, u, :], v3(drow, 3)[:, u % 3, :], iota_col[:, :], None, ALU.is_equal).then_inc(l_hot, 1)
                    dve.wait_ge(l_kc, last_)
                    dve.wait_ge(l_kq, last_)
                    tt(v3(prod, 2)[:, (u - 1) % 2, :].rearrange("d (p g) -> d p g", g=G),
                       bank((u - 1) % 2).rearrange("d (p g) -> d p g", g=G),
                       v3(kts, 2)[:, (u - 1) % 2, :].rearrange("d (g p) -> d p g", g=G), ALU.mult).then_inc(l_prod, 1)
                    w = (u - 2) % 2
                    dve.wait_ge(l_scr, last_)
                    dve.wait_ge(l_c, last_)
                    before = F[0:H, 1 - w, CH - 1:CH]
                    pn = pen_s[0:H, (u - 2) % 3, :]
                    tt(ucar[0:H, w:w + 1], before, pn[:, 0:1], ALU.add)
                    v.tensor_tensor_scan(F[0:H, w, :], pn[:, 0:CH], SC[0:H, w, :], before, op0=ALU.add, op1=ALU.max).then_inc(l_f, 1)
                    dve.wait_ge(l_f, last_)
                    v.tensor_tensor_scan(SC[CP:CP + H, w, ::-1], pn[:, CH:0:-1], F[0:H, w, ::-1], -BIG, op0=ALU.add, op1=ALU.max).then_inc(l_c, 1)
                    dve.wait_ge(l_dcr, last_)
                    tt(hot[:, u, :, :], iota_row[:, None, :].to_broadcast([P, G, P]), dcr[:, :, None].to_broadcast([P, G, P]), ALU.is_equal)
                    dve.wait_ge(l_e, last_)
                    c = con_s[:, (u - 3) % 2, :]
                    rows_ = c[:, H:].rearrange("p (g h w) -> p g h w", g=G, h=H)
                    ts(c[0:1, 0:H], c[0:1, 0:H], 1.0, None, ALU.subtract)
                    tt(rows_[:, :, :, 0:DH], kv_s[:, (u - 3) % U, :, D:2 * D].rearrange("p g (h w) -> p g h w", h=H),
                       rows_[:, :, :, DH:AW].to_broadcast([P, G, H, DH]), ALU.mult).then_inc(l_pv, 1)
                    dve.wait_ge(l_rsc, last_)
                    dve.wait_ge(l_acc, last_)
                    at = atmp.rearrange("p (h w) -> p h w", h=H)
                    tt(at, cur_s[:, (u + 1) % 2, :].rearrange("p (h w) -> p h w", h=H), rsc[:, :, None].to_broadcast([P, H, AW]), ALU.mult).then_inc(l_at, 1)
                    dve.wait_ge(l_at, last_)
                    tt(cur_s[:, u % 2, :], atmp, bank(6 + (u - 4) % 2)[:, H:H + RW], ALU.add).then_inc(l_acc, 1)
                    dve.reg_add(last_, last_, 1)
                dve.reg_add(landed_, landed_, 48)
            v.memset(mark[:, 0:1], 0.0).then_inc(l_over, 1)
            dve.wait_ge(l_over, 3)

            def normalise(to, t3, var, sdev, got, std_, mv_, sd_, rs_, inc=None):
                for t in range(GRP):
                    last = v.bn_stats(std_[:, t * 6:(t + 1) * 6], t3[:, t, :])
                link(last, apart=True)
                for t in range(GRP):
                    last = v.bn_aggr(mv_[:, 2 * t:2 * t + 2], std_[:, t * 6:(t + 1) * 6])
                last.then_inc(var, 1)
                dve.wait_ge(sdev, got)
                link(v.reciprocal(rs_, sd_))
                for t in range(GRP):
                    last = ts(to[:, t, :], t3[:, t, :], mv_[:, 2 * t:2 * t + 1], rs_[:, t:t + 1], ALU.subtract, ALU.mult)
                return last

            r3, h3, hc3, a4 = v3(res, GRP), v3(h1, GRP), v3(h1c, GRP), av.rearrange("p (t h w) -> p t h w", t=GRP, h=H)
            rowb = lambda k: rows[:, k:k + 1, :].to_broadcast([P, GRP, D])
            rd = rden.rearrange("p (t h) -> p t h", t=GRP)
            with dve.Fori(0, GROUPS) as i:
                sums = acc0[:, ds(i * (GRP * RW), GRP * RW)].rearrange("p (t h w) -> p t h w", t=GRP, h=H)
                xg = v3(xs[:, ds(i * (GRP * D), GRP * D)], GRP)
                link(ts(rd, sums[:, :, :, DH], 1e-9, None, ALU.add))
                link(v.reciprocal(rd, rd))
                tt(a4, sums[:, :, :, 0:DH], rd[:, :, :, None].to_broadcast([P, GRP, H, DH]), ALU.mult).then_inc(n_a, 1)
                dve.wait_ge(n_emb, i + 1)
                dve.wait_ge(n_x1c, i + 1)
                link(tt(r3, xg, v3(bank(2, 2)[:, 0:GRP * D], GRP), ALU.add))
                link(normalise(r3, r3, n_var, n_sd, 3 * i + 1, stats, mv, sd, rs))
                link(tt(r3, r3, rowb(0), ALU.mult))
                tt(h3, r3, rowb(1), ALU.add).then_inc(n_h1, 1)
                dve.wait_ge(n_f2, i + 1)
                dve.wait_ge(n_h1c, i + 1)
                link(tt(r3, hc3, v3(bank(2, 2)[:, 0:GRP * D], GRP), ALU.add))
                link(normalise(r3, r3, n_var, n_sd, 3 * i + 2, stats, mv, sd, rs))
                link(tt(r3, r3, rowb(3), ALU.mult))
                link(tt(r3, r3, rowb(4), ALU.add))
                link(tt(r3, r3, xg, ALU.add))
                normalise(r3, r3, n_var, n_sd, 3 * i + 3, stats, mv, sd, rs).then_inc(n_x1, 1)

            dve.wait_ge(n_y, GROUPS)
            dve.wait_ge(n_x1c, GROUPS + 1)
            v.memset(acc1, 0.0).then_inc(m_zero, 1)
            dve.wait_ge(m_zero, 1)
            dve.wait_ge(m_pool, 5)
            n1 = dve.value_load(iters_sb[0:1, 1:2], min_val=1, max_val=ITERS)
            bases(dve, (m_hot, 0), (m_hid, 1), (m_acc, 3))
            hot1 = s1.rearrange("p (u g n) -> p u g n", u=U, g=G)
            with dve.Fori(0, n1) as i:
                for u in range(U):
                    dve.wait_ge(m_ld[u], (i + 1) * 32)
                    entry = i * U + (u + LAG)
                    for t in range(G):
                        last = ts(hot1[:, u, t, :], iota_row[:, :], v3(dcol1, U)[:, u, t:t + 1], nj[1][:, ds(entry, 1)],
                                  ALU.subtract, ALU.is_equal)
                    last.then_inc(m_hot, 1)
                    dve.wait_ge(m_u, i * U + (u - 1 + 1 + BASE))
                    dve.wait_ge(m_con, i * U + (u - 3 + 1 + BASE))
                    tt(v3(hid, 2)[:, (u - 1) % 2, :], bank(1 + (u - 1) % 2), v3(yg, U)[:, (u - 1) % U, :], ALU.add).then_inc(m_hid, 1)
                    into = dve.value_load(tab_sb[1][0:1, ds(4 * (i * U + (u + LAG - 3)) + 2, 1)], min_val=0, max_val=VT * LW)
                    dve.wait_ge(m_agg, i * U + (u - 3 + 1 + BASE))
                    dve.wait_ge(m_acc, i * U + (u - 4 + 1 + BASE))
                    sums = acc1[:, ds(into, LW)]
                    tt(sums, sums, bank(3 + 2 * ((u - 3) % 2))[:, 0:LW], ALU.add).then_inc(m_acc, 1)

            d33, f3, o3 = v3(deg3, GRP), v3(fin, GRP), v3(fout, GRP)
            v.memset(mark[:, 1:2], 0.0).then_inc(m_over, 1)
            dve.wait_ge(m_over, 3)
            with dve.Fori(0, GROUPS) as i:
                xg = v3(xs[:, ds(i * (GRP * D), GRP * D)], GRP)
                dve.wait_ge(f_tp, i + 1)
                for k in range(2):
                    part = v3(acc1[:, ds(i * (GRP * LW) + k * TILES * LW, GRP * LW)], GRP)
                    v.tensor_copy(d33[:, :, k:k + 1], part[:, :, D:LW])
                v.tensor_copy(v3(fx[:, 0:GRP * D], GRP), v3(acc1[:, ds(i * (GRP * LW), GRP * LW)], GRP)[:, :, 0:D]).then_inc(f_deg, 1)
                dve.wait_ge(f_r, i + 2)
                link(tt(f3, f3, xg, ALU.add))
                dve.wait_ge(f_free, i + 1)
                normalise(o3, f3, f_var, f_sd, i + 1, fstats, fmv, fsd, frs).then_inc(f_out, 1)


_INS = ['x', 'src', 'dst', 'edge_attr_16', 'L0_gnn_Wq', 'L0_gnn_Wk', 'L0_gnn_Wv', 'L0_gnn_W0', 'L0_gnn_ln1_g',
        'L0_gnn_ln1_b', 'L0_gnn_fc1_w', 'L0_gnn_fc1_b', 'L0_gnn_fc2_w', 'L0_gnn_fc2_b', 'L0_gnn_ln2_g', 'L0_gnn_ln2_b',
        'L1_gnn_req_emb', 'L1_gnn_W1f', 'L1_gnn_b1f', 'L1_gnn_W2f', 'L1_gnn_b2f', 'L1_gnn_W1b', 'L1_gnn_b1b',
        'L1_gnn_W2b', 'L1_gnn_b2b', 'L1_gnn_Wu', 'L1_gnn_bu', 'L1_gnn_eps']
_OUTS = [((6250, 128), 'float32')]


def kernel(**inputs):
    import numpy as _np
    import concourse.bacc as _bacc
    from concourse import mybir as _mybir
    from concourse.bass_utils import run_bass_kernel_spmd as _run

    nc = _bacc.Bacc("TRN2", target_bir_lowering=False, num_devices=1)
    arrays, args = {}, []
    for name in _INS:
        a = _np.ascontiguousarray(inputs[name])
        arrays[f"in_{name}_dram"] = a
        args.append(nc.dram_tensor(f"in_{name}_dram", a.shape, _mybir.dt.from_np(a.dtype), kind="ExternalInput").ap())
    for i, (shape, dtype) in enumerate(_OUTS):
        dt = _mybir.dt.from_np(_np.dtype(dtype))
        args.append(nc.dram_tensor(f"out_{i}_dram", shape, dt, kind="ExternalOutput").ap())
    gnn_kernel(nc, *args)
    r = _run(nc, [arrays], core_ids=[0])
    got = tuple(r.results[0][f"out_{i}_dram"] for i in range(len(_OUTS)))
    return got[0]
```

```python
from contextlib import ExitStack

import concourse.bass as bass
from concourse import mybir

F32 = mybir.dt.float32
BF16 = mybir.dt.bfloat16
I32 = mybir.dt.int32
ALU = mybir.AluOpType
ACT = mybir.ActivationFunctionType
AX_X = mybir.AxisListType.X
ds = bass.ds

P = 128
N = 6250
D = 128
E = 100000
H = 8
DH = D // H
FF = 512
FC = FF // P
EA = 16
HALF = E // 2
EPS = 1e-5
BIG = 1e30

NT = 125
TILES = N // NT
GRP = 5
GROUPS = TILES // GRP
assert TILES * NT == N and GROUPS * GRP == TILES
G = 4
CH = G * P
VT = 2 * TILES
BASE1 = -(-(HALF + CH) // CH) * CH
END1 = BASE1 + HALF
CP = 32
AW = DH + 1
RW = H * AW
LW = D + 1

U = 6
LAG = 4
TR, TC = 88, 3
TE = TR * TC
ITERS = -(-((E + (CH - 1) * (TILES + 1)) // CH + LAG) // U)
assert ITERS * U + LAG <= TE
MAGIC = 1.5 * 2 ** 23
BASE = 8
EP, EQ = 125, 400


def gnn_kernel(nc, x, src, dst, ea, wq, wk, wv, w0, ln1g, ln1b, fc1w, fc1b, fc2w, fc2b, ln2g, ln2b,
               req, w1f, b1f, w2f, b2f, w1b, b1b, w2b, b2b, wu, bu, eps, out):
    with ExitStack() as ctx:
        def dram(name, shape, dt):
            return nc.dram_tensor(name, shape, dt, kind="Internal").ap()

        def sb(name, shape, dt=F32):
            return ctx.enter_context(nc.sbuf_tensor(name, shape, dt))

        def sem(name):
            return ctx.enter_context(nc.semaphore(name))

        kv_tab = dram("kv_tab", (N, 2 * D), F32)
        y_tab = dram("y_tab", (2 * N, D), F32)
        d0 = dram("d0", (E + CH + 1,), F32)
        pen0 = dram("pen0", (E + CH + 1,), F32)
        i0 = dram("i0", (E + CH,), I32)
        d1 = dram("d1", (END1 + CH,), F32)
        i1 = dram("i1", (END1 + CH,), I32)
        ea1 = dram("ea1", (END1 + CH, EA), F32)
        tabs = [dram(f"tab{l}", (TE, 4), I32) for l in range(2)]
        negs = [dram(f"neg{l}", (TE,), F32) for l in range(2)]
        keeps = dram("keeps", (TE,), F32)
        dm0 = dram("dm0", (E + CH,), F32)

        xs = sb("xs", [P, TILES * D])
        ident = sb("ident", [P, P])
        minus_low = sb("minus_low", [CP + H, H])
        minus = sb("minus", [CP + H, H])
        iota_row = sb("iota_row", [P, P])
        iota_col = sb("iota_col", [P, 1])
        ones = sb("ones", [P, P])
        wqkv = sb("wqkv", [P, 3 * D])
        w0_sb = sb("w0_sb", [P, D])
        fc1_sb = sb("fc1_sb", [P, FF])
        fc2_sb = sb("fc2_sb", [P, FC, D])
        fc1b_sb = sb("fc1b_sb", [P, FC])
        rows = sb("rows", [P, 5, D])
        w1x = sb("w1x", [P, 2 * D])
        w1blk = sb("w1blk", [G * EA + 1, 2 * CH])
        w1r = sb("w1r", [EA, 2 * D])
        reql = sb("reql", [EA, G * EA + 1])
        b1row = sb("b1row", [1, 2 * D])
        w2wu = sb("w2wu", [P, 4 * D])
        w2u = sb("w2u", [P, 3 * D])
        b2col = sb("b2col", [P, 3])
        burow = sb("burow", [1, D])
        dbu = sb("dbu", [3, D])
        sel3 = sb("sel3", [1, 3])
        epsc = sb("epsc", [P, 1])
        eps_ln = sb("eps_ln", [P, 1])
        blockones = sb("blockones", [P, H])
        tab_sb = [sb(f"tab_sb{l}", [1, 4 * TE], I32) for l in range(2)]
        iters_sb = sb("iters_sb", [1, 4], I32)
        nj = [sb(f"nj{l}", [P, TE]) for l in range(2)]
        keep = sb("keep", [P, TE])

        mark = sb("mark", [P, 4])
        reql_one = sb("reql_one", [1, G * EA + 1])

        ARENA = 38000
        arena = sb("arena", [P, ARENA])
        top = [0]

        def carve(n, start=None):
            if start is not None:
                top[0] = start
            a = arena[:, top[0]:top[0] + n]
            top[0] += n
            assert top[0] <= ARENA, top[0]
            return a

        PENW = CH + 8
        acc0 = carve((TILES + 1) * RW, 0)
        qsp = carve(TILES * 3 * D // 2).bitcast(BF16)
        zero0 = top[0]
        contrib = carve(2 * (H + G * RW))
        prod = carve(2 * CH)
        kts = carve(2 * CH)
        stk = carve(2 * CH)
        fmx = carve(2 * CH)
        cur = carve(2 * RW)
        ucar = carve(2)
        pen = carve(3 * PENW)
        s_hot = carve(U * CH)
        kvw = G * 2 * D
        kv = carve(U * kvw)
        zero1 = top[0]
        st = carve(U * CH // 2).bitcast(BF16)
        drow = carve(3 * CH)
        dcol = carve(U * G)
        idx = carve(U * G).bitcast(I32)
        dcr = carve(G)
        rsc = carve(H)
        atmp = carve(RW)
        xT = carve(GRP * P, zero1 - U * kvw)
        cmpb = carve(GRP * EQ).bitcast(BF16)
        kvst = carve(2 * GRP * 2 * D)
        qres = carve(GRP * D)
        xcp = carve(GRP * D)
        assert top[0] <= zero1 + U * CH // 2
        srci = carve(2 * EQ, 0).bitcast(I32)
        srcb = carve(EQ).bitcast(I32)
        dsti = carve(2 * EQ).bitcast(I32)
        dstf = carve(2 * EQ)
        dprev = carve(2 * EQ)
        tilef = carve(2 * EQ)
        dstm = carve(2 * EQ)
        fill = carve(2 * CH)
        filli = carve(CH).bitcast(I32)
        assert top[0] <= TILES * RW
        carve(0, zero1 + U * CH // 2 + 3 * CH + 2 * U * G + G + H + RW)
        cnt = carve(VT)
        kcol = carve(TC)
        iota_u = carve(64)
        thr = carve(TILES)
        seg = carve(VT)
        nch = carve(VT)
        nchi = carve(VT).bitcast(I32)
        cum = carve(VT)
        spos = carve(VT)
        hotv = carve(VT)
        col = carve(8 * TC)
        tbe = carve(16 * 2 + 12)
        av = carve(GRP * D, (TILES + 1) * RW)
        rden = carve(GRP * H)
        nTa = carve(GRP * P)
        nTh = carve(GRP * P)
        res = carve(GRP * D)
        h1 = carve(GRP * D)
        h1c = carve(2 * GRP * D)
        ffT = carve(FC * GRP * P)
        norm1 = [carve(n) for n in (GRP * 6, GRP * 2, GRP, GRP)]
        norm2 = [carve(n) for n in (GRP * 6, GRP * 2, GRP, GRP)]
        assert top[0] >= (VT + 1) * LW
        nTx = carve(GRP * P)
        res2 = carve(GRP * D)
        yst = carve(GRP * 2 * D)
        acc1 = carve((VT + 1) * LW, 0)
        late = max(top[0], (TILES + 1) * RW + 17000)
        con1 = carve(3 * G * LW, late)
        eaT = carve(2 * P)
        deg3 = carve(GRP * 3)
        yg = carve(U * G * D)
        s1 = carve(U * CH)
        hid = carve(2 * CH)
        eat = carve(U * P)
        dcol1 = carve(U * G)
        idx1 = carve(U * G).bitcast(I32)
        late_end = top[0]
        aT = carve(GRP * P * 3, late_end - (U * G * D + U * CH + 2 * CH + U * P + 2 * U * G))
        degT = carve(GRP * P)
        fin = carve(GRP * D)
        norm3 = [carve(n) for n in (GRP * 6, GRP * 2, GRP, GRP)]
        fout = carve(GRP * D)
        fx = carve(3 * GRP * D)

        ps = ctx.enter_context(nc.psum_tensor("ps", [P, 8 * 512], F32))

        def bank(b, n=1):
            return ps[:, b * 512:(b + n) * 512]

        s_zero = sem("s_zero"); s_const = sem("s_const"); s_pool = sem("s_pool")
        s_w = sem("s_w"); s_w2 = sem("s_w2"); s_blk = sem("s_blk"); s_x = sem("s_x"); s_dst = sem("s_dst")
        s_wmm = sem("s_wmm"); s_wcp = sem("s_wcp")
        s_xTp = sem("s_xTp"); s_xT = sem("s_xT"); s_q = sem("s_q"); s_kv = sem("s_kv")
        s_qs = sem("s_qs"); s_kvst = sem("s_kvst"); s_kvo = sem("s_kvo"); s_kvfree = sem("s_kvfree"); s_kz = sem("s_kz")
        s_pre = sem("s_pre"); s_dst_out = sem("s_dst_out"); s_prev = sem("s_prev"); s_pen = sem("s_pen")
        s_cnt = sem("s_cnt"); s_ac = sem("s_ac"); s_seg = sem("s_seg"); s_tab = sem("s_tab"); s_tabo = sem("s_tabo")
        s_tabi = sem("s_tabi"); s_arr = sem("s_arr"); s_ea = sem("s_ea"); s_eac = sem("s_eac"); s_dv = sem("s_dv")
        s_init = sem("s_init"); s_bank = sem("s_bank"); s_xcp = sem("s_xcp"); s_wu = sem("s_wu");
        l_ld = [sem(f"l_ld{k}") for k in range(U)]
        l_ix = [sem(f"l_ix{k}") for k in range(U)]
        l_g = [sem(f"l_g{k}") for k in range(U)]
        l_hot = sem("l_hot"); l_kq = sem("l_kq"); l_kt = sem("l_kt"); l_kc = sem("l_kc"); l_prod = sem("l_prod"); l_s = sem("l_s")
        l_scr = sem("l_scr"); l_f = sem("l_f"); l_c = sem("l_c"); l_d = sem("l_d"); l_e = sem("l_e")
        l_pv = sem("l_pv"); l_agg = sem("l_agg"); l_acc = sem("l_acc"); l_over = sem("l_over"); l_dcr = sem("l_dcr"); l_rsc = sem("l_rsc"); l_at = sem("l_at"); l_x = sem("l_x"); m_over = sem("m_over")
        n_a = sem("n_a"); n_aTp = sem("n_aTp"); n_aT = sem("n_aT"); n_emb = sem("n_emb")
        n_v = [sem(f"n_v{k}") for k in range(3)]
        n_s = [sem(f"n_s{k}") for k in range(3)]
        n_h1 = sem("n_h1"); n_hTp = sem("n_hTp")
        n_hT = sem("n_hT"); n_f1 = sem("n_f1"); n_f1s = sem("n_f1s"); n_f2 = sem("n_f2")
        n_h1c = sem("n_h1c"); n_x1 = sem("n_x1"); n_x1c = sem("n_x1c"); n_xTp = sem("n_xTp"); n_xT = sem("n_xT")
        n_y = sem("n_y"); n_ys = sem("n_ys"); n_yo = sem("n_yo"); n_yfree = sem("n_yfree")
        m_zero = sem("m_zero"); m_pool = sem("m_pool")
        m_ld = [sem(f"m_ld{k}") for k in range(U)]
        m_ix = [sem(f"m_ix{k}") for k in range(U)]
        m_g = [sem(f"m_g{k}") for k in range(U)]
        m_hot = sem("m_hot"); m_eTp = sem("m_eTp"); m_eT = sem("m_eT"); m_u = sem("m_u")
        m_hid = sem("m_hid"); m_con = sem("m_con"); m_agg = sem("m_agg"); m_acc = sem("m_acc")
        f_deg = sem("f_deg"); f_tp = sem("f_tp"); f_t = sem("f_t"); f_o = sem("f_o"); f_r = sem("f_r"); f_b = sem("f_b"); f_x = sem("f_x")
        f_var = sem("f_var"); f_sd = sem("f_sd"); f_out = sem("f_out"); f_dma = sem("f_dma"); f_free = sem("f_free")

        block = ctx.enter_context(nc.Block())
        dst_halves = dst.rearrange("(h p c) -> p h c", h=2, c=EQ)
        src_halves = src.rearrange("(h p c) -> p h c", h=2, c=EQ)
        v3 = lambda a, b: a.rearrange("p (b c) -> p b c", b=b)

        def bases(eng, *pairs):
            for s_, lag in pairs:
                eng.sem_inc(s_, BASE - lag)

        def counter(eng, name, start):
            c = eng.alloc_register(name)
            eng.reg_mov(c, start)
            return c

        def passes(eng, one_pass):
            one_pass(0, None)
            with eng.Fori(0, GROUPS - 1) as i:
                one_pass(i + 1, i)
            one_pass(None, GROUPS - 1)

        def passes3(eng, one_pass, between=None):
            one_pass(0, None, None)
            one_pass(1, 0, None)
            if between:
                between()
            with eng.Fori(0, GROUPS - 2) as i:
                one_pass(i + 2, i + 1, i)
            one_pass(None, GROUPS - 1, GROUPS - 2)
            one_pass(None, None, GROUPS - 1)

        def linker(eng, s_):
            made = eng.alloc_register("made")
            eng.reg_mov(made, 0)

            def link(ins, apart=False):
                ins.then_inc(s_, 1)
                eng.reg_add(made, made, 1)
                if apart:
                    eng.wait_ge(s_, 1)
                eng.wait_ge(s_, made)
            return link

        @block.sync
        def _(sp):
            for k, w in enumerate((wq, wk, wv)):
                sp.dma_start(wqkv[:, k * D:(k + 1) * D], w).then_inc(s_w, 16)
            sp.wait_ge(s_zero, 1)
            sp.dma_start(v3(xs[:, :], TILES)[0:NT], x.rearrange("(t p) d -> p t d", p=NT)).then_inc(s_x, 16)
            sp.dma_start(v3(dsti, 2)[0:EP], dst_halves).then_inc(s_dst, 16)
            sp.dma_start(v3(srci, 2)[0:EP], src_halves).then_inc(s_dst, 16)
            sp.wait_ge(s_pool, 4)
            one = lambda a: a.rearrange("(a n) -> a n", a=1)
            sp.dma_start(one(d0[0:1]), fill[0:1, 0:1]).then_inc(s_arr, 16)
            sp.dma_start(one(d0[E + 1:E + 1 + CH]), fill[0:1, 0:CH]).then_inc(s_arr, 16)
            sp.dma_start(one(pen0[E:E + CH + 1]), fill[1:2, 0:CH + 1]).then_inc(s_arr, 16)
            sp.dma_start(one(i0[E:E + CH]), filli[0:1, 0:CH]).then_inc(s_arr, 16)
            sp.dma_start(one(dm0[E:E + CH]), fill[0:1, 0:CH]).then_inc(s_arr, 16)
            gap = BASE1 - HALF
            sp.dma_start(one(d1[HALF:BASE1]), fill[0:1, 0:gap]).then_inc(s_ea, 16)
            sp.dma_start(one(d1[END1:END1 + CH]), fill[0:1, 0:CH]).then_inc(s_ea, 16)
            sp.dma_start(one(i1[HALF:BASE1]), fill[2:3, 0:gap].bitcast(I32)).then_inc(s_ea, 16)
            sp.dma_start(one(i1[END1:END1 + CH]), filli[0:1, 0:CH]).then_inc(s_ea, 16)
            sp.dma_start(ea1[HALF:BASE1, :].rearrange("(p a) f -> p (a f)", p=16),
                         fill[4:20, 0:gap * EA // 16]).then_inc(s_ea, 16)
            sp.dma_start(ea1[END1:END1 + CH, :].rearrange("(p a) f -> p (a f)", p=16),
                         fill[4:20, 0:CH * EA // 16]).then_inc(s_ea, 16)
            sp.wait_ge(s_pre, 5)
            sp.dma_start(d0[1:1 + E].rearrange("(h p c) -> p h c", h=2, c=EQ), v3(dstf, 2)[0:EP]).then_inc(s_dst_out, 16)
            sp.dma_start(i0[0:E].rearrange("(h p c) -> p h c", h=2, c=EQ), v3(srci, 2)[0:EP]).then_inc(s_arr, 16)
            sp.dma_start(dm0[0:E].rearrange("(h p c) -> p h c", h=2, c=EQ), v3(dstm, 2)[0:EP]).then_inc(s_arr, 16)
            for h, b in ((0, 0), (1, BASE1)):
                sp.dma_start(d1[b:b + HALF].rearrange("(p c) -> p c", c=EQ), v3(dstf, 2)[0:EP, h, :]).then_inc(s_ea, 16)
            sp.wait_ge(s_arr, 16 * 7)
            sp.wait_ge(s_dst_out, 16)
            sp.dma_start(v3(dprev, 2)[0:EP], d0[0:E].rearrange("(h p c) -> p h c", h=2, c=EQ)).then_inc(s_prev, 16)
            sp.wait_ge(s_pen, 2)
            sp.dma_start(pen0[0:E].rearrange("(h p c) -> p h c", h=2, c=EQ), v3(dprev, 2)[0:EP]).then_inc(s_arr, 16)
            for h, b in ((0, 0), (1, BASE1)):
                sp.dma_start(i1[b:b + HALF].rearrange("(p c) -> p c", c=EQ), (v3(srci, 2)[0:EP, 0, :], srcb[0:EP])[h]).then_inc(s_ea, 16)
            for h, b in ((0, 0), (1, BASE1)):
                sp.dma_start(ea1[b:b + HALF, :].rearrange("(p c) f -> p (c f)", p=EP),
                             ea[h * HALF:(h + 1) * HALF, :].rearrange("(p c) f -> p (c f)", p=EP)).then_inc(s_eac, 16)
            sp.sem_inc(s_kvfree, 2)
            with sp.Fori(0, GROUPS) as i:
                sp.wait_ge(s_kvst, i + 2)
                sp.dma_start(kv_tab[ds(i * (GRP * NT), GRP * NT), :].rearrange("(t p) d -> p t d", p=NT),
                             v3(kvst[:, ds((i % 2) * (GRP * 2 * D), GRP * 2 * D)], GRP)[0:NT]).then_inc(s_kvo, 16)
                sp.wait_ge(s_kvo, 16 * i + 16)
                sp.sem_inc(s_kvfree, 1)
            def store_table(l):
                sp.wait_ge(s_tab, l + 1)
                sp.dma_start(tabs[l].rearrange("(p c) f -> p c f", p=TR),
                             tbe[0:TR, 16 * l:16 * l + 12].bitcast(I32).rearrange("p (c f) -> p c f", c=TC)).then_inc(s_tabo, 16)
                sp.dma_start(negs[l].rearrange("(p c) -> p c", p=TR), tbe[0:TR, 32 + 4 * l:32 + 4 * l + TC]).then_inc(s_tabo, 16)

            def load_table(l):
                sp.dma_start(tab_sb[l][:, :], tabs[l].rearrange("(a e) f -> a (e f)", a=1)).then_inc(s_tabi, 16)
                sp.dma_start(nj[l][:, :], negs[l].rearrange("(a e) -> a e", a=1).to_broadcast([P, TE])).then_inc(s_tabi, 16)

            store_table(0)
            sp.dma_start(keeps.rearrange("(p c) -> p c", p=TR), tbe[0:TR, 40:40 + TC]).then_inc(s_tabo, 16)
            sp.wait_ge(s_tabo, 48)
            load_table(0)
            sp.dma_start(keep[:, :], keeps.rearrange("(a e) -> a e", a=1).to_broadcast([P, TE])).then_inc(s_tabi, 16)

            sp.wait_ge(s_tabi, 48)
            sp.wait_ge(s_arr, 16 * 8)
            sp.wait_ge(s_init, 3)
            n0 = sp.value_load(iters_sb[0:1, 0:1], min_val=1, max_val=ITERS)
            used = counter(sp, "used", BASE - 2)
            with sp.Fori(0, n0) as i:
                for u in range(U):
                    off = sp.value_load(tab_sb[0][0:1, ds(4 * (i * U + (u + LAG)), 1)], min_val=0, max_val=E)
                    off2 = sp.value_load(tab_sb[0][0:1, ds(4 * (i * U + (u + LAG - 2)), 1)], min_val=0, max_val=E)
                    sp.wait_ge(s_init, 3)
                    sp.wait_ge(l_pv, used)
                    sp.dma_start(v3(idx, U)[:, u, :], i0[ds(off, CH)].rearrange("(p g) -> p g", g=G)).then_inc(l_ix[u], 16)
                    sp.dma_start(v3(dcol, U)[:, u, :], d0[ds(off + 1, CH)].rearrange("(p g) -> p g", g=G)).then_inc(l_ld[u], 16)
                    sp.dma_start(v3(drow, 3)[:, u % 3, :],
                                 dm0[ds(off, CH)].rearrange("(a n) -> a n", a=1).to_broadcast([P, CH])).then_inc(l_ld[u], 16)
                    sp.dma_start(v3(pen, 3)[0:H, (u - 2) % 3, 0:CH],
                                 pen0[ds(off2, CH)].rearrange("(a n) -> a n", a=1).to_broadcast([H, CH])).then_inc(l_ld[u], 16)
                    sp.reg_add(used, used, 1)

            store_table(1)
            sp.wait_ge(s_tabo, 80)
            load_table(1)
            sp.sem_inc(n_yfree, 1)
            with sp.Fori(0, GROUPS) as i:
                sp.wait_ge(n_ys, i + 2)
                for h in range(2):
                    sp.dma_start(y_tab[ds(h * N + i * (GRP * NT), GRP * NT), :].rearrange("(t p) d -> p t d", p=NT),
                                 v3(yst, GRP)[0:NT, :, h * D:(h + 1) * D]).then_inc(n_yo, 16)
                sp.wait_ge(n_yo, 32 * i + 32)
                sp.sem_inc(n_yfree, 1)

            sp.wait_ge(m_pool, 5)
            sp.wait_ge(s_ea, 16 * 10)
            sp.wait_ge(s_eac, 32)
            sp.wait_ge(s_tabi, 80)
            n1 = sp.value_load(iters_sb[0:1, 1:2], min_val=1, max_val=ITERS)
            free6 = counter(sp, "free6", BASE - U + 1)
            with sp.Fori(0, n1) as i:
                for u in range(U):
                    off = sp.value_load(tab_sb[1][0:1, ds(4 * (i * U + (u + LAG)), 1)], min_val=0, max_val=END1)
                    sp.wait_ge(m_pool, 5)
                    sp.wait_ge(m_hid, free6)
                    sp.dma_start(v3(idx1, U)[:, u, :], i1[ds(off, CH)].rearrange("(p g) -> p g", g=G)).then_inc(m_ix[u], 16)
                    sp.dma_start(v3(dcol1, U)[:, u, :], d1[ds(off, CH)].rearrange("(p g) -> p g", g=G)).then_inc(m_ld[u], 16)
                    sp.dma_start(v3(eat, U)[:, u, 0:G * EA], ea1[ds(off, CH), :].rearrange("(p g) f -> p (g f)", g=G)).then_inc(m_ld[u], 16)
                    sp.reg_add(free6, free6, 1)

            sp.sem_inc(f_free, 1)
            with sp.Fori(0, GROUPS) as i:
                sp.wait_ge(f_out, i + 2)
                sp.dma_start(out[ds(i * (GRP * NT), GRP * NT), :].rearrange("(t p) d -> p t d", p=NT),
                             v3(fout, GRP)[0:NT]).then_inc(f_dma, 16)
                sp.wait_ge(f_dma, 16 * i + 16)
                sp.sem_inc(f_free, 1)
            sp.wait_ge(n_yo, 32 * GROUPS)

        @block.gpsimd
        def _(pool):
            g = nc.gpsimd
            g.memset(ident[:, :], 0.0).then_inc(s_const, 1)
            g.memset(ones[:, :], 1.0).then_inc(s_const, 1)
            pool.wait_ge(s_const, 2)
            g.affine_select(out=ident[:, :], in_=ident[:, :], compare_op=ALU.not_equal, fill=1.0, base=0,
                            pattern=[[-1, P]], channel_multiplier=1).then_inc(s_const, 1)
            g.memset(blockones[:, :], 0.25).then_inc(s_const, 1)
            pool.wait_ge(s_const, 4)
            g.affine_select(out=blockones[:, :], in_=blockones[:, :], compare_op=ALU.is_ge, fill=0.0, base=0,
                            pattern=[[-DH, H]], channel_multiplier=1).then_inc(s_const, 1)
            pool.wait_ge(s_const, 5)
            g.affine_select(out=blockones[:, :], in_=blockones[:, :], compare_op=ALU.is_ge, fill=0.0, base=DH - 1,
                            pattern=[[DH, H]], channel_multiplier=-1).then_inc(s_const, 1)
            g.iota(iota_row[:, :], [[1, P]], base=0, channel_multiplier=0, allow_small_or_imprecise_dtypes=True).then_inc(s_const, 1)
            g.iota(iota_col[:, :], [[0, 1]], base=0, channel_multiplier=1, allow_small_or_imprecise_dtypes=True).then_inc(s_const, 1)
            g.memset(fill, 0.0).then_inc(s_pool, 1)
            pool.wait_ge(s_pool, 1)
            g.affine_select(out=fill, in_=fill, compare_op=ALU.not_equal, fill=-BIG, base=-1,
                            pattern=[[0, 2 * CH]], channel_multiplier=1).then_inc(s_pool, 1)
            g.memset(filli, 0).then_inc(s_pool, 1)
            pool.wait_ge(s_pool, 3)
            g.memset(fill[0:1, :], -1.0).then_inc(s_pool, 1)
            g.iota(kcol[0:TR, :], [[1, TC]], base=-LAG, channel_multiplier=TC, allow_small_or_imprecise_dtypes=True).then_inc(s_pool, 1)
            g.iota(iota_u, [[U, 64]], base=0, channel_multiplier=0, allow_small_or_imprecise_dtypes=True).then_inc(s_pool, 1)
            g.iota(thr, [[1, TILES]], base=0, channel_multiplier=0, allow_small_or_imprecise_dtypes=True).then_inc(s_pool, 1)

            pool.wait_ge(s_x, 16)
            with pool.Fori(0, GROUPS) as i:
                pool.wait_ge(s_xTp, i + 1)
                g.tensor_copy(xcp, xs[:, ds(i * (GRP * D), GRP * D)]).then_inc(s_xcp, 1)

            g.memset(arena[:, zero0:zero1 - U * kvw], 0.0).then_inc(s_init, 1)
            pool.wait_ge(s_ac, GROUPS)
            pool.wait_ge(s_cnt, 1)
            pool.wait_ge(s_pen, 2)
            pool.wait_ge(s_prev, 16)
            pool.wait_ge(s_dst_out, 16)
            pool.wait_ge(s_arr, 16 * 8)
            pool.wait_ge(s_ea, 16 * 10)
            g.memset(acc0, 0.0).then_inc(s_init, 1)
            pool.wait_ge(s_qs, GROUPS + 1)
            pool.wait_ge(s_kvo, 16 * GROUPS)
            g.memset(kv[:, (U - 1) * kvw:], 0.0).then_inc(s_kz, 1)
            g.memset(kv[:, (U - 3) * kvw:(U - 1) * kvw], 0.0).then_inc(s_kz, 1)
            pool.wait_ge(s_kz, 2)
            pool.wait_ge(s_tabi, 48)
            pool.sem_inc(s_init, 1)

            pool.wait_ge(s_init, 3)
            slot_free = counter(pool, "slot_free", BASE - 2)
            landed = counter(pool, "landed", 16)
            n0 = pool.value_load(iters_sb[0:1, 0:1], min_val=1, max_val=ITERS)
            kv_s = kv.rearrange("p (u g d) -> p u g d", u=U, g=G)
            with pool.Fori(0, n0):
                for u in range(U):
                    pool.wait_ge(s_init, 3)
                    pool.wait_ge(l_pv, slot_free)
                    pool.wait_ge(l_ix[u], landed)
                    for t in range(G):
                        g.indirect_dma_start(kv_s[:, u, t, :], None, kv_tab,
                                             bass.IndirectOffsetOnAxis(ap=v3(idx, U)[:, u, t:t + 1], axis=0)).then_inc(l_g[u], 16)
                    pool.reg_add(slot_free, slot_free, 1)
                pool.reg_add(landed, landed, 16)

            pool.wait_ge(l_over, 3)
            g.memset(con1, 1.0).then_inc(m_pool, 1)
            g.memset(eaT, 1.0).then_inc(m_pool, 1)
            g.memset(deg3, 1.0).then_inc(m_pool, 1)
            g.memset(yg, 0.0).then_inc(m_pool, 1)
            g.memset(arena[:, late + 3 * G * LW + 2 * P + GRP * 3 + U * G * D:late_end], 0.0).then_inc(m_pool, 1)

            def pool_pass(new, mid, old):
                if old is not None:
                    pool.wait_ge(n_x1, old + 1)
                    g.tensor_copy(xs[:, ds(old * (GRP * D), GRP * D)], res2).then_inc(n_x1c, 1)
                if new is not None:
                    pool.wait_ge(n_h1, new + 1)
                    g.tensor_tensor(v3(h1c[:, ds((new % 2) * (GRP * D), GRP * D)], GRP), v3(h1, GRP),
                                    rows[:, 2:3, :].to_broadcast([P, GRP, D]), ALU.add).then_inc(n_h1c, 1)

            pool.sem_inc(n_x1c, 1)
            passes3(pool, pool_pass)

            pool.wait_ge(m_pool, 5)
            pool.wait_ge(n_yo, 32 * GROUPS)
            pool.reg_mov(slot_free, BASE - U + 1)
            pool.reg_mov(landed, 16)
            pool.wait_ge(s_tabi, 80)
            n1 = pool.value_load(iters_sb[0:1, 1:2], min_val=1, max_val=ITERS)
            yg_s = yg.rearrange("p (u g d) -> p u g d", u=U, g=G)
            with pool.Fori(0, n1):
                for u in range(U):
                    pool.wait_ge(m_pool, 5)
                    pool.wait_ge(m_hid, slot_free)
                    pool.wait_ge(m_ix[u], landed)
                    for t in range(G):
                        g.indirect_dma_start(yg_s[:, u, t, :], None, y_tab,
                                             bass.IndirectOffsetOnAxis(ap=v3(idx1, U)[:, u, t:t + 1], axis=0)).then_inc(m_g[u], 16)
                    pool.reg_add(slot_free, slot_free, 1)
                pool.reg_add(landed, landed, 16)

            pool.wait_ge(m_over, 3)
            def pool_last(new, old):
                if new is not None:
                    pool.wait_ge(f_tp, new + 1)
                    g.tensor_copy(fx[:, 2 * GRP * D:], xs[:, ds(new * (GRP * D), GRP * D)]).then_inc(f_x, 1)

            passes(pool, pool_last)

        @block.scalar
        def _(act):
            a = nc.scalar
            row = lambda t: t.rearrange("(a n) -> a n", a=1)
            act.dma_start(w0_sb[:, :], w0).then_inc(s_w2, 16)
            act.dma_start(fc1_sb[:, :], fc1w).then_inc(s_w2, 16)
            act.dma_start(fc2_sb[:, :, :], fc2w.rearrange("(c p) d -> p c d", p=P)).then_inc(s_w2, 16)
            act.dma_start(fc1b_sb[:, :], fc1b.rearrange("(c p) -> p c", p=P), allow_slow_non_contiguous=True).then_inc(s_w2, 16)
            for k, t in enumerate((ln1g, ln1b, fc2b, ln2g, ln2b)):
                act.dma_start(rows[:, k, :], row(t).to_broadcast([P, D])).then_inc(s_w2, 16)
            for k, (w, b) in enumerate(((w1f, b1f), (w1b, b1b))):
                act.dma_start(w1x[:, k * D:(k + 1) * D], w[0:D, :]).then_inc(s_w2, 16)
                act.dma_start(w1r[:, k * D:(k + 1) * D], w[D + EA:D + 2 * EA, :]).then_inc(s_w2, 16)
                act.dma_start(b1row[:, k * D:(k + 1) * D], row(b)).then_inc(s_w2, 16)
            for k, w in enumerate((w2f, w2b, wu)):
                act.dma_start(w2wu[:, k * D:(k + 1) * D], w).then_inc(s_w2, 16)
            act.dma_start(burow[:, :], row(bu)).then_inc(s_w2, 16)
            act.dma_start(epsc[:, :], row(eps).to_broadcast([P, 1])).then_inc(s_w2, 16)
            act.wait_ge(s_blk, 3)
            for k, w in enumerate((w1f, w1b)):
                for t in range(G):
                    act.dma_start(w1blk[t * EA:(t + 1) * EA, k * CH + t * D:k * CH + (t + 1) * D],
                                  w[D:D + EA, :]).then_inc(s_w2, 16)
            act.dma_start(reql[:, G * EA:G * EA + 1], req.rearrange("a f -> f a"), allow_slow_non_contiguous=True).then_inc(s_w2, 16)
            act.dma_start(b2col[:, 0:1], b2f.rearrange("(p a) -> p a", a=1)).then_inc(s_w2, 16)
            act.dma_start(b2col[:, 1:2], b2b.rearrange("(p a) -> p a", a=1)).then_inc(s_w2, 16)

            act.sem_inc(s_kvst, 1)
            tiles1 = v3(dsti.bitcast(BF16)[:, 0:2 * EQ], 2)[0:EP, 1, :]

            def act_first(new, old):
                if old is not None:
                    act.wait_ge(s_kv, old + 1)
                if new is not None:
                    act.wait_ge(s_xTp, new + 2)
                    a.activation(xT, bank(2, 2)[:, 0:GRP * P], ACT.Copy).then_inc(s_xT, 1)
                if old is not None:
                    act.wait_ge(s_kvfree, old + 1)
                    a.activation(kvst[:, ds((old % 2) * (GRP * 2 * D), GRP * 2 * D)], bank(4, 4)[:, 0:GRP * 2 * D], ACT.Copy).then_inc(s_kvst, 1)
                    act.wait_ge(s_pre, 7)
                    for t in range(GRP):
                        last = a.activation(cmpb[0:EP, (2 * t + 1) * EQ:(2 * t + 2) * EQ], tiles1, ACT.Sign,
                                            bias=thr[0:EP, ds(old * GRP + t, 1)], scale=-1.0,
                                            accum_out=cnt[0:EP, ds(old * GRP + (TILES + t), 1)])
                    last.then_inc(s_ac, 1)
                    act.wait_ge(s_ac, old + 1)

            passes(act, act_first)

            act.wait_ge(s_wmm, 1)
            a.activation(w2u[:, 0:2 * D], bank(0)[:, 0:2 * D], ACT.Copy).then_inc(s_wcp, 1)
            act.wait_ge(s_wmm, 2)
            a.activation(w1blk[G * EA:G * EA + 1, :].rearrange("p (k g d) -> p k g d", k=2, g=G),
                         bank(1)[G * EA:G * EA + 1, 0:2 * D].rearrange("p (k d) -> p k d", k=2)[:, :, None, :].to_broadcast([1, 2, G, D]),
                         ACT.Copy).then_inc(s_wcp, 1)
            act.wait_ge(s_wmm, 3)
            a.activation(w2u[:, 0:2 * D], bank(2)[:, 0:2 * D], ACT.Copy).then_inc(s_wcp, 1)
            a.activation(dbu[:, :], bank(3)[0:3, 0:D], ACT.Copy).then_inc(s_wcp, 1)

            act.wait_ge(s_init, 3)
            n0 = act.value_load(iters_sb[0:1, 0:1], min_val=1, max_val=ITERS)
            for s_, below in ((l_kc, 0), (l_scr, 0), (l_e, 0), (l_dcr, 1), (l_rsc, 1), (l_x, 1)):
                act.sem_inc(s_, BASE - below)
            last_ = counter(act, "act_last", BASE)
            now = counter(act, "act_now", BASE + 1)
            landed_ = counter(act, "act_landed", 48)
            con_s = v3(contrib, 2)
            with act.Fori(0, n0) as i:
                for u in range(U):
                    into = act.value_load(tab_sb[0][0:1, ds(4 * (i * U + u) + 2, 1)], min_val=0, max_val=TILES * RW)
                    act.wait_ge(l_ld[u], landed_)
                    a.activation(dcr, v3(dcol, U)[:, u, :], ACT.Identity, bias=nj[0][:, ds(i * U + (u + LAG), 1)]).then_inc(l_dcr, 1)
                    act.wait_ge(l_kt, now)
                    act.wait_ge(l_prod, last_)
                    a.activation(v3(kts, 2)[:, u % 2, :], bank(2 + u % 2), ACT.Copy).then_inc(l_kc, 1)
                    act.wait_ge(l_agg, last_)
                    kp = keep[:, ds(i * U + u, 1)]
                    a.activation(rsc, bank(6 + (u - 4) % 2)[:, 0:H], ACT.Identity, scale=kp, bias=kp).then_inc(l_rsc, 1)
                    act.wait_ge(l_s, now)
                    a.activation(v3(stk, 2)[0:H, (u - 1) % 2, :], bank(4)[0:H, :], ACT.Copy).then_inc(l_scr, 1)
                    act.wait_ge(l_d, now)
                    dps = bank(5)[:, 0:40]
                    c = con_s[:, (u - 2) % 2, :]
                    a.activation(c[:, H:].rearrange("p (g h w) -> p g h w", g=G, h=H)[:, :, :, DH],
                                 dps[:, 0:G * H].rearrange("p (g h) -> p g h", g=G), ACT.Exp)
                    a.activation(c[0:1, 0:H], dps[0:1, G * H:G * H + H], ACT.Exp).then_inc(l_x, 1)
                    act.wait_ge(l_x, last_)
                    a.activation(c[0:1, 0:H], c[0:1, 0:H], ACT.Identity, bias=-1.0).then_inc(l_e, 1)
                    act.wait_ge(l_acc, now)
                    a.activation(acc0[:, ds(into, RW)], v3(cur, 2)[:, u % 2, :], ACT.Copy)
                    act.reg_add(last_, last_, 1)
                    act.reg_add(now, now, 1)
                act.reg_add(landed_, landed_, 48)

            a.activation(mark[:, 2:3], eps_ln[:, :], ACT.Copy).then_inc(l_over, 1)
            act.wait_ge(l_over, 3)

            def sqrt(k, at, norm):
                act.wait_ge(n_v[k], at + 1)
                a.activation(norm[2], v3(norm[1], GRP)[:, :, 1], ACT.Sqrt, bias=eps_ln[:, :]).then_inc(n_s[k], 1)

            def relu(new, c):
                act.wait_ge(n_f1, new * FC + (c + 1))
                a.activation(v3(ffT, FC)[:, c, :], bank(4 + 2 * (c % 2), 2)[:, 0:GRP * P], ACT.Relu,
                             bias=fc1b_sb[:, c:c + 1]).then_inc(n_f1s, 1)

            def act_pass(new, mid, old):
                if mid is not None:
                    act.wait_ge(n_hTp, mid + 1)
                    a.activation(nTh, bank(0, 2)[:, 0:GRP * P], ACT.Copy).then_inc(n_hT, 1)
                    relu(mid, 0)
                if old is not None:
                    sqrt(1, old, norm2)
                if mid is not None:
                    relu(mid, 1)
                if new is not None:
                    act.wait_ge(n_aTp, new + 1)
                    a.activation(nTa, bank(0, 2)[:, 0:GRP * P], ACT.Copy).then_inc(n_aT, 1)
                if mid is not None:
                    relu(mid, 2)
                    relu(mid, 3)
                if old is not None:
                    sqrt(2, old, norm2)
                if new is not None:
                    sqrt(0, new, norm1)
                if old is not None:
                    act.wait_ge(n_xTp, old + 2)
                    a.activation(nTx, bank(0, 2)[:, 0:GRP * P], ACT.Copy).then_inc(n_xT, 1)
                    act.wait_ge(n_y, old + 1)
                    act.wait_ge(n_yfree, old + 1)
                    a.activation(yst, bank(4, 3)[:, 0:GRP * 2 * D], ACT.Copy).then_inc(n_ys, 1)

            act.sem_inc(n_ys, 1)
            passes3(act, act_pass)

            act.wait_ge(m_pool, 5)
            bases(act, (m_eT, 0), (m_con, 1))
            act.wait_ge(s_tabi, 80)
            n1 = act.value_load(iters_sb[0:1, 1:2], min_val=1, max_val=ITERS)
            hid_s = v3(hid, 2)
            con1_s = con1.rearrange("p (u g w) -> p u g w", u=3, g=G)
            with act.Fori(0, n1) as i:
                for u in range(U):
                    act.wait_ge(m_eTp, i * U + (u + 1 + BASE))
                    a.activation(v3(eaT, 2)[0:G * EA, u % 2, :], bank(4 * (u % 2))[0:G * EA, 0:P], ACT.Copy).then_inc(m_eT, 1)
                    act.wait_ge(m_hid, i * U + (u - 1 + 1 + BASE))
                    act.wait_ge(m_agg, i * U + (u - 4 + 1 + BASE))
                    a.activation(con1_s[:, (u - 1) % 3, :, 0:D], v3(hid_s[:, (u - 1) % 2, :], G), ACT.Relu).then_inc(m_con, 1)

            a.activation(mark[:, 3:4], eps_ln[:, :], ACT.Copy).then_inc(m_over, 1)
            act.wait_ge(m_over, 3)

            act.sem_inc(f_r, 1)
            def act_last(new, old):
                if new is not None:
                    act.wait_ge(f_tp, new + 1)
                    a.activation(v3(fx[:, GRP * D:2 * GRP * D], GRP),
                                 v3(acc1[:, ds(new * (GRP * LW) + TILES * LW, GRP * LW)], GRP)[:, :, 0:D], ACT.Copy).then_inc(f_b, 1)
                if old is not None:
                    act.wait_ge(f_o, old + 1)
                    act.wait_ge(f_out, old + 1)
                    a.activation(fin, bank(6, 2)[:, 0:GRP * D], ACT.Relu).then_inc(f_r, 1)
                    act.wait_ge(f_var, old + 1)
                    a.activation(norm3[2], v3(norm3[1], GRP)[:, :, 1], ACT.Sqrt, bias=eps_ln[:, :]).then_inc(f_sd, 1)
                if new is not None:
                    act.wait_ge(f_tp, new + 2)
                    a.activation(aT, bank(0, 4)[:, 0:3 * GRP * P], ACT.Copy)
                    a.activation(degT[0:3, :], bank(4, 2)[0:3, 0:GRP * P], ACT.Copy).then_inc(f_t, 1)

            passes(act, act_last)

        @block.tensor
        def _(pe):
            mm = nc.tensor.matmul
            tp = nc.tensor.transpose
            pe.wait_ge(s_const, 8)
            pe.wait_ge(s_bank, 1)
            pe.wait_ge(s_w, 48)
            pe.sem_inc(s_q, 1)
            pe.sem_inc(s_xTp, 1)

            def pe_first(new, old):
                if old is not None:
                    pe.wait_ge(s_xT, old + 1)
                    pe.wait_ge(s_qs, old + 1)
                    for t in range(GRP):
                        last = mm(bank(0, 2)[:, t * D:(t + 1) * D], xT[:, t * P:(t + 1) * P], wqkv[:, 0:D])
                    last.then_inc(s_q, 1)
                    pe.wait_ge(s_kvst, old + 1)
                    for t in range(GRP):
                        last = mm(bank(4, 4)[:, t * 2 * D:(t + 1) * 2 * D], xT[:, t * P:(t + 1) * P], wqkv[:, D:3 * D])
                    last.then_inc(s_kv, 1)
                if new is not None:
                    pe.wait_ge(s_xcp, new + 1)
                    for t in range(GRP):
                        last = tp(bank(2, 2)[:, t * P:(t + 1) * P], xcp[:, t * D:(t + 1) * D], ident[:, :])
                    last.then_inc(s_xTp, 1)

            passes(pe, pe_first)

            pe.wait_ge(s_cnt, 1)
            pe.wait_ge(s_ac, GROUPS)
            pe.wait_ge(s_kvst, GROUPS + 1)
            mm(bank(7)[:, 0:VT], ones[0:EP, :], cnt[0:EP, 0:VT]).then_inc(s_seg, 1)
            pe.wait_ge(s_w2, 16 * (9 + 6 + 5 + 8 + 3))
            pe.wait_ge(s_blk, 7)
            pe.wait_ge(s_qs, GROUPS + 1)
            for k in range(2):
                last = tp(bank(0)[:, k * D:(k + 1) * D], w2wu[:, k * D:(k + 1) * D], ident[:, :])
            last.then_inc(s_wmm, 1)
            for k in range(2):
                mm(bank(1)[0:G * EA + 1, k * D:(k + 1) * D], reql[:, :], w1r[:, k * D:(k + 1) * D], start=True, stop=False)
                last = mm(bank(1)[0:G * EA + 1, k * D:(k + 1) * D], reql_one[:, :], b1row[:, k * D:(k + 1) * D], start=False, stop=True)
            last.then_inc(s_wmm, 1)
            pe.wait_ge(s_wcp, 1)
            for k in range(2):
                mm(bank(2)[:, k * D:(k + 1) * D], w2u[:, k * D:(k + 1) * D], w2wu[:, 2 * D:3 * D])
            mm(bank(3)[0:3, 0:D], b2col[:, :], w2wu[:, 2 * D:3 * D], start=True, stop=False)
            mm(bank(3)[0:3, 0:D], sel3[:, :], burow[:, :], start=False, stop=True).then_inc(s_wmm, 1)

            pe.wait_ge(s_init, 3)
            pe.wait_ge(s_wcp, 4)
            n0 = pe.value_load(iters_sb[0:1, 0:1], min_val=1, max_val=ITERS)
            kv_s = kv.rearrange("p (u g d) -> p u g d", u=U, g=G)
            st_s = v3(st, U)
            con_s = v3(contrib, 2)
            for s_ in (l_kt, l_kq, l_s, l_d, l_agg):
                pe.sem_inc(s_, BASE)
            last_ = counter(pe, "pe_last", BASE)
            now = counter(pe, "pe_now", BASE + 1)
            landed_ = counter(pe, "pe_landed", 16 * G)
            with pe.Fori(0, n0) as i:
                for u in range(U):
                    tile = pe.value_load(tab_sb[0][0:1, ds(4 * (i * U + (u + LAG)) + 1, 1)], min_val=0, max_val=(TILES - 1) * 3 * D)
                    pe.wait_ge(l_g[u], landed_)
                    pe.wait_ge(l_kc, last_)
                    for t in range(G):
                        last = tp(bank(2 + u % 2)[:, t * P:(t + 1) * P], kv_s[:, u, t, 0:D], ident[:, :])
                    last.then_inc(l_kt, 1)
                    pe.wait_ge(l_hot, now)
                    pe.wait_ge(l_prod, last_)
                    for k in range(3):
                        last = mm(bank(u % 2), qsp[:, ds(tile + k * D, D)], st_s[:, u, :], start=(k == 0), stop=(k == 2))
                    last.then_inc(l_kq, 1)
                    pe.wait_ge(l_prod, now)
                    pe.wait_ge(l_scr, last_)
                    mm(bank(4)[0:H, :], blockones[:, :], v3(prod, 2)[:, (u - 1) % 2, :]).then_inc(l_s, 1)
                    pe.wait_ge(l_c, now)
                    pe.wait_ge(l_e, last_)
                    dps = bank(5)[:, 0:40]
                    w = (u - 2) % 2
                    both = v3(stk, 2)[0:CP + H, w, :].rearrange("h (p g) -> h g p", g=G)
                    for t in range(G):
                        mm(dps[:, t * H:(t + 1) * H], both[:, t, :], minus[:, :])
                    mm(dps[0:1, G * H:G * H + H], ucar[0:CP + H, w:w + 1], minus[:, :], start=True, stop=False)
                    mm(dps[0:1, G * H:G * H + H], both[:, 0, 0:1], minus_low[:, :], start=False, stop=True).then_inc(l_d, 1)
                    pe.wait_ge(l_pv, now)
                    pe.wait_ge(l_acc, last_)
                    agg = bank(6 + (u - 3) % 2)[:, 0:H + RW]
                    c = con_s[:, (u - 3) % 2, :]
                    hot = s_hot.rearrange("p (u g n) -> p u g n", u=U, g=G)[:, (u - 3) % U]
                    mm(agg, hot[:, 0, :], c[:, 0:H + RW], start=True, stop=False)
                    for t in range(1, G):
                        last = mm(agg[:, H:], hot[:, t, :], c[:, H + t * RW:H + (t + 1) * RW], start=False, stop=(t == G - 1))
                    last.then_inc(l_agg, 1)
                    pe.reg_add(last_, last_, 1)
                    pe.reg_add(now, now, 1)
                pe.reg_add(landed_, landed_, 16 * G)

            mm(bank(1)[0:1, 0:1], ones[:, 0:1], ones[:, 0:1]).then_inc(l_over, 1)
            pe.wait_ge(l_over, 3)

            def transposes(src, done):
                for t in range(GRP):
                    last = tp(bank(0, 2)[:, t * P:(t + 1) * P], src[:, t * D:(t + 1) * D], ident[:, :])
                last.then_inc(done, 1)

            def hidden(mid, c):
                for a0, a1 in ((0, 512), (512, GRP * P)):
                    last = mm(bank(4 + 2 * (c % 2), 2)[:, a0:a1], fc1_sb[:, c * P:(c + 1) * P], nTh[:, a0:a1])
                last.then_inc(n_f1, 1)

            def pe_pass(new, mid, old):
                if mid is not None:
                    pe.wait_ge(n_h1, mid + 1)
                    transposes(h1, n_hTp)
                    pe.wait_ge(n_hT, mid + 1)
                    pe.wait_ge(n_ys, 1 if old is None else old + 1)
                    hidden(mid, 0)
                    hidden(mid, 1)
                if new is not None:
                    pe.wait_ge(n_a, new + 1)
                    transposes(av, n_aTp)
                if mid is not None:
                    pe.wait_ge(n_f1s, mid * FC + 1)
                    hidden(mid, 2)
                if new is not None:
                    pe.wait_ge(n_aT, new + 1)
                    for t in range(GRP):
                        last = mm(bank(0, 2)[:, t * D:(t + 1) * D], nTa[:, t * P:(t + 1) * P], w0_sb[:, :])
                    last.then_inc(n_emb, 1)
                if mid is not None:
                    pe.wait_ge(n_f1s, mid * FC + 2)
                    hidden(mid, 3)
                    pe.wait_ge(n_f1s, mid * FC + FC)
                    if old is not None:
                        pe.wait_ge(n_v[1], old + 1)
                    for t in range(GRP):
                        for c in range(FC):
                            last = mm(bank(2, 2)[:, t * D:(t + 1) * D], v3(ffT, FC)[:, c, t * P:(t + 1) * P], fc2_sb[:, c, :],
                                      start=(c == 0), stop=(c == FC - 1))
                    last.then_inc(n_f2, 1)
                if old is not None:
                    if new is not None:
                        pe.wait_ge(n_v[0], new + 1)
                    pe.wait_ge(n_x1, old + 1)
                    transposes(res2, n_xTp)
                    pe.wait_ge(n_xT, old + 1)
                    for t in range(GRP):
                        last = mm(bank(4, 3)[:, t * 2 * D:(t + 1) * 2 * D], nTx[:, t * P:(t + 1) * P], w1x[:, :])
                    last.then_inc(n_y, 1)

            pe.sem_inc(n_xTp, 1)
            passes3(pe, pe_pass)

            pe.wait_ge(m_pool, 5)
            pe.wait_ge(n_ys, GROUPS + 1)
            bases(pe, (m_eTp, 0), (m_u, 1), (m_agg, 2))
            pe.wait_ge(s_tabi, 80)
            n1 = pe.value_load(iters_sb[0:1, 1:2], min_val=1, max_val=ITERS)
            con1_s = con1.rearrange("p (u g w) -> p u g w", u=3, g=G)
            hot1 = s1.rearrange("p (u g n) -> p u g n", u=U, g=G)
            with pe.Fori(0, n1) as i:
                for u in range(U):
                    way = pe.value_load(tab_sb[1][0:1, ds(4 * (i * U + (u + LAG - 1)) + 3, 1)], min_val=0, max_val=CH)
                    pe.wait_ge(m_ld[u], (i + 1) * 32)
                    pe.wait_ge(m_g[u], (i + 1) * (16 * G))
                    pe.wait_ge(m_eT, i * U + (u - 2 + 1 + BASE))
                    tp(bank(4 * (u % 2))[:, 0:P], v3(eat, U)[:, u, :], ident[:, :]).then_inc(m_eTp, 1)
                    pe.wait_ge(m_eT, i * U + (u - 1 + 1 + BASE))
                    pe.wait_ge(m_hid, i * U + (u - 3 + 1 + BASE))
                    mm(bank(1 + (u - 1) % 2), v3(eaT, 2)[0:G * EA + 1, (u - 1) % 2, :], w1blk[:, ds(way, CH)]).then_inc(m_u, 1)
                    pe.wait_ge(m_con, i * U + (u - 2 + 1 + BASE))
                    pe.wait_ge(m_acc, i * U + (u - 4 + 1 + BASE))
                    agg = bank(3 + 2 * ((u - 2) % 2))[:, 0:LW]
                    for t in range(G):
                        last = mm(agg, hot1[:, (u - 2) % U, t, :], con1_s[:, (u - 2) % 3, t, :], start=(t == 0), stop=(t == G - 1))
                    last.then_inc(m_agg, 1)

            mm(bank(7)[0:1, 0:1], ones[:, 0:1], ones[:, 0:1]).then_inc(m_over, 1)
            pe.wait_ge(m_over, 3)

            pe.sem_inc(f_tp, 1)
            def pe_last(new, old):
                if old is not None:
                    pe.wait_ge(f_t, old + 1)
                    pe.wait_ge(f_r, old + 1)
                    for t in range(GRP):
                        for k in range(3):
                            mm(bank(6, 2)[:, t * D:(t + 1) * D], aT[:, (k * GRP + t) * P:(k * GRP + t + 1) * P], w2u[:, k * D:(k + 1) * D],
                               start=(k == 0), stop=False)
                        last = mm(bank(6, 2)[:, t * D:(t + 1) * D], degT[0:3, t * P:(t + 1) * P], dbu[:, :], start=False, stop=True)
                    last.then_inc(f_o, 1)
                if new is not None:
                    pe.wait_ge(f_deg, new + 1)
                    pe.wait_ge(f_b, new + 1)
                    pe.wait_ge(f_x, new + 1)
                    for t in range(GRP):
                        for k in range(3):
                            at = (k * GRP + t) * P
                            tp(bank(0, 4)[:, at:at + P], fx[:, (k * GRP + t) * D:(k * GRP + t + 1) * D], ident[:, :])
                        last = mm(bank(4, 2)[0:3, t * P:(t + 1) * P], v3(deg3, GRP)[:, t, :], ident[:, :])
                    last.then_inc(f_tp, 1)

            passes(pe, pe_last)

        @block.vector
        def _(dve):
            v = nc.vector
            tt, ts = v.tensor_tensor, v.tensor_scalar
            link = linker(dve, s_dv)

            v.memset(xs[96:P, :], 0.0).then_inc(s_zero, 1)
            v.memset(ps[:, :], 0.0).then_inc(s_bank, 1)
            v.memset(w1blk[:, :], 0.0).then_inc(s_blk, 1)
            v.memset(reql[:, :], 0.0).then_inc(s_blk, 1)
            v.memset(b2col[:, :], 0.0).then_inc(s_blk, 1)
            v.memset(reql_one[:, :], 0.0)
            link(v.memset(sel3[:, :], 0.0))
            v.memset(reql_one[:, G * EA:], 1.0).then_inc(s_blk, 1)
            v.memset(sel3[:, 2:3], 1.0).then_inc(s_blk, 1)
            v.memset(eps_ln[:, :], EPS).then_inc(s_blk, 1)
            dve.wait_ge(s_const, 8)
            v.memset(minus_low[:, :], 0.0)
            link(v.memset(minus[:, :], 0.0))
            ts(minus_low[CP:CP + H, :], ident[0:H, 0:H], -1.0, None, ALU.mult)
            v.tensor_copy(minus[0:H, :], ident[0:H, 0:H])
            ts(minus[CP:CP + H, :], ident[0:H, 0:H], -1.0, None, ALU.mult).then_inc(s_blk, 1)

            dve.wait_ge(s_dst, 32)
            v.tensor_copy(dstf[0:EP], dsti[0:EP]).then_inc(s_pre, 1)
            dve.wait_ge(s_pre, 1)
            ts(tilef[0:EP], dstf[0:EP], 1.0 / NT, -0.5 * (NT - 1) / NT, ALU.mult, ALU.add).then_inc(s_pre, 1)
            dve.wait_ge(s_pre, 2)
            ts(dstm[0:EP], tilef[0:EP], MAGIC, None, ALU.add).then_inc(s_pre, 1)
            dve.wait_ge(s_pre, 3)
            ts(tilef[0:EP], dstm[0:EP], -MAGIC, None, ALU.add).then_inc(s_pre, 1)
            dve.wait_ge(s_pre, 4)
            v.scalar_tensor_tensor(dstm[0:EP], tilef[0:EP], -float(NT), dstf[0:EP], ALU.mult, ALU.add).then_inc(s_pre, 1)
            tileb = dsti.bitcast(BF16)[:, 0:2 * EQ]
            v.tensor_copy(tileb[0:EP], tilef[0:EP]).then_inc(s_pre, 1)
            ts(srcb[0:EP], v3(srci, 2)[0:EP, 1, :], float(N), None, ALU.add).then_inc(s_pen, 1)
            dve.wait_ge(s_prev, 16)
            link(tt(dprev[0:EP], dprev[0:EP], dstf[0:EP], ALU.not_equal))
            ts(dprev[0:EP], dprev[0:EP], -BIG, None, ALU.mult).then_inc(s_pen, 1)
            dve.wait_ge(s_pool, 7)
            ts(thr, thr, -0.5, None, ALU.add).then_inc(s_pre, 1)
            dve.wait_ge(s_pre, 7)
            t3 = v3(tileb, 2)
            dve.sem_inc(s_qs, 1)
            with dve.Fori(0, GROUPS) as i:
                dve.wait_ge(s_q, i + 2)
                q = v3(bank(0, 2)[:, 0:GRP * D], GRP)
                part = qsp[:, ds(i * (GRP * 3 * D), GRP * 3 * D)].rearrange("p (t k d) -> p t k d", t=GRP, k=3)
                r = v3(qres, GRP)
                link(v.tensor_copy(part[:, :, 0, :], q))
                link(tt(r, q, part[:, :, 0, :], ALU.subtract))
                link(v.tensor_copy(part[:, :, 1, :], r))
                tt(part[:, :, 2, :], r, part[:, :, 1, :], ALU.subtract).then_inc(s_qs, 1)
                for t in range(GRP):
                    last = ts(cmpb[0:EP, 2 * t * EQ:(2 * t + 1) * EQ], t3[0:EP, 0, :], thr[0:EP, ds(i * GRP + t, 1)], 0.0,
                              ALU.is_lt, ALU.add, accum_out=cnt[0:EP, ds(i * GRP + t, 1)])
                link(last)
            v.memset(mark[:, 1:2], 0.0).then_inc(s_cnt, 1)

            dve.wait_ge(s_seg, 1)
            v.tensor_copy(seg[:, 0:TILES], bank(7)[:, 0:TILES])
            link(ts(seg[:, TILES:VT], bank(7)[:, TILES:VT], 0.5, HALF / 2, ALU.mult, ALU.add))

            def chunk_table(l):
                nv = (TILES, VT)[l]
                end = (E, END1)[l]
                if l:
                    s2, n2 = v3(seg, 2), v3(nch, 2)
                    link(tt(n2[:, :, 0:TILES - 1], s2[:, :, 1:TILES], s2[:, :, 0:TILES - 1], ALU.subtract))
                    link(ts(n2[:, :, TILES - 1:TILES], s2[:, :, TILES - 1:TILES], -1.0, float(HALF), ALU.mult, ALU.add))
                    v.tensor_copy(spos[:, 0:TILES], seg[:, 0:TILES])
                    link(ts(spos[:, TILES:VT], seg[:, TILES:VT], float(BASE1), None, ALU.add))
                else:
                    link(tt(spos[:, 0:nv], seg[:, 0:TILES], seg[:, TILES:VT], ALU.add))
                    link(tt(nch[:, 0:nv - 1], spos[:, 1:nv], spos[:, 0:nv - 1], ALU.subtract))
                    link(ts(nch[:, nv - 1:nv], spos[:, nv - 1:nv], -1.0, float(E), ALU.mult, ALU.add))
                link(ts(nchi[:, 0:nv], nch[:, 0:nv], float(CH - 1), None, ALU.add))
                link(ts(nchi[:, 0:nv], nchi[:, 0:nv], CH.bit_length() - 1, None, ALU.arith_shift_right))
                link(v.tensor_copy(nch[:, 0:nv], nchi[:, 0:nv]))
                link(v.tensor_tensor_scan(cum[:, 0:nv], ones[:, 0:nv], nch[:, 0:nv], 0.0, op0=ALU.mult, op1=ALU.add))
                link(tt(nch[:, 0:nv], cum[:, 0:nv], nch[:, 0:nv], ALU.subtract))
                link(ts(nch[:, 0:nv], nch[:, 0:nv], -float(CH), None, ALU.mult))
                link(tt(spos[:, 0:nv], spos[:, 0:nv], nch[:, 0:nv], ALU.add))
                link(ts(col[0:1, 0:1], cum[0:1, nv - 1:nv], float(LAG), None, ALU.add))
                link(ts(hotv[0:1, 0:64], iota_u[0:1, :], col[0:1, 0:1], 0.0, ALU.is_lt, ALU.add, accum_out=col[0:1, 1:2]))
                link(v.tensor_copy(iters_sb[0:1, l:l + 1], col[0:1, 1:2]))
                k = kcol[0:TR, :]
                c = lambda n: col[0:TR, n * TC:(n + 1) * TC]
                which, below, off, tile, way, summed = (c(n) for n in range(6))
                for j in range(TC):
                    link(ts(hotv[0:TR, 0:nv], cum[0:TR, 0:nv], k[:, j:j + 1], 0.0, ALU.is_le, ALU.add, accum_out=which[:, j:j + 1]))
                if l == 0:
                    for j in range(TC):
                        link(ts(hotv[0:TR, 0:nv], cum[0:TR, 0:nv], k[:, j:j + 1], 0.0, ALU.is_lt, ALU.add, accum_out=below[:, j:j + 1]))
                    link(tt(tbe[0:TR, 40:40 + TC], which, below, ALU.is_equal))
                    link(ts(below, k, 0.0, None, ALU.is_gt))
                    link(tt(tbe[0:TR, 40:40 + TC], tbe[0:TR, 40:40 + TC], below, ALU.mult))
                link(ts(below, k, 0.0, float(nv), ALU.is_lt, ALU.mult))
                link(tt(which, which, below, ALU.add))
                for j in range(TC):
                    link(ts(hotv[0:TR, 0:nv], iota_row[0:TR, 0:nv], which[:, j:j + 1], None, ALU.is_equal))
                    link(tt(hotv[0:TR, 0:nv], hotv[0:TR, 0:nv], spos[0:TR, 0:nv], ALU.mult))
                    link(v.tensor_reduce(off[:, j:j + 1], hotv[0:TR, 0:nv], AX_X, ALU.add))
                link(ts(tile, k, float(CH), None, ALU.mult))
                link(tt(off, off, tile, ALU.add))
                link(ts(below, which, float(nv), float(2 * end), ALU.is_ge, ALU.mult))
                link(tt(off, off, below, ALU.add))
                link(ts(off, off, float(end), None, ALU.min))
                link(ts(way, which, float(TILES), None, ALU.is_ge))
                link(ts(tile, way, -float(TILES * l), None, ALU.mult))
                link(tt(tile, tile, which, ALU.add))
                link(ts(tile, tile, float(TILES - 1), None, ALU.min))
                entry = tbe[0:TR, 16 * l:16 * l + 12].bitcast(I32).rearrange("p (c f) -> p c f", c=TC)
                v.tensor_copy(entry[:, :, 0], off)
                ts(entry[:, :, 1], tile, float(3 * D), None, ALU.mult)
                ts(entry[:, :, 2], which, float((RW, LW)[l]), None, ALU.mult)
                ts(entry[:, :, 3], way, float(CH), None, ALU.mult)
                link(ts(tbe[0:TR, 32 + 4 * l:32 + 4 * l + TC], tile, -float(NT), None, ALU.mult))
            chunk_table(0)
            dve.sem_inc(s_tab, 1)
            dve.wait_ge(s_tabi, 48)

            dve.wait_ge(s_w2, 16 * 31)
            link(ts(epsc[:, :], epsc[:, :], 1.0, None, ALU.add))
            ts(w2u[:, 2 * D:3 * D], w2wu[:, 2 * D:3 * D], epsc[:, :], None, ALU.mult).then_inc(s_wu, 1)
            dve.wait_ge(s_wu, 1)

            dve.wait_ge(s_init, 3)
            dve.wait_ge(s_wcp, 4)
            n0 = dve.value_load(iters_sb[0:1, 0:1], min_val=1, max_val=ITERS)
            for s_, below in ((l_hot, 0), (l_prod, 0), (l_c, 0), (l_pv, 0), (l_acc, 0), (l_f, 1), (l_at, 1)):
                dve.sem_inc(s_, BASE - below)
            last_ = counter(dve, "dve_last", BASE)
            landed_ = counter(dve, "dve_landed", 48)
            kv_s = kv.rearrange("p (u g d) -> p u g d", u=U, g=G)
            hot = s_hot.rearrange("p (u g n) -> p u g n", u=U, g=G)
            pen_s = v3(pen, 3)
            F, SC = v3(fmx, 2), v3(stk, 2)
            con_s, cur_s = v3(contrib, 2), v3(cur, 2)
            with dve.Fori(0, n0) as i:
                for u in range(U):
                    dve.wait_ge(l_ld[u], landed_)
                    ts(v3(st, U)[:, u, :], v3(drow, 3)[:, u % 3, :], iota_col[:, :], None, ALU.is_equal).then_inc(l_hot, 1)
                    dve.wait_ge(l_kc, last_)
                    dve.wait_ge(l_kq, last_)
                    tt(v3(prod, 2)[:, (u - 1) % 2, :].rearrange("d (p g) -> d p g", g=G),
                       bank((u - 1) % 2).rearrange("d (p g) -> d p g", g=G),
                       v3(kts, 2)[:, (u - 1) % 2, :].rearrange("d (g p) -> d p g", g=G), ALU.mult).then_inc(l_prod, 1)
                    w = (u - 2) % 2
                    dve.wait_ge(l_scr, last_)
                    dve.wait_ge(l_c, last_)
                    before = F[0:H, 1 - w, CH - 1:CH]
                    pn = pen_s[0:H, (u - 2) % 3, :]
                    tt(ucar[0:H, w:w + 1], before, pn[:, 0:1], ALU.add)
                    v.tensor_tensor_scan(F[0:H, w, :], pn[:, 0:CH], SC[0:H, w, :], before, op0=ALU.add, op1=ALU.max).then_inc(l_f, 1)
                    dve.wait_ge(l_f, last_)
                    v.tensor_tensor_scan(SC[CP:CP + H, w, ::-1], pn[:, CH:0:-1], F[0:H, w, ::-1], -BIG, op0=ALU.add, op1=ALU.max).then_inc(l_c, 1)
                    dve.wait_ge(l_dcr, last_)
                    tt(hot[:, u, :, :], iota_row[:, None, :].to_broadcast([P, G, P]), dcr[:, :, None].to_broadcast([P, G, P]), ALU.is_equal)
                    dve.wait_ge(l_e, last_)
                    c = con_s[:, (u - 3) % 2, :]
                    rows_ = c[:, H:].rearrange("p (g h w) -> p g h w", g=G, h=H)
                    tt(rows_[:, :, :, 0:DH], kv_s[:, (u - 3) % U, :, D:2 * D].rearrange("p g (h w) -> p g h w", h=H),
                       rows_[:, :, :, DH:AW].to_broadcast([P, G, H, DH]), ALU.mult).then_inc(l_pv, 1)
                    dve.wait_ge(l_rsc, last_)
                    dve.wait_ge(l_acc, last_)
                    at = atmp.rearrange("p (h w) -> p h w", h=H)
                    tt(at, cur_s[:, (u + 1) % 2, :].rearrange("p (h w) -> p h w", h=H), rsc[:, :, None].to_broadcast([P, H, AW]), ALU.mult).then_inc(l_at, 1)
                    dve.wait_ge(l_at, last_)
                    tt(cur_s[:, u % 2, :], atmp, bank(6 + (u - 4) % 2)[:, H:H + RW], ALU.add).then_inc(l_acc, 1)
                    dve.reg_add(last_, last_, 1)
                dve.reg_add(landed_, landed_, 48)
            v.memset(mark[:, 0:1], 0.0).then_inc(l_over, 1)
            dve.wait_ge(l_over, 3)

            def statistics(t3, var, norm):
                for t in range(GRP):
                    last = v.bn_stats(norm[0][:, t * 6:(t + 1) * 6], t3[:, t, :])
                link(last, apart=True)
                for t in range(GRP):
                    last = v.bn_aggr(norm[1][:, 2 * t:2 * t + 2], norm[0][:, t * 6:(t + 1) * 6])
                last.then_inc(var, 1)

            def normalise(to, t3, norm):
                link(v.reciprocal(norm[3], norm[2]))
                for t in range(GRP):
                    last = ts(to[:, t, :], t3[:, t, :], norm[1][:, 2 * t:2 * t + 1], norm[3][:, t:t + 1], ALU.subtract, ALU.mult)
                return last

            r3, q3, h3, a4 = v3(res, GRP), v3(res2, GRP), v3(h1, GRP), av.rearrange("p (t h w) -> p t h w", t=GRP, h=H)
            rowb = lambda k: rows[:, k:k + 1, :].to_broadcast([P, GRP, D])
            rd = rden.rearrange("p (t h) -> p t h", t=GRP)

            def dve_pass(new, mid, old):
                xg = lambda at: v3(xs[:, ds(at * (GRP * D), GRP * D)], GRP)
                if new is not None:
                    sums = acc0[:, ds(new * (GRP * RW), GRP * RW)].rearrange("p (t h w) -> p t h w", t=GRP, h=H)
                    link(ts(rd, sums[:, :, :, DH], 1e-9, None, ALU.add))
                    link(v.reciprocal(rd, rd))
                    tt(a4, sums[:, :, :, 0:DH], rd[:, :, :, None].to_broadcast([P, GRP, H, DH]), ALU.mult).then_inc(n_a, 1)
                if old is not None:
                    dve.wait_ge(n_f2, old + 1)
                    dve.wait_ge(n_h1c, old + 1)
                    dve.wait_ge(n_x1c, old + 1)
                    dve.wait_ge(n_xTp, old + 1)
                    hc3 = v3(h1c[:, ds((old % 2) * (GRP * D), GRP * D)], GRP)
                    link(tt(q3, hc3, v3(bank(2, 2)[:, 0:GRP * D], GRP), ALU.add))
                    statistics(q3, n_v[1], norm2)
                    dve.wait_ge(n_s[1], old + 1)
                    link(normalise(q3, q3, norm2))
                    link(tt(q3, q3, rowb(3), ALU.mult))
                    link(tt(q3, q3, rowb(4), ALU.add))
                    link(tt(q3, q3, xg(old), ALU.add))
                    statistics(q3, n_v[2], norm2)
                if new is not None:
                    dve.wait_ge(n_emb, new + 1)
                    link(tt(r3, xg(new), v3(bank(0, 2)[:, 0:GRP * D], GRP), ALU.add))
                    statistics(r3, n_v[0], norm1)
                if old is not None:
                    dve.wait_ge(n_s[2], old + 1)
                    normalise(q3, q3, norm2).then_inc(n_x1, 1)
                if new is not None:
                    dve.wait_ge(n_s[0], new + 1)
                    link(normalise(r3, r3, norm1))
                    link(tt(r3, r3, rowb(0), ALU.mult))
                    if mid is not None:
                        dve.wait_ge(n_hTp, mid + 1)
                        dve.wait_ge(n_h1c, mid + 1)
                    tt(h3, r3, rowb(1), ALU.add).then_inc(n_h1, 1)

            def table_of_layer_1():
                chunk_table(1)
                dve.sem_inc(s_tab, 1)

            passes3(dve, dve_pass, table_of_layer_1)

            bases(dve, (m_hot, 0), (m_hid, 1), (m_acc, 3))
            v.memset(acc1, 0.0).then_inc(m_zero, 1)
            dve.wait_ge(n_y, GROUPS)
            dve.wait_ge(n_x1c, GROUPS + 1)
            dve.wait_ge(m_zero, 1)
            dve.wait_ge(m_pool, 5)
            dve.wait_ge(s_tabi, 80)
            n1 = dve.value_load(iters_sb[0:1, 1:2], min_val=1, max_val=ITERS)
            hot1 = s1.rearrange("p (u g n) -> p u g n", u=U, g=G)
            with dve.Fori(0, n1) as i:
                for u in range(U):
                    dve.wait_ge(m_ld[u], (i + 1) * 32)
                    entry = i * U + (u + LAG)
                    for t in range(G):
                        last = ts(hot1[:, u, t, :], iota_row[:, :], v3(dcol1, U)[:, u, t:t + 1], nj[1][:, ds(entry, 1)],
                                  ALU.subtract, ALU.is_equal)
                    last.then_inc(m_hot, 1)
                    dve.wait_ge(m_u, i * U + (u - 1 + 1 + BASE))
                    dve.wait_ge(m_con, i * U + (u - 3 + 1 + BASE))
                    tt(v3(hid, 2)[:, (u - 1) % 2, :], bank(1 + (u - 1) % 2), v3(yg, U)[:, (u - 1) % U, :], ALU.add).then_inc(m_hid, 1)
                    into = dve.value_load(tab_sb[1][0:1, ds(4 * (i * U + (u + LAG - 3)) + 2, 1)], min_val=0, max_val=VT * LW)
                    dve.wait_ge(m_agg, i * U + (u - 3 + 1 + BASE))
                    dve.wait_ge(m_acc, i * U + (u - 4 + 1 + BASE))
                    sums = acc1[:, ds(into, LW)]
                    tt(sums, sums, bank(3 + 2 * ((u - 3) % 2))[:, 0:LW], ALU.add).then_inc(m_acc, 1)

            d33, f3, o3 = v3(deg3, GRP), v3(fin, GRP), v3(fout, GRP)
            v.memset(mark[:, 1:2], 0.0).then_inc(m_over, 1)
            dve.wait_ge(m_over, 3)
            def dve_last(new, old):
                if new is not None:
                    dve.wait_ge(f_tp, new + 1)
                    for k in range(2):
                        part = v3(acc1[:, ds(new * (GRP * LW) + k * TILES * LW, GRP * LW)], GRP)
                        v.tensor_copy(d33[:, :, k:k + 1], part[:, :, D:LW])
                    v.tensor_copy(v3(fx[:, 0:GRP * D], GRP), v3(acc1[:, ds(new * (GRP * LW), GRP * LW)], GRP)[:, :, 0:D]).then_inc(f_deg, 1)
                if old is not None:
                    dve.wait_ge(f_r, old + 2)
                    link(tt(f3, f3, v3(xs[:, ds(old * (GRP * D), GRP * D)], GRP), ALU.add))
                    statistics(f3, f_var, norm3)
                    dve.wait_ge(f_sd, old + 1)
                    dve.wait_ge(f_free, old + 1)
                    normalise(o3, f3, norm3).then_inc(f_out, 1)

            dve.sem_inc(f_out, 1)
            passes(dve, dve_last)


_INS = ['x', 'src', 'dst', 'edge_attr_16', 'L0_gnn_Wq', 'L0_gnn_Wk', 'L0_gnn_Wv', 'L0_gnn_W0', 'L0_gnn_ln1_g',
        'L0_gnn_ln1_b', 'L0_gnn_fc1_w', 'L0_gnn_fc1_b', 'L0_gnn_fc2_w', 'L0_gnn_fc2_b', 'L0_gnn_ln2_g', 'L0_gnn_ln2_b',
        'L1_gnn_req_emb', 'L1_gnn_W1f', 'L1_gnn_b1f', 'L1_gnn_W2f', 'L1_gnn_b2f', 'L1_gnn_W1b', 'L1_gnn_b1b',
        'L1_gnn_W2b', 'L1_gnn_b2b', 'L1_gnn_Wu', 'L1_gnn_bu', 'L1_gnn_eps']
_OUTS = [((6250, 128), 'float32')]


def kernel(**inputs):
    import numpy as _np
    import concourse.bacc as _bacc
    from concourse import mybir as _mybir
    from concourse.bass_utils import run_bass_kernel_spmd as _run

    nc = _bacc.Bacc("TRN2", target_bir_lowering=False, num_devices=1)
    arrays, args = {}, []
    for name in _INS:
        a = _np.ascontiguousarray(inputs[name])
        arrays[f"in_{name}_dram"] = a
        args.append(nc.dram_tensor(f"in_{name}_dram", a.shape, _mybir.dt.from_np(a.dtype), kind="ExternalInput").ap())
    for i, (shape, dtype) in enumerate(_OUTS):
        dt = _mybir.dt.from_np(_np.dtype(dtype))
        args.append(nc.dram_tensor(f"out_{i}_dram", shape, dt, kind="ExternalOutput").ap())
    gnn_kernel(nc, *args)
    r = _run(nc, [arrays], core_ids=[0])
    got = tuple(r.results[0][f"out_{i}_dram"] for i in range(len(_OUTS)))
    return got[0]
```
